# Optimizing a Trainium2 kernel written in Bass

```python
import numpy as np
import jax
import jax.numpy as jnp

def _softmax(x, axis=-1):
    return jax.nn.softmax(x, axis=axis)

def _gelu(x):
    return jax.nn.gelu(x, approximate=True)

def _silu(x):
    return jax.nn.silu(x)

def _sigmoid(x):
    return jax.nn.sigmoid(x)

def _layernorm(x, axis=-1, eps=1e-05):
    m = jnp.mean(x, axis=axis, keepdims=True)
    v = jnp.var(x, axis=axis, keepdims=True)
    return (x - m) / jnp.sqrt(v + eps)

def _scatter_add(tgt, idx, src, axis=0):
    return tgt.at[idx].add(src)

def _segment_sum(src, seg, n):
    return jax.ops.segment_sum(src, seg, n)
kernel_name = 'mk_decoder_preln_d1_seqx_r8_efc212'

def setup_inputs(seed: int=0):
    np.random.seed(seed)
    _w = jnp.asarray

    def _rec_inputs():
        import jax
        import jax.numpy as jnp
        _rk = jax.random.key(seed)
        x = 0.002226 + 0.9996 * jax.random.normal(jax.random.fold_in(_rk, 1), (8, 256, 128), jnp.float32)
        _lenS = 256 - jax.random.randint(jax.random.fold_in(_rk, 7), (8,), 0, max(1, 256 // 4) + 1, jnp.int32)
        _lenS2 = 256 - jax.random.randint(jax.random.fold_in(_rk, 8), (8,), 0, max(1, 256 // 4) + 1, jnp.int32)
        _ctx_1024P = jax.random.normal(jax.random.fold_in(_rk, 11), (8, 16, 128), jnp.float32)
        _ctx_1024c = jax.random.dirichlet(jax.random.fold_in(_rk, 511), 0.3 * jnp.ones((16,), jnp.float32), (8, 256))
        _ctx_1024t = jnp.einsum('bsk,bkd->bsd', _ctx_1024c, _ctx_1024P)
        _ctx_1024t = _ctx_1024t * jax.lax.rsqrt(jnp.mean(jnp.square(_ctx_1024t)) + 1e-12) * 0.953939
        ctx_1024 = -7.10856e-05 + 0.999911 * (_ctx_1024t + 0.3 * jax.random.normal(jax.random.fold_in(_rk, 611), (8, 256, 128), jnp.float32))
        return (x, ctx_1024)
    x, ctx_1024 = _rec_inputs()

    def _L0_attn_setup():
        import jax, jax.numpy as jnp
        import numpy as np
        ALPHA = 1.2
        A = 1.0
        BANDWIDTH = 1.0
        D_INTRINSIC = 2
        SPHERE_RADIUS = 1.0
        NUM_HEADS = 16
        HIDDEN = 128
        HEAD_DIM = HIDDEN // NUM_HEADS
        EPS = 1e-07

        def _l2norm(t):
            n = jnp.sqrt(jnp.sum(t * t, axis=-1, keepdims=True))
            return t / jnp.maximum(n, 1e-12)
        key = jax.random.key(seed)
        k1, k2, k3, k4, k5 = jax.random.split(key, 5)
        B, S = (2, 256)
        scale = 0.02
        return {'x': jax.random.normal(k1, (B, S, HIDDEN), dtype=jnp.float32), 'w_qkv': jax.random.normal(k2, (3 * HIDDEN, HIDDEN), dtype=jnp.float32) * scale, 'b_qkv': jnp.zeros((3 * HIDDEN,), dtype=jnp.float32), 'w_out': jax.random.normal(k3, (HIDDEN, HIDDEN), dtype=jnp.float32) * scale, 'b_out': jnp.zeros((HIDDEN,), dtype=jnp.float32)}
    _L0_attn_all = _L0_attn_setup()
    _L0_attn_in = {k: v for k, v in _L0_attn_all.items() if k in ('w_qkv', 'b_qkv', 'w_out', 'b_out')}
    del _L0_attn_all

    def _L0_xattn_setup():
        import jax, jax.numpy as jnp
        import numpy as np
        DIM = 128
        HEAD_DIM = 64
        NUM_HEADS = 8
        INNER = HEAD_DIM * NUM_HEADS
        ROT_DIM = HEAD_DIM
        ROPE_BASE = 10000.0
        EPS = 1e-05

        def layer_norm(x, g, b):
            mu = jnp.mean(x, axis=-1, keepdims=True)
            var = jnp.var(x, axis=-1, keepdims=True)
            return (x - mu) * jax.lax.rsqrt(var + EPS) * g + b

        def rope_rotate_k(k):
            n = k.shape[1]
            half = ROT_DIM // 2
            inv_freq = 1.0 / ROPE_BASE ** (jnp.arange(0, ROT_DIM, 2, dtype=jnp.float32) / ROT_DIM)
            theta = jnp.arange(n, dtype=jnp.float32)[:, None] * inv_freq[None, :]
            angles = jnp.concatenate([theta, theta], axis=-1)
            cos = jnp.cos(angles)[None, :, None, :].astype(k.dtype)
            sin = jnp.sin(angles)[None, :, None, :].astype(k.dtype)
            k_rope, k_pass = (k[..., :ROT_DIM], k[..., ROT_DIM:])
            neg_half = jnp.concatenate([-k_rope[..., half:], k_rope[..., :half]], axis=-1)
            k_rope = k_rope * cos + neg_half * sin
            return jnp.concatenate([k_rope, k_pass], axis=-1)
        key = jax.random.key(seed)
        ks = jax.random.split(key, 5)
        b, n, m = (8, 1024, 64)
        s = 1.0 / np.sqrt(DIM)
        return {'x': jax.random.normal(ks[0], (b, n, DIM), jnp.float32), 'latents': jax.random.normal(ks[1], (b, m, DIM), jnp.float32), 'gamma_x': jnp.ones((DIM,), jnp.float32), 'beta_x': jnp.zeros((DIM,), jnp.float32), 'gamma_l': jnp.ones((DIM,), jnp.float32), 'beta_l': jnp.zeros((DIM,), jnp.float32), 'Wq': jax.random.normal(ks[2], (DIM, INNER), jnp.float32) * s, 'Wkv': jax.random.normal(ks[3], (DIM, 2 * INNER), jnp.float32) * s, 'Wo': jax.random.normal(ks[4], (INNER, DIM), jnp.float32) * (1.0 / np.sqrt(INNER))}
    _L0_xattn_all = _L0_xattn_setup()
    _L0_xattn_in = {k: v for k, v in _L0_xattn_all.items() if k in ('gamma_x', 'beta_x', 'gamma_l', 'beta_l', 'Wq', 'Wkv', 'Wo')}
    del _L0_xattn_all

    def _L0_ffn_setup():
        import math
        import jax, jax.numpy as jnp
        import numpy as np
        D_MODEL = 128
        D_FF = 512
        N_EXPERTS = 8
        CAPACITY_FACTOR = 1.25
        L, B = (64, 8)

        def _route(tokens, router_w):
            T = tokens.shape[0]
            E = router_w.shape[0]
            capacity = int(math.ceil(T / E * CAPACITY_FACTOR))
            logits = tokens @ router_w.T
            probs = jax.nn.softmax(logits, axis=-1)
            top1_idx = jnp.argmax(probs, axis=-1)
            top1_prob = jnp.max(probs, axis=-1)
            order = jnp.lexsort((-top1_prob, top1_idx))
            sorted_e = top1_idx[order]
            counts = jnp.bincount(top1_idx, length=E)
            start = jnp.cumsum(counts) - counts
            pos_in_group = jnp.arange(T) - start[sorted_e]
            keep_sorted = pos_in_group < capacity
            keep = jnp.zeros((T,), bool).at[order].set(keep_sorted)
            return jnp.where(keep, top1_idx, 0).astype(jnp.int32)
        key = jax.random.key(seed)
        ks = jax.random.split(key, 6)
        s_in = 1.0 / math.sqrt(D_MODEL)
        s_ff = 1.0 / math.sqrt(D_FF)
        return {'x': jax.random.normal(ks[0], (L, B, D_MODEL), dtype=jnp.float32), 'router_w': jax.random.uniform(ks[1], (N_EXPERTS, D_MODEL), minval=-s_in, maxval=s_in), 'W1': jax.random.uniform(ks[2], (N_EXPERTS, D_MODEL, D_FF), minval=-s_in, maxval=s_in), 'b1': jax.random.uniform(ks[3], (N_EXPERTS, D_FF), minval=-s_in, maxval=s_in), 'W2': jax.random.uniform(ks[4], (N_EXPERTS, D_FF, D_MODEL), minval=-s_ff, maxval=s_ff), 'b2': jax.random.uniform(ks[5], (N_EXPERTS, D_MODEL), minval=-s_ff, maxval=s_ff)}
    _L0_ffn_all = _L0_ffn_setup()
    _L0_ffn_in = {k: v for k, v in _L0_ffn_all.items() if k in ('router_w', 'W1', 'b1', 'W2', 'b2')}
    del _L0_ffn_all
    return {'x': x, 'ctx_1024': ctx_1024, 'L0_attn_w_qkv': _L0_attn_in['w_qkv'], 'L0_attn_b_qkv': _L0_attn_in['b_qkv'], 'L0_attn_w_out': _L0_attn_in['w_out'], 'L0_attn_b_out': _L0_attn_in['b_out'], 'L0_xattn_gamma_x': _L0_xattn_in['gamma_x'], 'L0_xattn_beta_x': _L0_xattn_in['beta_x'], 'L0_xattn_gamma_l': _L0_xattn_in['gamma_l'], 'L0_xattn_beta_l': _L0_xattn_in['beta_l'], 'L0_xattn_Wq': _L0_xattn_in['Wq'], 'L0_xattn_Wkv': _L0_xattn_in['Wkv'], 'L0_xattn_Wo': _L0_xattn_in['Wo'], 'L0_ffn_router_w': _L0_ffn_in['router_w'], 'L0_ffn_W1': _L0_ffn_in['W1'], 'L0_ffn_b1': _L0_ffn_in['b1'], 'L0_ffn_W2': _L0_ffn_in['W2'], 'L0_ffn_b2': _L0_ffn_in['b2']}

def reference(x, ctx_1024, L0_attn_w_qkv, L0_attn_b_qkv, L0_attn_w_out, L0_attn_b_out, L0_xattn_gamma_x, L0_xattn_beta_x, L0_xattn_gamma_l, L0_xattn_beta_l, L0_xattn_Wq, L0_xattn_Wkv, L0_xattn_Wo, L0_ffn_router_w, L0_ffn_W1, L0_ffn_b1, L0_ffn_W2, L0_ffn_b2):
    import jax
    import jax.numpy as jnp

    def _L0_attn_ref(x, w_qkv, b_qkv, w_out, b_out):
        import jax, jax.numpy as jnp
        import numpy as np
        ALPHA = 1.2
        A = 1.0
        BANDWIDTH = 1.0
        D_INTRINSIC = 2
        SPHERE_RADIUS = 1.0
        NUM_HEADS = 16
        HIDDEN = 128
        HEAD_DIM = HIDDEN // NUM_HEADS
        EPS = 1e-07

        def _l2norm(t):
            n = jnp.sqrt(jnp.sum(t * t, axis=-1, keepdims=True))
            return t / jnp.maximum(n, 1e-12)
        B, S, H = x.shape
        qkv = x @ w_qkv.T + b_qkv
        q, k, v = jnp.split(qkv, 3, axis=-1)
        to_heads = lambda t: t.reshape(B, S, NUM_HEADS, HEAD_DIM).transpose(0, 2, 1, 3)
        q = _l2norm(to_heads(q))
        k = _l2norm(to_heads(k))
        v = to_heads(v)
        cos = jnp.einsum('bhsd,bhtd->bhst', q, k)
        g_dist = jnp.arccos(jnp.clip(cos, -1.0 + EPS, 1.0 - EPS)) * SPHERE_RADIUS
        attn_score = (1.0 + g_dist / BANDWIDTH ** 0.5) ** (-D_INTRINSIC - ALPHA)
        n_r = jnp.sum(attn_score, axis=-1)
        n_c = jnp.sum(attn_score, axis=-2)
        k_tilde = (n_r ** (-A))[..., :, None] * attn_score * (n_c ** (-A))[..., None, :]
        probs = k_tilde / jnp.maximum(jnp.sum(k_tilde, axis=-1, keepdims=True), 1e-12)
        out = jnp.einsum('bhst,bhtd->bhsd', probs, v)
        out = out.transpose(0, 2, 1, 3).reshape(B, S, H)
        return out @ w_out.T + b_out

    def _L0_xattn_ref(x, latents, gamma_x, beta_x, gamma_l, beta_l, Wq, Wkv, Wo):
        import jax, jax.numpy as jnp
        import numpy as np
        DIM = 128
        HEAD_DIM = 64
        NUM_HEADS = 8
        INNER = HEAD_DIM * NUM_HEADS
        ROT_DIM = HEAD_DIM
        ROPE_BASE = 10000.0
        EPS = 1e-05

        def layer_norm(x, g, b):
            mu = jnp.mean(x, axis=-1, keepdims=True)
            var = jnp.var(x, axis=-1, keepdims=True)
            return (x - mu) * jax.lax.rsqrt(var + EPS) * g + b

        def rope_rotate_k(k):
            n = k.shape[1]
            half = ROT_DIM // 2
            inv_freq = 1.0 / ROPE_BASE ** (jnp.arange(0, ROT_DIM, 2, dtype=jnp.float32) / ROT_DIM)
            theta = jnp.arange(n, dtype=jnp.float32)[:, None] * inv_freq[None, :]
            angles = jnp.concatenate([theta, theta], axis=-1)
            cos = jnp.cos(angles)[None, :, None, :].astype(k.dtype)
            sin = jnp.sin(angles)[None, :, None, :].astype(k.dtype)
            k_rope, k_pass = (k[..., :ROT_DIM], k[..., ROT_DIM:])
            neg_half = jnp.concatenate([-k_rope[..., half:], k_rope[..., :half]], axis=-1)
            k_rope = k_rope * cos + neg_half * sin
            return jnp.concatenate([k_rope, k_pass], axis=-1)
        b, n, _ = x.shape
        m = latents.shape[1]
        h, d = (NUM_HEADS, HEAD_DIM)
        scale = d ** (-0.5)
        xn = layer_norm(x, gamma_x, beta_x)
        ln = layer_norm(latents, gamma_l, beta_l)
        q = (ln @ Wq).reshape(b, m, h, d)
        kv_x = xn @ Wkv
        k_x, v_x = (kv_x[..., :INNER], kv_x[..., INNER:])
        kv_l = ln @ Wkv
        k_l, v_l = (kv_l[..., :INNER], kv_l[..., INNER:])
        k_x = k_x.reshape(b, n, h, d)
        v_x = v_x.reshape(b, n, h, d)
        k_x = rope_rotate_k(k_x)
        q = jnp.transpose(q, (0, 2, 1, 3)) * scale
        k_x = jnp.transpose(k_x, (0, 2, 1, 3))
        v_x = jnp.transpose(v_x, (0, 2, 1, 3))
        k_l = jnp.transpose(k_l.reshape(b, m, h, d), (0, 2, 1, 3))
        v_l = jnp.transpose(v_l.reshape(b, m, h, d), (0, 2, 1, 3))
        k = jnp.concatenate([k_x, k_l], axis=2)
        v = jnp.concatenate([v_x, v_l], axis=2)
        sim = jnp.einsum('bhid,bhjd->bhij', q, k)
        attn = jax.nn.softmax(sim, axis=-1)
        out = jnp.einsum('bhij,bhjd->bhid', attn, v)
        out = jnp.transpose(out, (0, 2, 1, 3)).reshape(b, m, INNER)
        return out @ Wo

    def _L0_ffn_ref(x, router_w, W1, b1, W2, b2):
        import math
        import jax, jax.numpy as jnp
        import numpy as np
        D_MODEL = 128
        D_FF = 512
        N_EXPERTS = 8
        CAPACITY_FACTOR = 1.25
        L, B = (64, 8)

        def _route(tokens, router_w):
            T = tokens.shape[0]
            E = router_w.shape[0]
            capacity = int(math.ceil(T / E * CAPACITY_FACTOR))
            logits = tokens @ router_w.T
            probs = jax.nn.softmax(logits, axis=-1)
            top1_idx = jnp.argmax(probs, axis=-1)
            top1_prob = jnp.max(probs, axis=-1)
            order = jnp.lexsort((-top1_prob, top1_idx))
            sorted_e = top1_idx[order]
            counts = jnp.bincount(top1_idx, length=E)
            start = jnp.cumsum(counts) - counts
            pos_in_group = jnp.arange(T) - start[sorted_e]
            keep_sorted = pos_in_group < capacity
            keep = jnp.zeros((T,), bool).at[order].set(keep_sorted)
            return jnp.where(keep, top1_idx, 0).astype(jnp.int32)
        Lx, Bx, D = x.shape
        T = Lx * Bx
        E = router_w.shape[0]
        tokens = x.reshape(T, D)
        final_e = _route(tokens, router_w)
        out = jnp.zeros_like(tokens)
        for e in range(E):
            h = jax.nn.relu(tokens @ W1[e] + b1[e])
            y = h @ W2[e] + b2[e]
            out = out + jnp.where((final_e == e)[:, None], y, 0.0)
        return out.reshape(Lx, Bx, D)
    x = x + _L0_attn_ref(_layernorm(x, axis=-1), L0_attn_w_qkv, L0_attn_b_qkv, L0_attn_w_out, L0_attn_b_out)
    x = x + _L0_xattn_ref(ctx_1024, _layernorm(x, axis=-1), L0_xattn_gamma_x, L0_xattn_beta_x, L0_xattn_gamma_l, L0_xattn_beta_l, L0_xattn_Wq, L0_xattn_Wkv, L0_xattn_Wo)
    x = x + _L0_ffn_ref(_layernorm(x, axis=-1), L0_ffn_router_w, L0_ffn_W1, L0_ffn_b1, L0_ffn_W2, L0_ffn_b2)
    return x

_drawn_inputs = setup_inputs


def setup_inputs(seed=0):
    import zlib

    import numpy as np

    out = dict(_drawn_inputs(seed))
    spreads = {'L0_attn_b_qkv': (0.0, 0.1),
     'L0_attn_b_out': (0.0, 0.1),
     'L0_xattn_gamma_x': (1.0, 0.2),
     'L0_xattn_beta_x': (0.0, 0.1),
     'L0_xattn_gamma_l': (1.0, 0.2),
     'L0_xattn_beta_l': (0.0, 0.1)}
    factors = {'L0_attn_w_qkv': 3.965, 'L0_ffn_b1': 2.881}
    for name, (base, spread) in spreads.items():
        noise = np.random.default_rng([zlib.crc32(name.encode()), seed]).standard_normal(out[name].shape)
        drawn = base * np.exp(spread * noise) if base else spread * noise
        out[name] = jnp.asarray(drawn.astype(out[name].dtype))
    for name, factor in factors.items():
        out[name] = (out[name] * factor).astype(out[name].dtype)
    return out
```

```python
import math
from contextlib import ExitStack

import numpy as np

import concourse.bass as bass
from concourse import mybir

ALU = mybir.AluOpType
ACT = mybir.ActivationFunctionType
AX = mybir.AxisListType.X
F32 = mybir.dt.float32
F16 = mybir.dt.float16
BF16 = mybir.dt.bfloat16
I32 = mybir.dt.int32

P = 128
NB, S, D = 8, 256, 128
NT = NB * S // P
NH, DH = 16, 8
XH, XD = 8, 64
INNER = XH * XD
KC = 2 * S // P
NE, FF = 8, 512
FC = FF // P
CAP = math.ceil(NB * S / NE * 1.25)
SLOTS = (NE - 1) * CAP
LN_EPS = 1e-5
CLIP = 1e-7
DECAY = -3.2
FAR = 100000
LE_TABLE, TA_TABLE = "natural_log_exp_and_others", "sigmoid_and_others"

C_ID, C_ROPE, C_TRI, C_EXP, C_FAR, C_END = 0, 128, 128 + 512, 768, 776, 792


def shape_constants():
    c = np.zeros((P, C_END), np.float32)
    c[:, C_ID:C_ID + P] = np.eye(P)
    half = XD // 2
    inv = (1.0 / 10000.0 ** (np.arange(0, XD, 2, dtype=np.float32) / XD)).astype(np.float32)
    theta = np.arange(S, dtype=np.float32)[None, :] * inv[:, None]
    row = np.arange(P) % XD
    ang = theta[row % half]
    c[:, C_ROPE:C_ROPE + S] = np.cos(ang)
    c[:, C_ROPE + S:C_ROPE + 2 * S] = np.sin(ang) * np.where(row < half, -1.0, 1.0)[:, None]
    c[:, C_TRI:C_TRI + P] = np.arange(P)[:, None] < np.arange(P)[None, :]
    c[:, C_EXP:C_EXP + NE] = np.arange(NE) - NE
    c[:, C_FAR:C_FAR + NT] = FAR + np.arange(P)[:, None] + P * np.arange(NT)[None, :]
    sel = np.zeros((XH, XH, P), np.float32)
    sel[np.arange(XH), np.arange(XH), :] = 1.0
    return c, sel.reshape(XH, XH * P)


class Step:

    def __init__(self, t=None, r=None):
        self.t = t
        if r is None:
            self.f, self.a, self.b, self.c = t + 1, t, t - 1, t - 2
            self.F, self.A, self.B, self.C = (0 <= n < NB for n in (t + 1, t, t - 1, t - 2))
        else:
            self.f, self.a, self.b, self.c = r + 3, r + 2, r + 1, r
            self.F = self.A = self.B = self.C = True
            self.t = None
            self.r = r

    def uses(self):
        u = []
        u += ["xnT"] * self.F + ["ctxT"] * self.B
        u += [f"qkv{c}" for c in range(2)] * self.F
        u += [f"kx{n}" for n in range(4)] * self.B + [f"v{n}" for n in range(2)] * self.B
        u += ["yT"] * self.C + ["latT"] * self.B
        u += ["v2", "v3", "q0", "q1", "kl0", "kl1"] * self.B
        u += ["logits"] * self.C
        u += [f"mx{n}" for n in range(2 * XH)] * self.B
        u += ["qS", "kS"] * self.F + ["mT"] * self.B
        u += ["pT0", "pT1"] * self.B + ["ao0", "ao1"] * self.A + ["pT2"] * self.B
        u += ["oT", "att"] * self.A + ["pT3", "o2T0", "o2T1", "xo"] * self.B
        return u

    def use(self, name):
        here = self.uses()
        at = here.index(name)
        bank = at % 2
        local = at // 2
        def rises(t):
            n = len(Step(t).uses())
            return (n + 1 - bank) // 2
        if self.t is not None:
            return bank, sum(rises(t) for t in range(-1, self.t)) + local
        before = sum(rises(t) for t in range(-1, 2))
        return bank, self.r * rises(2) + (before + local)


def each_step(engine, body):
    for t in (-1, 0, 1):
        body(Step(t))
    with engine.Fori(0, 5) as r:
        body(Step(r=r))
    for t in (7, 8, 9):
        body(Step(t))


def wait(engine, sem, value):
    if not isinstance(value, int) or value > 0:
        engine.wait_ge(sem, value)


def build(nc, x, ctx_in, wqkv, bqkv, wout, bout, gam, wq, wk, wks, wv, wo, wr, w1, b1, w2, b2, cst, sel, out):
    ctx = ExitStack()
    with ctx:
        def sb(name, shape, dt=F32):
            return ctx.enter_context(nc.sbuf_tensor(name, shape, dt))

        def pb(name, shape, dt=F32):
            return ctx.enter_context(nc.psum_tensor(name, shape, dt))

        def sem(name):
            return ctx.enter_context(nc.semaphore(name))

        xs = sb("xs", [P, NT, D])
        cx = sb("cx", [P, NT, D])
        vall = sb("vall", [P, NT, D])
        y3 = vall
        yT = cx[:, :, :].rearrange("p t d -> p (t d)")
        lgs = sb("lgs", [P, NT, NE])
        wqkv_s = sb("wqkv_s", [P, 3 * D])
        bqkv_s = sb("bqkv_s", [P, 3 * D])
        wout_s = sb("wout_s", [P, D])
        bout_s = sb("bout_s", [1, D])
        gam_s = sb("gam_s", [P, 4])
        wq_s = sb("wq_s", [P, INNER])
        wk_s = sb("wk_s", [P, INNER])
        wks_s = sb("wks_s", [P, INNER])
        wv_s = sb("wv_s", [P, INNER])
        wo_s = sb("wo_s", [P, 4, D])
        wr_s = sb("wr_s", [P, NE])
        b1_s = sb("b1_s", [P, NE, FC])
        b2_s = sb("b2_s", [1, NE * D])
        cst_s = sb("cst_s", [P, C_END])
        sel_s = sb("sel_s", [XH, XH * P], BF16)
        id16 = sb("id16", [P, P], F16)
        idb = sb("idb", [P, P], BF16)
        ones_row = sb("ones_row", [1, P])
        cols = sb("cols", [P, 2])
        ident = cst_s[:, C_ID:C_ID + P]
        rope = cst_s[:, C_ROPE:C_ROPE + 2 * S]

        st = sb("st", [P, 2 * NT, 6])
        mv = sb("mv", [P, 2 * NT, 2])
        lnrs = sb("lnrs", [P, 2 * NT])
        lnvar = sb("lnvar", [P, 2 * NT])
        st2 = sb("st2", [P, 4, 6])
        mv2 = sb("mv2", [P, 4, 2])
        var4 = sb("var4", [P, 4])
        lv4 = sb("lv4", [P, 4])
        rs4 = sb("rs4", [P, 4])

        xn = sb("xn", [P, 2, D])
        xnT = sb("xnT", [P, S])
        qk = sb("qk", [P, 2, 2 * D])
        ss = sb("ss", [P, 2, 2, NH])
        l2 = sb("l2", [P, 2, 2, NH])
        qn = sb("qn", [P, 2, 2, D])
        sq = qn[:, :, :, :].rearrange("p k c d -> p k (c d)")
        stack = sb("stack", [P, 2, 2 * NH, 4, DH], F16)
        qT = sb("qT", [P, 4, S], F16)
        kT = sb("kT", [P, 4, S], F16)
        X = sb("X", [P, NH, 2, S])
        L = sb("L", [P, NH, 2, S])
        ncol = sb("ncol", [P, NH, 2])
        rcol = sb("rcol", [P, NH, 2])
        vp = sb("vp", [P, NH, 2, DH + 2])
        aoT = sb("aoT", [P, 4, S])
        den = sb("den", [P, 2, NH])
        rden = sb("rden", [P, 2, NH])
        o = sb("o", [P, 2, D])
        oT = sb("oT", [P, S])

        cn = sb("cn", [P, 2, D])
        cT = sb("cT", [P, S])
        ln = sb("ln", [P, 2, D])
        lT = sb("lT", [P, S])
        kcs = sb("kcs", [P, 4, 2, S])
        k1 = sb("k1", [P, 4, 2 * S], F16)
        k2 = sb("k2", [P, 4, 2 * S], F16)
        q1 = sb("q1", [P, 4, S], F16)
        q2 = sb("q2", [P, 4, S], F16)
        KS = sb("KS", [P, XH, 2 * S], F16)
        QQ = sb("QQ", [P, 2, XH, S], F16)
        Q1 = QQ[:, 0]
        Q2 = QQ[:, 1]
        V = sb("V", [P, KC, XH, XD + 1])
        mx = sb("mx", [P, 2, XH])
        negm = sb("negm", [P, 2, XH], BF16)
        mT = sb("mT", [XH, S], BF16)
        E = sb("E", [P, 2, KC, S])
        sel_f = E[:, :, :, :].rearrange("p a b c -> p (a b c)")[0:XH, 0:XH * P]
        rpv = sb("rpv", [P, 2, 4])
        oh = sb("oh", [XD + 1, 4, S])
        o2 = sb("o2", [P, 2, INNER])
        o2T = sb("o2T", [P, 4, S])
        yn = sb("yn", [P, 2, D])
        yTs = sb("yTs", [P, S])

        Xf = X[:, :, :, :].rearrange("p a b c -> p (a b c)")
        w1_s = Xf[:, 0:NE * FF].rearrange("p (e f) -> p e f", e=NE)
        w2_s = Xf[:, NE * FF:2 * NE * FF].rearrange("p (e c d) -> p e c d", e=NE, c=FC)
        Lf = L[:, :, :, :].rearrange("p a b c -> p (a b c)")
        res = Lf[:, 0:NT * D].rearrange("p (t d) -> p t d", t=NT)
        pbc = Lf[:, 0:NT * P].rearrange("p (t q) -> p t q", t=NT)
        prow = Lf[:, NT * P:2 * NT * P]
        G = Lf[:, 2 * NT * P:4 * NT * P].bitcast(BF16).rearrange("p (r q) -> p r q", r=4)
        o2f = o2[:, :, :].rearrange("p a b -> p (a b)")
        probs, tmp8, hot = (o2f[:, n * NT * NE:(n + 1) * NT * NE].rearrange("p (t e) -> p t e", t=NT) for n in range(3))
        hotb = o2f[:, 768:768 + NT * NE // 2].bitcast(BF16).rearrange("p (t e) -> p t e", t=NT)
        dest = o2f[:, 832:832 + NT].bitcast(I32)
        r16 = o2f[:, 848:848 + 6 * NT].rearrange("p (n t) -> p n t", n=6)
        eqd = o2f[:, 512:512 + 2 * P].rearrange("p (r q) -> p r q", r=2)
        zero = aoT[:, :, :].rearrange("p g q -> p (g q)")[:, 0:CAP]
        zb = sb("zb", [P, P], BF16)
        xin = E[:, :, :, :].rearrange("p a b c -> p (a b c)")[:, 0:4 * 3 * D].rearrange("p (r c d) -> p r c d", r=4, c=3)
        xinT = kcs[:, :, :, :].rearrange("p a b c -> p (a b c)")[:, 0:2 * CAP].rearrange("p (r s) -> p r s", r=2)
        hT = [KS[:, :, :].rearrange("p a b -> p (a b)").bitcast(F32).rearrange("p (c s) -> p c s", c=FC),
              QQ[:, :, :, :].rearrange("p k a b -> p (k a b)").bitcast(F32).rearrange("p (c s) -> p c s", c=FC)]
        yo = o2T[:, :, :].rearrange("p a b -> p (a b)")[:, 0:2 * 3 * D].rearrange("p (r c d) -> p r c d", r=2, c=3)

        x_slots = nc.dram_tensor("x_slots", (SLOTS, D), F32, kind="Internal").ap()
        y_slots = nc.dram_tensor("y_slots", (SLOTS, D), F32, kind="Internal").ap()

        psW = pb("psW", [P, 2, 512])
        psC = pb("psC", [P, 2, 512])
        psS = pb("psS", [P, KC, S])
        psA = pb("psA", [P, 512])
        psP = pb("psP", [P, 512])
        psAg = psA[:, :].rearrange("p (g q) -> p g q", g=2)
        psPh = psP[:, :].rearrange("p (h q) -> p h q", h=2)
        ring = [psC[:, 0, :], psC[:, 1, :], psS[:, 0:2, :].rearrange("p a b -> p (a b)"),
                psS[:, 2:4, :].rearrange("p a b -> p (a b)")]
        psR = psA[:, 0:NT * NE].rearrange("p (t e) -> p t e", t=NT)

        x_loaded, ctx_loaded, attn_w_loaded = sem("x_loaded"), sem("ctx_loaded"), sem("attn_w_loaded")
        xattn_w_loaded, exp_b_loaded, exp_w_loaded = sem("xattn_w_loaded"), sem("exp_b_loaded"), sem("exp_w_loaded")
        dve_consts = sem("dve_consts")
        x_var_ready, x_rs_ready = sem("x_var_ready"), sem("x_rs_ready")
        work_filled = [sem(f"work_filled{n}") for n in range(2)]
        work_read = [sem(f"work_read{n}") for n in range(2)]
        xn_ready, ss_ready, l2_ready, stack_ready = sem("xn_ready"), sem("ss_ready"), sem("l2_ready"), sem("stack_ready")
        cos_done, clip_done, ln_done, diff_done = sem("cos_done"), sem("clip_done"), sem("ln_done"), sem("diff_done")
        act_chain, kern_done, vp_ready, av_done = sem("act_chain"), sem("kern_done"), sem("vp_ready"), sem("av_done")
        ao_stored, o_ready, oh_stored = sem("ao_stored"), sem("o_ready"), sem("oh_stored")
        x1_var_ready, x1_rs_ready = sem("x1_var_ready"), sem("x1_rs_ready")
        x2_var_ready, x2_rs_ready = sem("x2_var_ready"), sem("x2_rs_ready")
        cn_ready, ln_ready, yn_ready = sem("cn_ready"), sem("ln_ready"), sem("yn_ready")
        split_ready, stacked = sem("split_ready"), sem("stacked")
        negm_ready, scores_done, exps_done, pv_done = sem("negm_ready"), sem("scores_done"), sem("exps_done"), sem("pv_done")
        lg_sub, lg_exp, pbc_ready, prow_filled, prow_ready = sem("lg_sub"), sem("lg_exp"), sem("pbc_ready"), sem("prow_filled"), sem("prow_ready")
        g_ready, g_used, rank_done, dest_ready = sem("g_ready"), sem("g_used"), sem("rank_done"), sem("dest_ready")
        zeroed, scattered = sem("zeroed"), sem("scattered")
        xin_loaded = [sem(f"xin_loaded{n}") for n in range(4)]
        xinT_filled, xinT_ready = sem("xinT_filled"), sem("xinT_ready")
        h_filled, h_stored, y_filled, y_stored = sem("h_filled"), sem("h_stored"), sem("y_filled"), sem("y_stored")
        gathered, final_ready, out_done = sem("gathered"), sem("final_ready"), sem("out_done")
        y_saved = [sem(f"y_saved{n}") for n in range(2)]

        block = ctx.enter_context(nc.Block())

        def W(s, name):
            bank, n = s.use(name)
            return bank, n, psW[:, bank, :]

        blocks = [(0, blk) for blk in range(4)] + [(e, 0) for e in range(1, NE)]

        def store_hidden(eng, m, first):
            e, _ = blocks[m]
            width = FF if e == 0 else CAP
            if m >= 2:
                eng.wait_ge(y_filled, m - 1)
            for c in range(first, FC, 2):
                eng.wait_ge(h_filled, FC * m + c + 1)
                dst, src, bias = hT[m % 2][:, c, 0:width], ring[c][:, 0:width], b1_s[:, e, c:c + 1]
                if first == 0:
                    eng.activation(dst, src, ACT.Relu, bias=bias).then_inc(h_even, 1)
                else:
                    eng.tensor_scalar(dst, src, bias, 0.0, ALU.add, ALU.max).then_inc(h_odd, 1)

        h_even, h_odd = sem("h_even"), sem("h_odd")
        ybank = [psP[:, :], psW[:, 1, :]]

        @block.sync
        def _(sp):
            sp.dma_start(xs[:, :, :], x.rearrange("(t p) d -> p t d", p=P)).then_inc(x_loaded, 16)
            for dst, src in ((cst_s, cst), (wqkv_s, wqkv), (bqkv_s, bqkv), (wout_s, wout), (bout_s, bout)):
                sp.dma_start(dst[:, :], src).then_inc(attn_w_loaded, 16)
            sp.dma_start(cx[:, :, :], ctx_in.rearrange("(t p) d -> p t d", p=P)).then_inc(ctx_loaded, 16)
            for dst, src in ((gam_s, gam), (wk_s, wk), (wks_s, wks), (wv_s, wv), (wq_s, wq), (sel_f, sel), (wr_s, wr)):
                sp.dma_start(dst if dst is sel_f else dst[:, :], src).then_inc(xattn_w_loaded, 16)
            sp.dma_start(wo_s[:, :, :], wo.rearrange("(c p) d -> p c d", p=P)).then_inc(xattn_w_loaded, 16)
            sp.dma_start(b1_s[:, :, :], b1.rearrange("p (e c) -> p e c", e=NE)).then_inc(exp_b_loaded, 16)
            sp.dma_start(b2_s[:, :], b2).then_inc(exp_b_loaded, 16)
            sp.wait_ge(dve_consts, 1)
            for n in range(NE - 1):
                rows = x_slots[n * CAP:(n + 1) * CAP, :].rearrange("a d -> (a d)").rearrange("(p f) -> p f", p=P)
                sp.dma_start(rows, zero[:, :]).then_inc(zeroed, 16)

            def body(s):
                if s.t == 8:
                    sp.wait_ge(av_done, 4 * NB)
                    sp.dma_start(w1_s, w1.rearrange("e p f -> p e f")).then_inc(exp_w_loaded, 16)
                    sp.dma_start(w2_s, w2.rearrange("e (c p) d -> p e c d", p=P)).then_inc(exp_w_loaded, 16)
                if not s.B:
                    return
                sp.wait_ge(split_ready, s.b + 1)
                wait(sp, scores_done, s.b * XH)
                for dst, low, high in ((KS[:, :, :], k1, k2), (Q1, q1, q1), (Q2, q2, q2)):
                    heads = dst.rearrange("p (c two) n -> p two c n", two=2)
                    for two in range(2):
                        for half, src in ((0, low), (1, high)):
                            sp.dma_start(heads[64 * half:64 * half + 64, two], src[64 * two:64 * two + 64, :, :])\
                              .then_inc(stacked, 16)

            each_step(sp, body)

            sp.wait_ge(scattered, 16 * NT)
            for e in range(1, NE):
                r = (e - 1) % 4
                if e > 4:
                    sp.wait_ge(xinT_filled, e - 4)
                row = (e - 1) * CAP
                sp.dma_start(xin[:, r, 0:2, :], x_slots[row:row + 2 * P, :].rearrange("(c p) d -> p c d", p=P))\
                  .then_inc(xin_loaded[r], 16)
                sp.dma_start(xin[0:CAP - 2 * P, r, 2, :], x_slots[row + 2 * P:row + CAP, :]).then_inc(xin_loaded[r], 16)
            for e in range(1, NE):
                r = e % 2
                sp.wait_ge(y_stored, 4 + e)
                row = (e - 1) * CAP
                sp.dma_start(y_slots[row:row + 2 * P, :].rearrange("(c p) d -> p c d", p=P), yo[:, r, 0:2, :])\
                  .then_inc(y_saved[r], 16)
                sp.dma_start(y_slots[row + 2 * P:row + CAP, :], yo[0:CAP - 2 * P, r, 2, :]).then_inc(y_saved[r], 16)
            out_v = out.rearrange("(t p) d -> p t d", p=P)
            for n in range(4):
                sp.wait_ge(final_ready, n + 1)
                sp.dma_start(out_v[:, 4 * n:4 * n + 4, :], xs[:, 4 * n:4 * n + 4, :]).then_inc(out_done, 16)
            sp.wait_ge(out_done, 64)
            for r in range(2):
                sp.wait_ge(y_saved[r], 32 * len(range(r or 2, NE, 2)))
            sp.wait_ge(zeroed, 16 * 7)

        @block.gpsimd
        def _(pool):
            def body(s):
                if not s.A:
                    return
                for g in range(4):
                    pool.wait_ge(ln_done, s.a * 4 + g + 1)
                    pool.tensor_tensor(X[:, 4 * g:4 * g + 4, :, :], X[:, 4 * g:4 * g + 4, :, :],
                                       L[:, 4 * g:4 * g + 4, :, :], ALU.subtract).then_inc(diff_done, 1)

            each_step(pool, body)

            pool.wait_ge(dest_ready, 1)
            pool.wait_ge(zeroed, 16 * 7)
            for t in range(NT):
                pool.indirect_dma_start(x_slots, bass.IndirectOffsetOnAxis(ap=dest[:, t:t + 1], axis=0),
                                        y3[:, t, :], None, bounds_check=SLOTS - 1, oob_is_err=False)\
                    .then_inc(scattered, 16)
            for r in range(2):
                pool.wait_ge(y_saved[r], 32 * len(range(r or 2, NE, 2)))
            pool.wait_ge(y_stored, 4)
            for t in range(NT):
                pool.indirect_dma_start(res[:, t, :], None, y_slots,
                                        bass.IndirectOffsetOnAxis(ap=dest[:, t:t + 1], axis=0),
                                        bounds_check=SLOTS - 1, oob_is_err=False).then_inc(gathered, 16)

        @block.scalar
        def _(act):
            act.preload_act_table_set(LE_TABLE)
            act.wait_ge(x_var_ready, 1)
            act.activation(lnrs[:, :], lnvar[:, :], ACT.Ln)
            act.drain()
            act.activation(lnrs[:, :], lnrs[:, :], ACT.Exp, scale=-0.5).then_inc(x_rs_ready, 1)

            def head(s, h):
                act.wait_ge(scores_done, s.b * XH + h + 1)
                wait(act, pv_done, s.b * XH + h - 1)
                act.activation(E[:, h % 2, :, :], psS[:, :, :], ACT.Exp).then_inc(exps_done, 1)

            def store_head(s, h):
                act.wait_ge(pv_done, s.b * XH + h + 1)
                if h >= 4:
                    bank, u, _ = W(s, f"pT{h // 2 - 2}")
                    act.wait_ge(work_filled[bank], u + 1)
                act.activation(oh[:, h % 4, :], psPh[0:XD + 1, h % 2, :], ACT.Copy).then_inc(oh_stored, 1)

            def inv_std(c, var, rs, value):
                act.wait_ge(var, value)
                act.activation(lv4[:, c:c + 2], var4[:, c:c + 2], ACT.Ln)
                act.drain()
                act.activation(rs4[:, c:c + 2], lv4[:, c:c + 2], ACT.Exp, scale=-0.5).then_inc(rs, 1)

            def body(s):
                def value_tile(n):
                    bank, u, w = W(s, f"v{n}")
                    if n == 0:
                        wait(act, pv_done, s.b * XH)
                    act.wait_ge(work_filled[bank], u + 1)
                    act.activation(V[:, n, :, 0:XD], w.rearrange("p (h d) -> p h d", h=XH), ACT.Copy)\
                       .then_inc(work_read[bank], 1)

                for g in range(4):
                    if s.A:
                        hs = slice(4 * g, 4 * g + 4)
                        act.wait_ge(clip_done, s.a * 8 + 2 * g + 2)
                        act.activation(L[:, hs, :, :], X[:, hs, :, :], ACT.Ln, bias=1.0)
                        act.activation(X[:, hs, :, :], X[:, hs, :, :], ACT.Ln, bias=1.0, scale=-1.0)\
                           .then_inc(ln_done, 1)
                    if g == 0 and s.C:
                        inv_std(2, x2_var_ready, x2_rs_ready, s.c + 1)
                    if g == 1 and s.B:
                        value_tile(0)
                        value_tile(1)
                    if g == 1 and s.F:
                        act.wait_ge(ss_ready, s.f + 1)
                        act.activation(l2[:, :, :, :], ss[:, :, :, :], ACT.Ln)
                        act.drain()
                        act.activation(l2[:, :, :, :], l2[:, :, :, :], ACT.Exp, scale=-0.5).then_inc(l2_ready, 1)
                    if g == 2 and s.B:
                        value_tile(2)
                        value_tile(3)
                if s.A:
                    act.preload_act_table_set(TA_TABLE)
                    for g in range(4):
                        act.wait_ge(diff_done, s.a * 4 + g + 1)
                        xg = X[:, 4 * g:4 * g + 4, :, :]
                        act.activation(xg, xg, ACT.Tanh, scale=0.25).then_inc(act_chain, 1)
                    for g in range(4):
                        act.wait_ge(act_chain, s.a * 12 + g + 1)
                        xg = X[:, 4 * g:4 * g + 4, :, :]
                        act.activation(xg, xg, ACT.Arctan).then_inc(act_chain, 1)
                    act.preload_act_table_set(LE_TABLE)
                def log_angle(g):
                    act.wait_ge(act_chain, s.a * 12 + 4 + g + 1)
                    xg = X[:, 4 * g:4 * g + 4, :, :]
                    act.activation(xg, xg, ACT.Ln, bias=cols[:, 0:1], scale=2.0).then_inc(act_chain, 1)

                def kernel_value(g):
                    act.wait_ge(act_chain, s.a * 12 + 8 + g + 1)
                    xg = X[:, 4 * g:4 * g + 4, :, :]
                    act.activation(xg, xg, ACT.Exp, scale=DECAY).then_inc(kern_done, 1)

                if s.A:
                    log_angle(0)
                for g in range(4):
                    if s.A:
                        if g < 3:
                            log_angle(g + 1)
                        kernel_value(g)
                    if s.B:
                        head(s, g)
                        if g > 0:
                            store_head(s, g - 1)
                if s.B:
                    for h in range(4, XH):
                        head(s, h)
                        store_head(s, h - 1)
                    store_head(s, XH - 1)
                if s.A:
                    inv_std(0, x1_var_ready, x1_rs_ready, s.a + 1)

            each_step(act, body)

            act.wait_ge(lg_sub, 1)
            act.activation(probs[:, :, :], tmp8[:, :, :], ACT.Exp).then_inc(lg_exp, 1)
            act.wait_ge(exp_b_loaded, 32)
            for m in range(len(blocks)):
                store_hidden(act, m, 0)

        def norm_pair(dve, dst, src, mean, rs, done):
            for c in range(2):
                last = dve.tensor_scalar(dst(c), src(c), mean(c), rs(c), ALU.subtract, ALU.mult)
            last.then_inc(done, 1)

        @block.vector
        def _(dve):
            dve.memset(zero[:, :], 0.0).then_inc(dve_consts, 1)
            dve.memset(zb[:, :], 0.0)
            dve.memset(ones_row[:, :], 1.0)
            dve.memset(cols[:, 0:1], 1.0 + math.pi / 2)
            dve.memset(vp[:, :, :, DH + 1:DH + 2], 1.0)
            dve.memset(V[:, :, :, XD:XD + 1], 1.0)
            dve.memset(psA[:, :], 0.0)
            dve.wait_ge(x_loaded, 16)
            for t in range(NT):
                dve.bn_stats(st[:, t, :], xs[:, t, :])
            dve.wait_ge(ctx_loaded, 16)
            for t in range(NT):
                dve.bn_stats(st[:, NT + t, :], cx[:, t, :])
            dve.drain()
            for t in range(2 * NT):
                dve.bn_aggr(mv[:, t, :], st[:, t, :])
            dve.drain()
            dve.tensor_scalar(lnvar[:, :], mv[:, :, 1], LN_EPS, None, ALU.add).then_inc(x_var_ready, 1)
            dve.wait_ge(attn_w_loaded, 80)
            dve.tensor_copy(id16[:, :], ident)
            dve.tensor_copy(idb[:, :], ident)
            dve.wait_ge(xattn_w_loaded, 128)
            dve.tensor_copy(sel_s[:, :], sel_f).then_inc(dve_consts, 1)
            dve.wait_ge(x_rs_ready, 1)

            def flat(ap):
                return ap.rearrange("p a b -> p (a b)")

            def body(s):
                def filled(name):
                    bank, u, w = W(s, name)
                    dve.wait_ge(work_filled[bank], u + 1)
                    return work_read[bank], w

                if s.F:
                    norm_pair(dve, lambda c: xn[:, c, :], lambda c: flat(xs[:, bass.ds(2 * s.f + c, 1), :]),
                              lambda c: flat(mv[:, bass.ds(2 * s.f + c, 1), 0:1]),
                              lambda c: lnrs[:, bass.ds(2 * s.f + c, 1)], xn_ready)
                if s.B:
                    norm_pair(dve, lambda c: cn[:, c, :], lambda c: flat(cx[:, bass.ds(2 * s.b + c, 1), :]),
                              lambda c: flat(mv[:, bass.ds(NT + 2 * s.b + c, 1), 0:1]),
                              lambda c: lnrs[:, bass.ds(NT + 2 * s.b + c, 1)], cn_ready)
                if s.F:
                    read, w = filled("xnT")
                    dve.tensor_copy(xnT[:, :], w[:, 0:S]).then_inc(read, 1)
                if s.B:
                    read, w = filled("ctxT")
                    dve.tensor_scalar(cT[:, :], w[:, 0:S], gam_s[:, 0:1], gam_s[:, 1:2], ALU.mult, ALU.add)\
                       .then_inc(read, 1)
                if s.F:
                    for c in range(2):
                        read, w = filled(f"qkv{c}")
                        dve.tensor_tensor(qk[:, c, :], w[:, 0:2 * D], bqkv_s[:, 0:2 * D], ALU.add)
                        dve.tensor_tensor(flat(vall[:, bass.ds(2 * s.f + c, 1), :]), w[:, 2 * D:3 * D],
                                          bqkv_s[:, 2 * D:3 * D], ALU.add).then_inc(read, 1)
                    dve.drain()
                    dve.tensor_tensor(sq[:, :, :], qk[:, :, :], qk[:, :, :], ALU.mult)
                    dve.drain()
                    dve.tensor_reduce(out=ss[:, :, :, :].rearrange("p c k h -> p (c k h)"),
                                      in_=sq[:, :, :].rearrange("p c (g d) -> p (c g) d", d=DH), op=ALU.add, axis=AX)
                    dve.drain()
                    dve.tensor_scalar(ss[:, :, :, :], ss[:, :, :, :], 1e-24, None, ALU.max).then_inc(ss_ready, 1)
                if s.B:
                    for n in range(4):
                        read, w = filled(f"kx{n}")
                        dve.tensor_tensor(kcs[:, n, :, :].rearrange("p a b -> p (a b)"), w, rope, ALU.mult)\
                           .then_inc(read, 1)
                if s.C:
                    dve.wait_ge(x2_rs_ready, s.c + 1)
                    for c in range(2):
                        dve.tensor_scalar(yn[:, c, :], flat(xs[:, bass.ds(2 * s.c + c, 1), :]), mv2[:, 2 + c, 0:1],
                                          rs4[:, 2 + c:3 + c], ALU.subtract, ALU.mult)
                    last = dve.tensor_scalar(flat(y3[:, bass.ds(2 * s.c, 1), :]), flat(xs[:, bass.ds(2 * s.c, 1), :]),
                                             mv2[:, 2, 0:1], rs4[:, 2:3], ALU.subtract, ALU.mult)
                    last.then_inc(yn_ready, 1)
                    dve.tensor_scalar(flat(y3[:, bass.ds(2 * s.c + 1, 1), :]), flat(xs[:, bass.ds(2 * s.c + 1, 1), :]),
                                      mv2[:, 3, 0:1], rs4[:, 3:4], ALU.subtract, ALU.mult)
                if s.B:
                    dve.wait_ge(x1_rs_ready, s.b + 1)
                    norm_pair(dve, lambda c: ln[:, c, :], lambda c: flat(xs[:, bass.ds(2 * s.b + c, 1), :]),
                              lambda c: mv2[:, c, 0:1], lambda c: rs4[:, c:c + 1], ln_ready)
                if s.B:
                    dve.drain()
                    dve.tensor_tensor(kcs[:, :, 0, :], kcs[:, :, 0, :], kcs[:, :, 1, :], ALU.add)
                    wait(dve, stacked, s.b * 192)
                if s.C:
                    read, w = filled("yT")
                    dve.tensor_copy(yT[:, bass.ds(s.c * S, S)], w[:, 0:S])
                    dve.tensor_copy(yTs[:, :], w[:, 0:S]).then_inc(read, 1)
                if s.B:
                    read, w = filled("latT")
                    dve.tensor_scalar(lT[:, :], w[:, 0:S], gam_s[:, 2:3], gam_s[:, 3:4], ALU.mult, ALU.add)\
                       .then_inc(read, 1)
                    dve.drain()
                    dve.tensor_copy(k1[:, :, 0:S], kcs[:, :, 0, :])
                    dve.drain()
                    dve.tensor_tensor(k2[:, :, 0:S], kcs[:, :, 0, :], k1[:, :, 0:S], ALU.subtract)
                    qs = [filled(f"q{n}") for n in range(2)]
                    for n, (read, w) in enumerate(qs):
                        dve.tensor_scalar(q1[:, 2 * n:2 * n + 2, :].rearrange("p a b -> p (a b)"), w,
                                          XD ** -0.5, None, ALU.mult)
                    dve.drain()
                    for n, (read, w) in enumerate(qs):
                        dve.scalar_tensor_tensor(q2[:, 2 * n:2 * n + 2, :].rearrange("p a b -> p (a b)"), w,
                                                 XD ** -0.5, q1[:, 2 * n:2 * n + 2, :].rearrange("p a b -> p (a b)"),
                                                 ALU.mult, ALU.subtract).then_inc(read, 1)
                    ks = [filled(f"kl{n}") for n in range(2)]
                    for n, (read, w) in enumerate(ks):
                        dve.tensor_copy(k1[:, 2 * n:2 * n + 2, S:2 * S], w.rearrange("p (a b) -> p a b", a=2))
                    dve.drain()
                    for n, (read, w) in enumerate(ks):
                        dve.tensor_tensor(k2[:, 2 * n:2 * n + 2, S:2 * S], w.rearrange("p (a b) -> p a b", a=2),
                                          k1[:, 2 * n:2 * n + 2, S:2 * S], ALU.subtract).then_inc(read, 1)
                    dve.drain().then_inc(split_ready, 1)
                if s.C:
                    read, w = filled("logits")
                    dve.tensor_copy(lgs[:, bass.ds(2 * s.c, 2), :], w[:, 0:2 * NE].rearrange("p (c e) -> p c e", c=2))\
                       .then_inc(read, 1)
                if s.F:
                    dve.wait_ge(l2_ready, s.f + 1)
                    for kind in range(2):
                        dve.tensor_tensor(
                            qn[:, kind, :, :].rearrange("p c (h d) -> p c h d", h=NH),
                            qk[:, :, kind * D:kind * D + D].rearrange("p c (h d) -> p c h d", h=NH),
                            l2[:, :, kind, :].rearrange("p c (h a) -> p c h a", a=1).to_broadcast([P, 2, NH, DH]), ALU.mult)
                    dve.drain()

                    def twice(ap):
                        return ap.rearrange("p g (a d) -> p g a d", a=1).to_broadcast([P, 2 * NH, 2, DH])

                    for kind in range(2):
                        unit = qn[:, kind, :, :].rearrange("p c (h d) -> p (c h) d", h=NH)
                        high = stack[:, kind, :, 0:3:2, :] if kind == 0 else stack[:, kind, :, 0:2, :]
                        dve.tensor_copy(high, twice(unit))
                    dve.drain()
                    for kind in range(2):
                        unit = qn[:, kind, :, :].rearrange("p c (h d) -> p (c h) d", h=NH)
                        low = stack[:, kind, :, 1:4:2, :] if kind == 0 else stack[:, kind, :, 2:4, :]
                        last = dve.tensor_tensor(low, twice(unit), twice(stack[:, kind, :, 0, :]), ALU.subtract)
                    last.then_inc(stack_ready, 1)
                if s.B:
                    for n in range(2 * XH):
                        read, w = filled(f"mx{n}")
                        dve.tensor_reduce(out=mx[:, n % 2, n // 2:n // 2 + 1], in_=w, op=ALU.max, axis=AX).then_inc(read, 1)
                    dve.drain()
                    dve.tensor_scalar(negm[:, :, :], mx[:, :, :], -1.0, None, ALU.mult).then_inc(negm_ready, 1)
                if s.F:
                    for name, dst in (("qS", qT), ("kS", kT)):
                        read, w = filled(name)
                        dve.tensor_copy(dst[:, :, :].rearrange("p a b -> p (a b)"), w.bitcast(F16)).then_inc(read, 1)
                if s.B:
                    read, w = filled("mT")
                    dve.tensor_copy(mT[:, :], w[0:XH, :].bitcast(BF16)[:, 0:S]).then_inc(read, 1)

                def norm_heads(n):
                    read, w = filled(f"pT{n}")
                    heads = w[:, 0:4 * (XD + 1)].rearrange("p (h q d) -> p h q d", h=2, q=2)
                    dve.reciprocal(rpv[:, n % 2, :].rearrange("p (h q) -> p h q", h=2), heads[:, :, :, XD])
                    dve.drain()
                    dst = o2[:, :, 2 * n * XD:(2 * n + 2) * XD].rearrange("p q (h d) -> p h q d", h=2)
                    dve.tensor_tensor(dst, heads[:, :, :, 0:XD],
                                      rpv[:, n % 2, :].rearrange("p (h q a) -> p h q a", h=2, a=1).to_broadcast([P, 2, 2, XD]),
                                      ALU.mult).then_inc(read, 1)

                def statistics(c, sources, scale, shift, ready):
                    dve.drain()
                    for n, src in enumerate(sources):
                        dve.bn_stats(st2[:, c + n, :], src)
                    dve.drain()
                    for n in range(2):
                        dve.bn_aggr(mv2[:, c + n, :], st2[:, c + n, :])
                    dve.drain()
                    dve.tensor_scalar(var4[:, c:c + 2], mv2[:, c:c + 2, 1], scale, shift, ALU.mult, ALU.add).then_inc(ready, 1)

                for g in range(4):
                    hs = slice(4 * g, 4 * g + 4)
                    if s.A:
                        dve.wait_ge(kern_done, s.a * 4 + g + 1)
                        dve.tensor_reduce(out=ncol[:, hs, :], in_=X[:, hs, :, :], op=ALU.add, axis=AX)
                        dve.drain()
                        dve.reciprocal(rcol[:, hs, :], ncol[:, hs, :])
                        dve.drain()
                        for c in range(2):
                            dve.tensor_tensor(vp[:, hs, c, 0:DH],
                                              vall[:, bass.ds(2 * s.a + c, 1), 32 * g:32 * g + 32]
                                              .rearrange("p a (h d) -> p (a h) d", h=4),
                                              rcol[:, hs, c:c + 1].to_broadcast([P, 4, DH]), ALU.mult)
                        dve.tensor_copy(vp[:, hs, :, DH], rcol[:, hs, :]).then_inc(vp_ready, 1)
                    if s.F:
                        wait(dve, av_done, s.f * 4 + g - 3)
                        for pair in range(2):
                            dve.wait_ge(cos_done, s.f * 8 + 2 * g + pair + 1)
                            dve.tensor_scalar(X[:, 4 * g + 2 * pair:4 * g + 2 * pair + 2, :, :].rearrange("p a b c -> p (a b c)"),
                                              psC[:, :, :].rearrange("p a b -> p (a b)"),
                                              float(np.float32(-1.0 + CLIP)), float(np.float32(1.0 - CLIP)),
                                              ALU.max, ALU.min).then_inc(clip_done, 1)
                    if s.A:
                        if s.t == 0 and g == 0:
                            dve.wait_ge(zeroed, 16 * 7)
                        dve.wait_ge(av_done, s.a * 4 + g + 1)
                        dve.tensor_copy(aoT[:, g, :], psAg[:, g % 2, :]).then_inc(ao_stored, 1)
                    if s.B and g == 2:
                        norm_heads(0)
                if s.B:
                    norm_heads(1)
                if s.A:
                    aos = []
                    for q in range(2):
                        read, w = filled(f"ao{q}")
                        aos.append((read, w.rearrange("p (h d) -> p h d", h=NH)))
                        dve.tensor_scalar(den[:, q, :], aos[q][1][:, :, DH + 1], 1e-12, None, ALU.mult)
                    dve.drain()
                    for q in range(2):
                        dve.tensor_tensor(den[:, q, :], den[:, q, :], aos[q][1][:, :, DH], ALU.max)
                    dve.drain()
                    dve.reciprocal(rden[:, :, :], den[:, :, :])
                    dve.drain()
                    for q in range(2):
                        dve.tensor_tensor(o[:, q, :].rearrange("p (h d) -> p h d", h=NH), aos[q][1][:, :, 0:DH],
                                          rden[:, q, :].rearrange("p (h a) -> p h a", a=1).to_broadcast([P, NH, DH]),
                                          ALU.mult).then_inc(aos[q][0], 1)
                    dve.drain().then_inc(o_ready, 1)
                if s.B:
                    norm_heads(2)
                if s.A:
                    read, w = filled("oT")
                    dve.tensor_copy(oT[:, :], w[:, 0:S]).then_inc(read, 1)
                    read, w = filled("att")
                    xa = xs[:, bass.ds(2 * s.a, 2), :]
                    dve.tensor_tensor(xa, xa,
                                      w[:, 0:S].rearrange("p (c d) -> p c d", c=2), ALU.add).then_inc(read, 1)
                    statistics(0, [flat(xs[:, bass.ds(2 * s.a + c, 1), :]) for c in range(2)],
                               1.0 + LN_EPS, LN_EPS * LN_EPS, x1_var_ready)
                if s.B:
                    norm_heads(3)
                    for n in range(2):
                        read, w = filled(f"o2T{n}")
                        dve.tensor_copy(o2T[:, 2 * n:2 * n + 2, :].rearrange("p a b -> p (a b)"), w).then_inc(read, 1)
                    read, w = filled("xo")
                    xo_t = xs[:, bass.ds(2 * s.b, 2), :]
                    dve.tensor_tensor(xo_t, xo_t, w[:, 0:S].rearrange("p (c d) -> p c d", c=2), ALU.add).then_inc(read, 1)
                    statistics(2, [flat(xs[:, bass.ds(2 * s.b + c, 1), :]) for c in range(2)], 1.0, LN_EPS, x2_var_ready)

            each_step(dve, body)

            def bc8(ap):
                return ap.rearrange("p (t a) -> p t a", a=1).to_broadcast([P, NT, NE])

            sc, pm, ex, rank, slot, valid = (r16[:, n, :] for n in range(6))
            experts = cst_s[:, C_EXP:C_EXP + NE].rearrange("p (a e) -> p a e", a=1).to_broadcast([P, NT, NE])
            dve.drain()
            dve.tensor_reduce(out=sc, in_=lgs[:, :, :], op=ALU.max, axis=AX)
            dve.drain()
            dve.tensor_tensor(tmp8[:, :, :], lgs[:, :, :], bc8(sc), ALU.subtract).then_inc(lg_sub, 1)
            dve.wait_ge(lg_exp, 1)
            dve.tensor_reduce(out=sc, in_=probs[:, :, :], op=ALU.add, axis=AX)
            dve.drain()
            dve.reciprocal(sc, sc)
            dve.drain()
            dve.tensor_tensor(probs[:, :, :], probs[:, :, :], bc8(sc), ALU.mult)
            dve.drain()
            dve.tensor_reduce(out=pm, in_=probs[:, :, :], op=ALU.max, axis=AX)
            dve.drain()
            dve.wait_ge(diff_done, 4 * NB)
            dve.tensor_copy(pbc, pm.rearrange("p (t a) -> p t a", a=1).to_broadcast([P, NT, P])).then_inc(pbc_ready, 1)
            dve.tensor_tensor(tmp8[:, :, :], probs[:, :, :], bc8(pm), ALU.is_ge)
            dve.drain()
            dve.tensor_tensor(tmp8[:, :, :], tmp8[:, :, :], experts, ALU.mult)
            dve.drain()
            dve.tensor_reduce(out=ex, in_=tmp8[:, :, :], op=ALU.min, axis=AX)
            dve.drain()
            dve.tensor_tensor(hot[:, :, :], bc8(ex), experts, ALU.is_equal)
            dve.drain()
            dve.tensor_copy(hotb[:, :, :], hot[:, :, :])
            dve.wait_ge(prow_filled, 1)
            for n in range(4):
                dve.tensor_copy(prow[:, n * 512:(n + 1) * 512], ring[n])
            dve.drain().then_inc(prow_ready, 1)
            tri = cst_s[:, C_TRI:C_TRI + P]
            for j in range(NT):
                r = j % 4
                if j >= 4:
                    dve.wait_ge(g_used, j - 3)
                pj = r16[:, 1, j:j + 1]
                own = prow[:, j * P:(j + 1) * P]
                dve.scalar_tensor_tensor(eqd[:, j % 2, :], own, pj, tri, ALU.is_equal, ALU.mult)
                if j > 0:
                    dve.tensor_scalar(G[:, r, 0:j * P], prow[:, 0:j * P], pj, None, ALU.is_lt)
                if j < NT - 1:
                    dve.tensor_scalar(G[:, r, (j + 1) * P:NT * P], prow[:, (j + 1) * P:NT * P], pj, None, ALU.is_le)
                dve.drain()
                dve.scalar_tensor_tensor(G[:, r, j * P:(j + 1) * P], own, pj, eqd[:, j % 2, :], ALU.is_lt, ALU.add)\
                   .then_inc(g_ready, 1)
            dve.wait_ge(rank_done, 1)
            dve.tensor_tensor(tmp8[:, :, :], psR, hot[:, :, :], ALU.mult)
            dve.drain()
            dve.tensor_reduce(out=rank, in_=tmp8[:, :, :], op=ALU.add, axis=AX)
            dve.drain()
            dve.tensor_scalar(slot, ex, float(CAP), float((NE - 1) * CAP), ALU.mult, ALU.add)
            dve.tensor_scalar(valid, ex, float(-NE), None, ALU.is_gt)
            dve.drain()
            dve.tensor_tensor(slot, slot, rank, ALU.add)
            dve.scalar_tensor_tensor(valid, rank, float(CAP), valid, ALU.is_lt, ALU.mult)
            dve.drain()
            far = cst_s[:, C_FAR:C_FAR + NT]
            dve.tensor_tensor(slot, slot, far, ALU.subtract)
            dve.drain()
            dve.tensor_tensor(slot, slot, valid, ALU.mult)
            dve.drain()
            dve.tensor_tensor(slot, slot, far, ALU.add)
            dve.drain()
            dve.tensor_copy(dest[:, :], slot).then_inc(dest_ready, 1)

            def store_inputs(m):
                e = blocks[m][0]
                dve.wait_ge(xinT_filled, e)
                if e > 2:
                    dve.wait_ge(h_filled, FC * (m - 1))
                dve.tensor_copy(xinT[:, e % 2, :], psW[:, 0, 0:CAP]).then_inc(xinT_ready, 1)

            def store_outputs(m):
                e, blk = blocks[m]
                dve.wait_ge(y_filled, m + 1)
                if e == 0:
                    dve.tensor_copy(res[:, 4 * blk:4 * blk + 4, :],
                                    ybank[m % 2].rearrange("p (t d) -> p t d", t=4)).then_inc(y_stored, 1)
                else:
                    if e > 2:
                        dve.wait_ge(y_saved[e % 2], 32 * ((e - 1) // 2))
                    dve.tensor_copy(yo[:, e % 2, 0:2, :],
                                    ybank[m % 2][:, 0:2 * D].rearrange("p (c d) -> p c d", c=2))
                    dve.tensor_copy(yo[0:CAP - 2 * P, e % 2, 2, :], ybank[m % 2][0:CAP - 2 * P, 2 * D:3 * D])\
                       .then_inc(y_stored, 1)

            dve.wait_ge(exp_b_loaded, 32)
            for m in range(len(blocks)):
                if blocks[m][0] > 0:
                    store_inputs(m)
                store_hidden(dve, m, 1)
                if m > 0:
                    store_outputs(m - 1)
            store_outputs(len(blocks) - 1)

            for n in range(4):
                dve.wait_ge(gathered, 16 * NT) if n == 0 else None
                dve.tensor_tensor(xs[:, 4 * n:4 * n + 4, :], xs[:, 4 * n:4 * n + 4, :],
                                  res[:, 4 * n:4 * n + 4, :], ALU.add).then_inc(final_ready, 1)

        @block.tensor
        def _(pe):
            pe.wait_ge(attn_w_loaded, 80)
            pe.wait_ge(dve_consts, 2)

            def body(s):
                def fill(name):
                    bank, u, w = W(s, name)
                    wait(pe, work_read[bank], u)
                    return work_filled[bank], w

                def stored(name):
                    bank, u, _ = W(s, name)
                    pe.wait_ge(work_read[bank], u + 1)

                def turn(name, src, ready, value):
                    pe.wait_ge(ready, value)
                    full, w = fill(name)
                    for c in range(2):
                        mm = pe.transpose(w[:, c * P:(c + 1) * P], src[:, c, :], ident)
                    mm.then_inc(full, 1)

                if s.F:
                    turn("xnT", xn, xn_ready, s.f + 1)
                if s.B:
                    turn("ctxT", cn, cn_ready, s.b + 1)
                if s.F:
                    for c in range(2):
                        full, w = fill(f"qkv{c}")
                        if c == 0:
                            stored("xnT")
                        pe.matmul(w[:, 0:3 * D], xnT[:, c * P:(c + 1) * P], wqkv_s[:, :], start=True, stop=True)\
                          .then_inc(full, 1)
                if s.B:
                    for n in range(4):
                        full, w = fill(f"kx{n}")
                        if n == 0:
                            stored("ctxT")
                        pe.matmul(w[:, 0:S], wk_s[:, n * P:(n + 1) * P], cT[:, :], start=True, stop=True)
                        pe.matmul(w[:, S:2 * S], wks_s[:, n * P:(n + 1) * P], cT[:, :], start=True, stop=True)\
                          .then_inc(full, 1)
                    for n in range(2):
                        full, w = fill(f"v{n}")
                        pe.matmul(w, cT[:, n * P:(n + 1) * P], wv_s[:, :], start=True, stop=True).then_inc(full, 1)
                if s.C:
                    turn("yT", yn, yn_ready, s.c + 1)
                if s.B:
                    turn("latT", ln, ln_ready, s.b + 1)
                    for n in range(2):
                        full, w = fill(f"v{2 + n}")
                        if n == 0:
                            stored("latT")
                        pe.matmul(w, lT[:, n * P:(n + 1) * P], wv_s[:, :], start=True, stop=True).then_inc(full, 1)
                    for name, weights in (("q", wq_s), ("kl", wk_s)):
                        for n in range(2):
                            full, w = fill(f"{name}{n}")
                            for m in range(2):
                                c = 2 * n + m
                                mm = pe.matmul(w[:, m * S:(m + 1) * S], weights[:, c * P:(c + 1) * P], lT[:, :],
                                               start=True, stop=True)
                            mm.then_inc(full, 1)
                if s.C:
                    full, w = fill("logits")
                    stored("yT")
                    for c in range(2):
                        mm = pe.matmul(w[:, c * NE:(c + 1) * NE], yTs[:, c * P:(c + 1) * P], wr_s[:, :],
                                       start=True, stop=True)
                    mm.then_inc(full, 1)
                if s.B:
                    pe.wait_ge(stacked, (s.b + 1) * 192)
                    for n in range(2 * XH):
                        h, c = n // 2, n % 2
                        full, w = fill(f"mx{n}")
                        pe.matmul(w, Q1[:, h, c * P:(c + 1) * P], KS[:, h, :], start=True, stop=True).then_inc(full, 1)
                if s.F:
                    pe.wait_ge(stack_ready, s.f + 1)
                    for kind, name in enumerate(("qS", "kS")):
                        full, w = fill(name)
                        wv_ = w.bitcast(F16).rearrange("p (g c t) -> p g c t", g=4, c=2)
                        for g in range(4):
                            for c in range(2):
                                src = stack[:, kind, c * NH + 4 * g:c * NH + 4 * g + 4, :, :].rearrange("p h s d -> p (h s d)")
                                mm = pe.transpose(wv_[:, g, c, :], src, id16[:, :])
                        mm.then_inc(full, 1)
                if s.B:
                    pe.wait_ge(negm_ready, s.b + 1)
                    full, w = fill("mT")
                    for c in range(2):
                        mm = pe.transpose(w[0:XH, :].bitcast(BF16)[:, c * P:(c + 1) * P], negm[:, c, :], idb[:, :])
                    mm.then_inc(full, 1)

                def scores(h):
                    wait(pe, exps_done, s.b * XH + h)
                    if h == 0:
                        stored("mT")
                    for c in range(KC):
                        dst = psS[:, c, :]
                        keys = KS[:, h, c * P:(c + 1) * P]
                        pe.matmul(dst, keys, Q1[:, h, :], start=True, stop=False)
                        pe.matmul(dst, keys, Q2[:, h, :], start=False, stop=False)
                        mm = pe.matmul(dst, sel_s[:, h * P:(h + 1) * P], mT[:, :], start=False, stop=True)
                    mm.then_inc(scores_done, 1)

                def weighted(h):
                    pe.wait_ge(exps_done, s.b * XH + h + 1)
                    wait(pe, oh_stored, s.b * XH + h)
                    for c in range(KC):
                        mm = pe.matmul(psPh[0:XD + 1, h % 2, :], V[:, c, h, :], E[:, h % 2, c, :],
                                       start=(c == 0), stop=(c == KC - 1))
                    mm.then_inc(pv_done, 1)

                def attention(g):
                    pe.wait_ge(vp_ready, s.a * 4 + g + 1)
                    wait(pe, ao_stored, s.a * 4 + g - 1)
                    for c in range(2):
                        for j in range(4):
                            h = 4 * g + j
                            mm = pe.matmul(psAg[32 * j:32 * j + DH + 2, g % 2, :], vp[:, h, c, :], X[:, h, c, :],
                                           start=(c == 0), stop=(c == 1), tile_position=(0, 32 * j))
                    mm.then_inc(av_done, 1)

                def cosines(g, pair):
                    if g == 0 and pair == 0:
                        stored("kS")
                    wait(pe, clip_done, s.f * 8 + 2 * g + pair)
                    for c in range(2):
                        for m in range(2):
                            j = 2 * pair + m
                            rows = slice(32 * j, 32 * j + 32)
                            mm = pe.matmul(psC[:, m, c * S:(c + 1) * S], kT[rows, g, c * P:(c + 1) * P], qT[rows, g, :],
                                           start=True, stop=True)
                    mm.then_inc(cos_done, 1)

                if s.B:
                    stored("v3")
                    scores(0)
                def turn_heads(n):
                    pe.wait_ge(oh_stored, s.b * XH + 2 * n + 2)
                    full, w = fill(f"pT{n}")
                    for m in range(2):
                        for q in range(2):
                            at = (2 * m + q) * (XD + 1)
                            mm = pe.transpose(w[:, at:at + XD + 1], oh[:, (2 * n + m) % 4, q * P:(q + 1) * P],
                                              ident[0:XD + 1, 0:XD + 1])
                    mm.then_inc(full, 1)

                for g in range(4):
                    if s.A:
                        attention(g)
                    if s.F:
                        cosines(g, 0)
                        cosines(g, 1)
                    if s.B:
                        scores(g + 1)
                        weighted(g)
                        if g == 2:
                            turn_heads(0)
                if s.B:
                    scores(5)
                    weighted(4)
                    turn_heads(1)
                if s.A:
                    pe.wait_ge(ao_stored, s.a * 4 + 4)
                    for q in range(2):
                        full, w = fill(f"ao{q}")
                        for g in range(4):
                            mm = pe.transpose(w[:, g * P:(g + 1) * P], aoT[:, g, q * P:(q + 1) * P], ident)
                        mm.then_inc(full, 1)
                if s.B:
                    scores(6)
                    weighted(5)
                    scores(7)
                    weighted(6)
                    turn_heads(2)
                if s.A:
                    turn("oT", o, o_ready, s.a + 1)
                    full, w = fill("att")
                    stored("oT")
                    for c in range(2):
                        pe.matmul(w[:, c * D:(c + 1) * D], ones_row[:, :], bout_s[:, :], start=True, stop=False)
                        mm = pe.matmul(w[:, c * D:(c + 1) * D], oT[:, c * P:(c + 1) * P], wout_s[:, :], start=False, stop=True)
                    mm.then_inc(full, 1)
                if s.B:
                    weighted(7)
                    turn_heads(3)
                    for n in range(2):
                        full, w = fill(f"o2T{n}")
                        if n == 0:
                            stored("pT3")
                        for m in range(2):
                            for q in range(2):
                                c = 2 * n + m
                                mm = pe.transpose(w[:, m * S + q * P:m * S + (q + 1) * P], o2[:, q, c * P:(c + 1) * P], ident)
                        mm.then_inc(full, 1)
                    full, w = fill("xo")
                    stored("o2T1")
                    for q in range(2):
                        for c in range(4):
                            mm = pe.matmul(w[:, q * D:(q + 1) * D], o2T[:, c, q * P:(q + 1) * P], wo_s[:, c, :],
                                           start=(c == 0), stop=(c == 3))
                    mm.then_inc(full, 1)

            each_step(pe, body)

            pe.wait_ge(pbc_ready, 1)
            for t in range(NT):
                mm = pe.transpose(ring[t // 4][:, (t % 4) * P:(t % 4 + 1) * P], pbc[:, t, :], ident)
            mm.then_inc(prow_filled, 1)
            pe.wait_ge(exp_w_loaded, 32)
            pe.wait_ge(exp_b_loaded, 32)
            pe.wait_ge(prow_ready, 1)

            count = [0, 0]

            def hidden(e, src, width):
                for c in range(FC):
                    n = count[0]
                    if n >= 4:
                        m = n - 4
                        pe.wait_ge(h_even if m % 2 == 0 else h_odd, m // 2 + 1)
                    pe.matmul(ring[n % 4][:, 0:width], w1_s[:, e, c * P:(c + 1) * P], src, start=True, stop=True)\
                      .then_inc(h_filled, 1)
                    count[0] += 1

            def outputs(e, tiles):
                m = count[1]
                pe.wait_ge(h_even, 2 * (m + 1))
                pe.wait_ge(h_odd, 2 * (m + 1))
                if m >= 2:
                    pe.wait_ge(y_stored, m - 1)
                at = 0
                for t, rows in enumerate(tiles):
                    dst = ybank[m % 2][0:rows, t * D:(t + 1) * D]
                    pe.matmul(dst, ones_row[:, 0:rows], b2_s[:, e * D:(e + 1) * D], start=True, stop=False)
                    for c in range(FC):
                        mm = pe.matmul(dst, hT[m % 2][:, c, at:at + rows], w2_s[:, e, c, :], start=False, stop=(c == FC - 1))
                    at += rows
                mm.then_inc(y_filled, 1)
                count[1] += 1

            pe.matmul(psR.rearrange("p t e -> p (t e)"), zb[:, :], zb[:, :], start=True, stop=False, skip_group_check=True)
            for j in range(NT):
                pe.wait_ge(g_ready, j + 1)
                for t in range(NT):
                    mm = pe.matmul(psR[:, t, :], G[:, j % 4, t * P:(t + 1) * P], hotb[:, j, :], start=False,
                                   stop=(j == NT - 1), skip_group_check=True)
                mm.then_inc(g_used, 1)
            pe.drain().then_inc(rank_done, 1)

            def inputs(m):
                e = blocks[m][0]
                pe.wait_ge(xin_loaded[(e - 1) % 4], 32 * ((e + 3) // 4))
                if e > 1:
                    pe.wait_ge(xinT_ready, e - 1)
                at = 0
                for c, rows in enumerate((P, P, CAP - 2 * P)):
                    mm = pe.transpose(psW[:, 0, at:at + rows], xin[0:rows, (e - 1) % 4, c, :], ident[0:rows, 0:rows])
                    at += rows
                mm.then_inc(xinT_filled, 1)
                pe.wait_ge(xinT_ready, e)

            def hidden(m):
                e, blk = blocks[m]
                src = yT[:, blk * FF:(blk + 1) * FF] if e == 0 else xinT[:, e % 2, :]
                for c in range(FC):
                    if m > 0:
                        pe.wait_ge(h_odd if c % 2 else h_even, 2 * (m - 1) + c // 2 + 1)
                    pe.matmul(ring[c][:, 0:FF if e == 0 else CAP], w1_s[:, e, c * P:(c + 1) * P], src,
                              start=True, stop=True).then_inc(h_filled, 1)

            def outputs(m):
                e, blk = blocks[m]
                pe.wait_ge(h_even, 2 * (m + 1))
                pe.wait_ge(h_odd, 2 * (m + 1))
                if m >= 2:
                    pe.wait_ge(y_stored, m - 1)
                at = 0
                for t, rows in enumerate((P, P, P, P) if e == 0 else (P, P, CAP - 2 * P)):
                    dst = ybank[m % 2][0:rows, t * D:(t + 1) * D]
                    pe.matmul(dst, ones_row[:, 0:rows], b2_s[:, e * D:(e + 1) * D], start=True, stop=False)
                    for c in range(FC):
                        mm = pe.matmul(dst, hT[m % 2][:, c, at:at + rows], w2_s[:, e, c, :], start=False, stop=(c == FC - 1))
                    at += rows
                mm.then_inc(y_filled, 1)

            for m in range(len(blocks)):
                if blocks[m][0] > 0:
                    inputs(m)
                hidden(m)
                if m > 0:
                    outputs(m - 1)
            outputs(len(blocks) - 1)

    return nc


def kernel(x, ctx_1024, L0_attn_w_qkv, L0_attn_b_qkv, L0_attn_w_out, L0_attn_b_out, L0_xattn_gamma_x,
           L0_xattn_beta_x, L0_xattn_gamma_l, L0_xattn_beta_l, L0_xattn_Wq, L0_xattn_Wkv, L0_xattn_Wo,
           L0_ffn_router_w, L0_ffn_W1, L0_ffn_b1, L0_ffn_W2, L0_ffn_b2):
    import concourse.bacc as bacc
    from concourse.bass_utils import run_bass_kernel_spmd

    cst, sel = shape_constants()
    wkv = np.asarray(L0_xattn_Wkv)
    wk = wkv[:, 0:INNER]
    arrays = {
        "x": np.asarray(x).reshape(NB * S, D),
        "ctx_in": np.asarray(ctx_1024).reshape(NB * S, D),
        "wqkv": np.asarray(L0_attn_w_qkv).T,
        "bqkv": np.broadcast_to(np.asarray(L0_attn_b_qkv), (P, 3 * D)),
        "wout": np.asarray(L0_attn_w_out).T,
        "bout": np.asarray(L0_attn_b_out).reshape(1, D),
        "gam": np.stack([np.asarray(a) for a in (L0_xattn_gamma_x, L0_xattn_beta_x, L0_xattn_gamma_l,
                                                 L0_xattn_beta_l)], axis=1),
        "wq": np.asarray(L0_xattn_Wq),
        "wk": wk,
        "wks": wk.reshape(D, XH, 2, XD // 2)[:, :, ::-1, :].reshape(D, INNER),
        "wv": wkv[:, INNER:],
        "wo": np.asarray(L0_xattn_Wo),
        "wr": np.asarray(L0_ffn_router_w).T,
        "w1": np.asarray(L0_ffn_W1),
        "b1": np.asarray(L0_ffn_b1).reshape(NE, FC, P).transpose(2, 0, 1).reshape(P, NE * FC),
        "w2": np.asarray(L0_ffn_W2),
        "b2": np.asarray(L0_ffn_b2).reshape(1, NE * D),
        "cst": cst,
        "sel": sel,
    }
    arrays = {f"in_{name}": np.ascontiguousarray(a) for name, a in arrays.items()}
    nc = bacc.Bacc("TRN2", target_bir_lowering=False, num_devices=1)
    args = [nc.dram_tensor(n, a.shape, mybir.dt.from_np(a.dtype), kind="ExternalInput").ap() for n, a in arrays.items()]
    out = nc.dram_tensor("out_x", (NB * S, D), F32, kind="ExternalOutput").ap()
    build(nc, *args, out)
    r = run_bass_kernel_spmd(nc, [arrays], core_ids=[0])
    return r.results[0]["out_x"].reshape(NB, S, D)
```

```python
import math
from contextlib import ExitStack

import numpy as np

import concourse.bass as bass
from concourse import mybir

ALU = mybir.AluOpType
ACT = mybir.ActivationFunctionType
AX = mybir.AxisListType.X
F32 = mybir.dt.float32
F16 = mybir.dt.float16
BF16 = mybir.dt.bfloat16
I32 = mybir.dt.int32

P = 128
NB, S, D = 8, 256, 128
NT = NB * S // P
NH, DH = 16, 8
XH, XD = 8, 64
INNER = XH * XD
KC = 2 * S // P
NE, FF = 8, 512
FC = FF // P
CAP = math.ceil(NB * S / NE * 1.25)
SLOTS = (NE - 1) * CAP
LN_EPS = 1e-5
CLIP = 1e-7
DECAY = -3.2
FAR = 100000
LE_TABLE, TA_TABLE = "natural_log_exp_and_others", "sigmoid_and_others"

C_ID, C_ROPE, C_TRI, C_EXP, C_FAR, C_END = 0, 128, 128 + 512, 768, 776, 792


def shape_constants():
    c = np.zeros((P, C_END), np.float32)
    c[:, C_ID:C_ID + P] = np.eye(P)
    half = XD // 2
    inv = (1.0 / 10000.0 ** (np.arange(0, XD, 2, dtype=np.float32) / XD)).astype(np.float32)
    theta = np.arange(S, dtype=np.float32)[None, :] * inv[:, None]
    row = np.arange(P) % XD
    ang = theta[row % half]
    c[:, C_ROPE:C_ROPE + S] = np.cos(ang)
    c[:, C_ROPE + S:C_ROPE + 2 * S] = np.sin(ang) * np.where(row < half, -1.0, 1.0)[:, None]
    c[:, C_TRI:C_TRI + P] = np.arange(P)[:, None] < np.arange(P)[None, :]
    c[:, C_EXP:C_EXP + NE] = np.arange(NE) - NE
    c[:, C_FAR:C_FAR + NT] = FAR + np.arange(P)[:, None] + P * np.arange(NT)[None, :]
    sel = np.zeros((XH, XH, P), np.float32)
    sel[np.arange(XH), np.arange(XH), :] = 1.0
    return c, sel.reshape(XH, XH * P)


class Step:

    def __init__(self, t=None, r=None):
        self.t = t
        if r is None:
            self.f, self.a, self.b, self.c = t + 1, t, t - 1, t - 2
            self.F, self.A, self.B, self.C = (0 <= n < NB for n in (t + 1, t, t - 1, t - 2))
        else:
            self.f, self.a, self.b, self.c = r + 3, r + 2, r + 1, r
            self.F = self.A = self.B = self.C = True
            self.t = None
            self.r = r

    def uses(self):
        u = []
        u += ["xnT"] * self.F + ["ctxT", "ao0", "ao1"] * self.B + ["pT1"] * self.C + ["qkv0", "qkv1"] * self.F
        u += ["oT", "att", "kx0", "kx1"] * self.B + ["pT2"] * self.C + ["kx2", "kx3", "latT"] * self.B
        u += ["pT3"] * self.C + ["q0", "q1"] * self.B + ["qS", "kS"] * self.F + ["kl0", "kl1"] * self.B
        u += [f"mx{n}" for n in range(2 * XH)] * self.B + ["mT"] * self.B
        u += ["o2T0", "o2T1", "xo", "yT", "logits"] * self.C + ["pT0"] * self.B
        return u

    def use(self, name):
        here = self.uses()
        at = here.index(name)
        bank = at % 2
        local = at // 2
        def rises(t):
            n = len(Step(t).uses())
            return (n + 1 - bank) // 2
        if self.t is not None:
            return bank, sum(rises(t) for t in range(-1, self.t)) + local
        before = sum(rises(t) for t in range(-1, 2))
        return bank, self.r * rises(2) + (before + local)


def each_step(engine, body):
    for t in (-1, 0, 1):
        body(Step(t))
    with engine.Fori(0, 5) as r:
        body(Step(r=r))
    for t in (7, 8, 9):
        body(Step(t))


def wait(engine, sem, value):
    if not isinstance(value, int) or value > 0:
        engine.wait_ge(sem, value)


def build(nc, x, ctx_in, wqkv, bqkv, wout, bout, gam, wq, wk, wks, wv, wo, wr, w1, b1, w2, b2, cst, sel, out):
    ctx = ExitStack()
    with ctx:
        def sb(name, shape, dt=F32):
            return ctx.enter_context(nc.sbuf_tensor(name, shape, dt))

        def pb(name, shape, dt=F32):
            return ctx.enter_context(nc.psum_tensor(name, shape, dt))

        def sem(name):
            return ctx.enter_context(nc.semaphore(name))

        xs = sb("xs", [P, NT, D])
        cx = sb("cx", [P, NT, D])
        vall = sb("vall", [P, NT, D])
        y3 = vall
        yT = cx[:, :, :].rearrange("p t d -> p (t d)")
        lgs = sb("lgs", [P, NT, NE])
        wqkv_s = sb("wqkv_s", [P, 3 * D])
        bqkv_s = sb("bqkv_s", [P, 3 * D])
        wout_s = sb("wout_s", [P, D])
        bout_s = sb("bout_s", [1, D])
        gam_s = sb("gam_s", [P, 4])
        wq_s = sb("wq_s", [P, INNER])
        wk_s = sb("wk_s", [P, INNER])
        wks_s = sb("wks_s", [P, INNER])
        wv_s = sb("wv_s", [P, INNER])
        wo_s = sb("wo_s", [P, 4, D])
        wr_s = sb("wr_s", [P, NE])
        b1_s = sb("b1_s", [P, NE, FC])
        b2_s = sb("b2_s", [1, NE * D])
        cst_s = sb("cst_s", [P, C_END])
        sel_s = sb("sel_s", [P, XH * P], BF16)
        id16 = sb("id16", [P, P], F16)
        idb = sb("idb", [P, P], BF16)
        ones_row = sb("ones_row", [1, P])
        cols = sb("cols", [P, 2])
        ident = cst_s[:, C_ID:C_ID + P]
        rope = cst_s[:, C_ROPE:C_ROPE + 2 * S]

        st = sb("st", [P, 2 * NT, 6])
        mv = sb("mv", [P, 2 * NT, 2])
        lnrs = sb("lnrs", [P, 2 * NT])
        lnvar = sb("lnvar", [P, 2 * NT])
        st2 = sb("st2", [P, 4, 6])
        mv2 = sb("mv2", [P, 4, 2])
        var4 = sb("var4", [P, 4])
        lv4 = sb("lv4", [P, 4])
        rs4 = sb("rs4", [P, 4])

        xn = sb("xn", [P, 2, D])
        xnT = sb("xnT", [P, S])
        qk = sb("qk", [P, 2, 2 * D])
        ss = sb("ss", [P, 2, 2, NH])
        l2 = sb("l2", [P, 2, 2, NH])
        qn = sb("qn", [P, 2, 2, D])
        sq = qn[:, :, :, :].rearrange("p k c d -> p k (c d)")
        stack = sb("stack", [P, 2, 2 * NH, 4, DH], F16)
        qT = sb("qT", [P, 4, S], F16)
        kT = sb("kT", [P, 4, S], F16)
        X = sb("X", [P, NH, 2, S])
        L = sb("L", [P, NH, 2, S])
        ncol = sb("ncol", [P, NH, 2])
        rcol = sb("rcol", [P, NH, 2])
        vp = sb("vp", [P, NH, 2, DH + 2])
        aoT = sb("aoT", [P, 4, S])
        den = sb("den", [P, 2, NH])
        rden = sb("rden", [P, 2, NH])
        o = sb("o", [P, 2, D])
        oT = sb("oT", [P, S])

        cn = sb("cn", [P, 2, D])
        cT = sb("cT", [P, S])
        ln = sb("ln", [P, 2, D])
        lT = sb("lT", [P, S])
        kcs = sb("kcs", [P, 4, 2, S])
        kf = sb("kf", [P, 4, 2 * S])
        qf = sb("qf", [P, XH, S])
        kb = kf[:, :, :].bitcast(BF16)
        qb = qf[:, :, :].bitcast(BF16)
        V = sb("V", [P, KC, XH, XD + 1])
        mx = sb("mx", [P, 2, XH])
        negm = sb("negm", [P, 2, XH], BF16)
        mT = sb("mT", [P, S], BF16)
        E = sb("E", [P, 2, KC, S])
        sel_f = E[:, :, :, :].rearrange("p a b c -> p (a b c)")[0:XH, 0:XH * P]
        rpv = sb("rpv", [P, 2, 4])
        oh = sb("oh", [XD + 1, 4, S])
        o2 = sb("o2", [P, 2, INNER])
        o2T = sb("o2T", [P, 4, S])
        yn = sb("yn", [P, 2, D])
        yTs = sb("yTs", [P, S])

        Xf = X[:, :, :, :].rearrange("p a b c -> p (a b c)")
        w1_s = Xf[:, 0:NE * FF].rearrange("p (e f) -> p e f", e=NE)
        w2_s = Xf[:, NE * FF:2 * NE * FF].rearrange("p (e c d) -> p e c d", e=NE, c=FC)
        Lf = L[:, :, :, :].rearrange("p a b c -> p (a b c)")
        res = Lf[:, 0:NT * D].rearrange("p (t d) -> p t d", t=NT)
        pbc = Lf[:, 0:NT * P].rearrange("p (t q) -> p t q", t=NT)
        prow = Lf[:, NT * P:2 * NT * P]
        G = Lf[:, 2 * NT * P:4 * NT * P].bitcast(BF16).rearrange("p (r q) -> p r q", r=4)
        o2f = o2[:, :, :].rearrange("p a b -> p (a b)")
        probs, tmp8, hot = (o2f[:, n * NT * NE:(n + 1) * NT * NE].rearrange("p (t e) -> p t e", t=NT) for n in range(3))
        hotb = o2f[:, 768:768 + NT * NE // 2].bitcast(BF16).rearrange("p (t e) -> p t e", t=NT)
        dest = o2f[:, 832:832 + NT].bitcast(I32)
        r16 = o2f[:, 848:848 + 6 * NT].rearrange("p (n t) -> p n t", n=6)
        eqd = o2f[:, 512:512 + 2 * P].rearrange("p (r q) -> p r q", r=2)
        zero = aoT[:, :, :].rearrange("p g q -> p (g q)")[:, 0:CAP]
        zb = sb("zb", [P, P], BF16)
        xin = E[:, :, :, :].rearrange("p a b c -> p (a b c)")[:, 0:4 * 3 * D].rearrange("p (r c d) -> p r c d", r=4, c=3)
        xinT = kcs[:, :, :, :].rearrange("p a b c -> p (a b c)")[:, 0:2 * CAP].rearrange("p (r s) -> p r s", r=2)
        hT = [kf, sb("hT1", [P, FC, 2 * S])]
        yo = o2T[:, :, :].rearrange("p a b -> p (a b)")[:, 0:2 * 3 * D].rearrange("p (r c d) -> p r c d", r=2, c=3)

        x_slots = nc.dram_tensor("x_slots", (SLOTS, D), F32, kind="Internal").ap()
        y_slots = nc.dram_tensor("y_slots", (SLOTS, D), F32, kind="Internal").ap()

        psW = pb("psW", [P, 2, 512])
        psC = pb("psC", [P, 2, 512])
        psS = pb("psS", [P, KC, S])
        psA = pb("psA", [P, 512])
        psP = pb("psP", [P, 512])
        psAg = psA[:, :].rearrange("p (g q) -> p g q", g=2)
        psPh = psP[:, :].rearrange("p (h q) -> p h q", h=2)
        ring = [psC[:, 0, :], psC[:, 1, :], psS[:, 0:2, :].rearrange("p a b -> p (a b)"),
                psS[:, 2:4, :].rearrange("p a b -> p (a b)")]
        psR = psA[:, 0:NT * NE].rearrange("p (t e) -> p t e", t=NT)

        x_loaded, ctx_loaded, attn_w_loaded = sem("x_loaded"), sem("ctx_loaded"), sem("attn_w_loaded")
        xattn_w_loaded, exp_b_loaded, exp_w_loaded = sem("xattn_w_loaded"), sem("exp_b_loaded"), sem("exp_w_loaded")
        dve_consts = sem("dve_consts")
        x_var_ready, x_rs_ready = sem("x_var_ready"), sem("x_rs_ready")
        work_filled = [sem(f"work_filled{n}") for n in range(2)]
        work_read = [sem(f"work_read{n}") for n in range(2)]
        xn_ready, ss_ready, l2_ready, stack_ready = sem("xn_ready"), sem("ss_ready"), sem("l2_ready"), sem("stack_ready")
        cos_done, clip_done, ln_done, diff_done = sem("cos_done"), sem("clip_done"), sem("ln_done"), sem("diff_done")
        act_chain, kern_done, vp_ready, av_done = sem("act_chain"), sem("kern_done"), sem("vp_ready"), sem("av_done")
        ao_stored, o_ready, oh_stored = sem("ao_stored"), sem("o_ready"), sem("oh_stored")
        x1_var_ready, x1_rs_ready = sem("x1_var_ready"), sem("x1_rs_ready")
        x2_var_ready, x2_rs_ready = sem("x2_var_ready"), sem("x2_rs_ready")
        cn_ready, ln_ready, yn_ready = sem("cn_ready"), sem("ln_ready"), sem("yn_ready")
        heads_ready = sem("heads_ready")
        fold_done = sem("fold_done")
        v_filled, v_stored = sem("v_filled"), sem("v_stored")
        negm_ready, scores_done, exps_done, pv_done = sem("negm_ready"), sem("scores_done"), sem("exps_done"), sem("pv_done")
        lg_sub, lg_exp, pbc_ready, prow_filled, prow_ready = sem("lg_sub"), sem("lg_exp"), sem("pbc_ready"), sem("prow_filled"), sem("prow_ready")
        g_ready, g_used, rank_done, dest_ready = sem("g_ready"), sem("g_used"), sem("rank_done"), sem("dest_ready")
        zeroed, scattered = sem("zeroed"), sem("scattered")
        xin_loaded = [sem(f"xin_loaded{n}") for n in range(4)]
        xinT_filled, xinT_ready = sem("xinT_filled"), sem("xinT_ready")
        h_filled, h_stored, y_filled, y_stored = sem("h_filled"), sem("h_stored"), sem("y_filled"), sem("y_stored")
        gathered, final_ready, out_done = sem("gathered"), sem("final_ready"), sem("out_done")
        y_saved = [sem(f"y_saved{n}") for n in range(2)]

        block = ctx.enter_context(nc.Block())

        def W(s, name):
            bank, n = s.use(name)
            return bank, n, psW[:, bank, :]

        blocks = [(0, blk) for blk in range(4)] + [(e, 0) for e in range(1, NE)]

        def store_hidden(eng, m, first):
            e, _ = blocks[m]
            width = FF if e == 0 else CAP
            if m >= 2:
                eng.wait_ge(y_filled, m - 1)
            for c in range(first, FC, 2):
                eng.wait_ge(h_filled, FC * m + c + 1)
                dst, src, bias = hT[m % 2][:, c, 0:width], ring[c][:, 0:width], b1_s[:, e, c:c + 1]
                if first == 0:
                    eng.activation(dst, src, ACT.Relu, bias=bias).then_inc(h_even, 1)
                else:
                    eng.tensor_scalar(dst, src, bias, 0.0, ALU.add, ALU.max).then_inc(h_odd, 1)

        h_even, h_odd = sem("h_even"), sem("h_odd")
        ybank = [psP[:, :], psW[:, 1, :]]

        @block.sync
        def _(sp):
            sp.dma_start(xs[:, :, :], x.rearrange("(t p) d -> p t d", p=P)).then_inc(x_loaded, 16)
            for dst, src in ((cst_s, cst), (wqkv_s, wqkv), (bqkv_s, bqkv), (wout_s, wout), (bout_s, bout)):
                sp.dma_start(dst[:, :], src).then_inc(attn_w_loaded, 16)
            sp.dma_start(cx[:, :, :], ctx_in.rearrange("(t p) d -> p t d", p=P)).then_inc(ctx_loaded, 16)
            for dst, src in ((gam_s, gam), (wk_s, wk), (wks_s, wks), (wv_s, wv), (wq_s, wq), (sel_f, sel), (wr_s, wr)):
                sp.dma_start(dst if dst is sel_f else dst[:, :], src).then_inc(xattn_w_loaded, 16)
            sp.dma_start(wo_s[:, :, :], wo.rearrange("(c p) d -> p c d", p=P)).then_inc(xattn_w_loaded, 16)
            sp.dma_start(b1_s[:, :, :], b1.rearrange("p (e c) -> p e c", e=NE)).then_inc(exp_b_loaded, 16)
            sp.dma_start(b2_s[:, :], b2).then_inc(exp_b_loaded, 16)
            sp.wait_ge(dve_consts, 1)
            for n in range(NE - 1):
                rows = x_slots[n * CAP:(n + 1) * CAP, :].rearrange("a d -> (a d)").rearrange("(p f) -> p f", p=P)
                sp.dma_start(rows, zero[:, :]).then_inc(zeroed, 16)

            sp.wait_ge(av_done, 4 * NB)
            sp.dma_start(w1_s, w1.rearrange("e p f -> p e f")).then_inc(exp_w_loaded, 16)
            sp.dma_start(w2_s, w2.rearrange("e (c p) d -> p e c d", p=P)).then_inc(exp_w_loaded, 16)

            sp.wait_ge(scattered, 16 * NT)
            for e in range(1, NE):
                r = (e - 1) % 4
                if e > 4:
                    sp.wait_ge(xinT_filled, e - 4)
                row = (e - 1) * CAP
                sp.dma_start(xin[:, r, 0:2, :], x_slots[row:row + 2 * P, :].rearrange("(c p) d -> p c d", p=P))\
                  .then_inc(xin_loaded[r], 16)
                sp.dma_start(xin[0:CAP - 2 * P, r, 2, :], x_slots[row + 2 * P:row + CAP, :]).then_inc(xin_loaded[r], 16)
            for e in range(1, NE):
                r = e % 2
                sp.wait_ge(y_stored, 4 + e)
                row = (e - 1) * CAP
                sp.dma_start(y_slots[row:row + 2 * P, :].rearrange("(c p) d -> p c d", p=P), yo[:, r, 0:2, :])\
                  .then_inc(y_saved[r], 16)
                sp.dma_start(y_slots[row + 2 * P:row + CAP, :], yo[0:CAP - 2 * P, r, 2, :]).then_inc(y_saved[r], 16)
            out_v = out.rearrange("(t p) d -> p t d", p=P)
            for n in range(4):
                sp.wait_ge(final_ready, n + 1)
                sp.dma_start(out_v[:, 4 * n:4 * n + 4, :], xs[:, 4 * n:4 * n + 4, :]).then_inc(out_done, 16)
            sp.wait_ge(out_done, 64)
            for r in range(2):
                sp.wait_ge(y_saved[r], 32 * len(range(r or 2, NE, 2)))
            sp.wait_ge(zeroed, 16 * 7)

        @block.gpsimd
        def _(pool):
            def body(s):
                if not s.A:
                    return
                for g in range(4):
                    pool.wait_ge(ln_done, s.a * 4 + g + 1)
                    pool.tensor_tensor(X[:, 4 * g:4 * g + 4, :, :], X[:, 4 * g:4 * g + 4, :, :],
                                       L[:, 4 * g:4 * g + 4, :, :], ALU.subtract).then_inc(diff_done, 1)

                for g in range(4):
                    hs = slice(4 * g, 4 * g + 4)
                    pool.wait_ge(kern_done, s.a * 4 + g + 1)
                    pool.tensor_tensor(L[:, hs, :, 0:P], X[:, hs, :, 0:P], X[:, hs, :, P:S], ALU.add)
                    pool.drain()
                    pool.tensor_tensor(L[:, hs, :, P:P + P // 2], L[:, hs, :, 0:P // 2], L[:, hs, :, P // 2:P], ALU.add)\
                        .then_inc(fold_done, 1)

            each_step(pool, body)

            pool.wait_ge(dest_ready, 1)
            pool.wait_ge(zeroed, 16 * 7)
            for t in range(NT):
                pool.indirect_dma_start(x_slots, bass.IndirectOffsetOnAxis(ap=dest[:, t:t + 1], axis=0),
                                        y3[:, t, :], None, bounds_check=SLOTS - 1, oob_is_err=False)\
                    .then_inc(scattered, 16)
            for r in range(2):
                pool.wait_ge(y_saved[r], 32 * len(range(r or 2, NE, 2)))
            pool.wait_ge(y_stored, 4)
            for t in range(NT):
                pool.indirect_dma_start(res[:, t, :], None, y_slots,
                                        bass.IndirectOffsetOnAxis(ap=dest[:, t:t + 1], axis=0),
                                        bounds_check=SLOTS - 1, oob_is_err=False).then_inc(gathered, 16)

        @block.scalar
        def _(act):
            act.preload_act_table_set(LE_TABLE)
            act.wait_ge(x_var_ready, 1)
            act.activation(lnrs[:, :], lnvar[:, :], ACT.Ln)
            act.drain()
            act.activation(lnrs[:, :], lnrs[:, :], ACT.Exp, scale=-0.5).then_inc(x_rs_ready, 1)

            def head(n, h):
                act.wait_ge(scores_done, n * XH + h + 1)
                wait(act, pv_done, n * XH + h - 1)
                act.activation(E[:, h % 2, :, :], psS[:, :, :], ACT.Exp).then_inc(exps_done, 1)

            def store_head(n, h):
                act.wait_ge(pv_done, n * XH + h + 1)
                act.activation(oh[:, h % 4, :], psPh[0:XD + 1, h % 2, :], ACT.Copy).then_inc(oh_stored, 1)

            def inv_std(c, var, rs, value):
                act.wait_ge(var, value)
                act.activation(lv4[:, c:c + 2], var4[:, c:c + 2], ACT.Ln)
                act.drain()
                act.activation(rs4[:, c:c + 2], lv4[:, c:c + 2], ACT.Exp, scale=-0.5).then_inc(rs, 1)

            def body(s):
                def value_tiles(n):
                    if n == 0:
                        wait(act, pv_done, s.b * XH)
                    act.wait_ge(v_filled, 2 * s.b + n + 1)
                    act.activation(V[:, 2 - 2 * n:4 - 2 * n, :, 0:XD],
                                   psS[:, :, :].rearrange("p (t c) (h d) -> p t (c h) d", t=2, d=XD), ACT.Copy)\
                       .then_inc(v_stored, 1)

                for g in range(4):
                    if s.C:
                        head(s.c, 4 + g)
                        store_head(s.c, 3 + g)
                    if s.A:
                        hs = slice(4 * g, 4 * g + 4)
                        act.wait_ge(clip_done, s.a * 8 + 2 * g + 2)
                        act.activation(L[:, hs, :, :], X[:, hs, :, :], ACT.Ln, bias=1.0)
                        act.activation(X[:, hs, :, :], X[:, hs, :, :], ACT.Ln, bias=1.0, scale=-1.0)\
                           .then_inc(ln_done, 1)
                    if g == 2 and s.B:
                        inv_std(0, x1_var_ready, x1_rs_ready, s.b + 1)
                    if g == 2 and s.F:
                        act.wait_ge(ss_ready, s.f + 1)
                        act.activation(l2[:, :, :, :], ss[:, :, :, :], ACT.Ln)
                        act.drain()
                        act.activation(l2[:, :, :, :], l2[:, :, :, :], ACT.Exp, scale=-0.5).then_inc(l2_ready, 1)
                if s.C:
                    store_head(s.c, XH - 1)
                if s.A:
                    act.preload_act_table_set(TA_TABLE)
                    for g in range(4):
                        act.wait_ge(diff_done, s.a * 4 + g + 1)
                        xg = X[:, 4 * g:4 * g + 4, :, :]
                        act.activation(xg, xg, ACT.Tanh, scale=0.25).then_inc(act_chain, 1)
                if s.B:
                    value_tiles(0)
                if s.A:
                    for g in range(4):
                        act.wait_ge(act_chain, s.a * 12 + g + 1)
                        xg = X[:, 4 * g:4 * g + 4, :, :]
                        act.activation(xg, xg, ACT.Arctan).then_inc(act_chain, 1)
                        if g == 2 and s.B:
                            value_tiles(1)
                    act.preload_act_table_set(LE_TABLE)
                elif s.B:
                    value_tiles(1)

                def log_angle(g):
                    act.wait_ge(act_chain, s.a * 12 + 4 + g + 1)
                    xg = X[:, 4 * g:4 * g + 4, :, :]
                    act.activation(xg, xg, ACT.Ln, bias=cols[:, 0:1], scale=2.0).then_inc(act_chain, 1)

                def kernel_value(g):
                    act.wait_ge(act_chain, s.a * 12 + 8 + g + 1)
                    xg = X[:, 4 * g:4 * g + 4, :, :]
                    act.activation(xg, xg, ACT.Exp, scale=DECAY).then_inc(kern_done, 1)

                if s.A:
                    log_angle(0)
                    log_angle(1)
                    kernel_value(0)
                for g in range(4):
                    if s.A and g < 2:
                        log_angle(g + 2)
                    if s.A and g < 2:
                        kernel_value(g + 1)
                    if s.A and g == 1:
                        kernel_value(3)
                    if s.B:
                        head(s.b, g)
                        if g > 0:
                            store_head(s.b, g - 1)
                    if s.C and g == 1:
                        inv_std(2, x2_var_ready, x2_rs_ready, s.c + 1)
            each_step(act, body)

            act.wait_ge(lg_sub, 1)
            act.activation(probs[:, :, :], tmp8[:, :, :], ACT.Exp).then_inc(lg_exp, 1)
            act.wait_ge(exp_b_loaded, 32)
            for m in range(len(blocks)):
                store_hidden(act, m, 0)

        def norm_pair(dve, dst, src, mean, rs, done):
            for c in range(2):
                last = dve.tensor_scalar(dst(c), src(c), mean(c), rs(c), ALU.subtract, ALU.mult)
            last.then_inc(done, 1)

        @block.vector
        def _(dve):
            dve.memset(zero[:, :], 0.0).then_inc(dve_consts, 1)
            dve.memset(zb[:, :], 0.0)
            dve.memset(qf[:, :, :], 0.0)
            dve.memset(sel_s[:, :], 0.0)
            dve.memset(mT[:, :], 0.0)
            dve.memset(ones_row[:, :], 1.0)
            dve.memset(cols[:, 0:1], 1.0 + math.pi / 2)
            dve.memset(vp[:, :, :, DH + 1:DH + 2], 1.0)
            dve.memset(V[:, :, :, XD:XD + 1], 1.0)
            dve.memset(psA[:, :], 0.0)
            dve.wait_ge(x_loaded, 16)
            for t in range(NT):
                dve.bn_stats(st[:, t, :], xs[:, t, :])
            dve.wait_ge(ctx_loaded, 16)
            for t in range(NT):
                dve.bn_stats(st[:, NT + t, :], cx[:, t, :])
            dve.drain()
            for t in range(2 * NT):
                dve.bn_aggr(mv[:, t, :], st[:, t, :])
            dve.drain()
            dve.tensor_scalar(lnvar[:, :], mv[:, :, 1], LN_EPS, None, ALU.add).then_inc(x_var_ready, 1)
            dve.wait_ge(attn_w_loaded, 80)
            dve.tensor_copy(id16[:, :], ident)
            dve.tensor_copy(idb[:, :], ident)
            dve.wait_ge(xattn_w_loaded, 128)
            dve.tensor_copy(sel_s[0:XH, :], sel_f).then_inc(dve_consts, 1)
            dve.wait_ge(x_rs_ready, 1)

            def flat(ap):
                return ap.rearrange("p a b -> p (a b)")

            def body(s):
                def filled(name):
                    bank, u, w = W(s, name)
                    dve.wait_ge(work_filled[bank], u + 1)
                    return work_read[bank], w

                def norm_heads(n):
                    read, w = filled(f"pT{n}")
                    heads = w[:, 0:4 * (XD + 1)].rearrange("p (h q d) -> p h q d", h=2, q=2)
                    dve.reciprocal(rpv[:, n % 2, :].rearrange("p (h q) -> p h q", h=2), heads[:, :, :, XD])
                    dve.drain()
                    dst = o2[:, :, 2 * n * XD:(2 * n + 2) * XD].rearrange("p q (h d) -> p h q d", h=2)
                    dve.tensor_tensor(dst, heads[:, :, :, 0:XD],
                                      rpv[:, n % 2, :].rearrange("p (h q a) -> p h q a", h=2, a=1).to_broadcast([P, 2, 2, XD]),
                                      ALU.mult).then_inc(read, 1)

                def statistics(c, sources, scale, shift, ready):
                    dve.drain()
                    for n, src in enumerate(sources):
                        dve.bn_stats(st2[:, c + n, :], src)
                    dve.drain()
                    for n in range(2):
                        dve.bn_aggr(mv2[:, c + n, :], st2[:, c + n, :])
                    dve.drain()
                    dve.tensor_scalar(var4[:, c:c + 2], mv2[:, c:c + 2, 1], scale, shift, ALU.mult, ALU.add).then_inc(ready, 1)

                if s.F:
                    norm_pair(dve, lambda c: xn[:, c, :], lambda c: flat(xs[:, bass.ds(2 * s.f + c, 1), :]),
                              lambda c: flat(mv[:, bass.ds(2 * s.f + c, 1), 0:1]),
                              lambda c: lnrs[:, bass.ds(2 * s.f + c, 1)], xn_ready)
                if s.B:
                    norm_pair(dve, lambda c: cn[:, c, :], lambda c: flat(cx[:, bass.ds(2 * s.b + c, 1), :]),
                              lambda c: flat(mv[:, bass.ds(NT + 2 * s.b + c, 1), 0:1]),
                              lambda c: lnrs[:, bass.ds(NT + 2 * s.b + c, 1)], cn_ready)
                if s.F:
                    read, w = filled("xnT")
                    dve.tensor_copy(xnT[:, :], w[:, 0:S]).then_inc(read, 1)
                if s.B:
                    read, w = filled("ctxT")
                    dve.tensor_scalar(cT[:, :], w[:, 0:S], gam_s[:, 0:1], gam_s[:, 1:2], ALU.mult, ALU.add)\
                       .then_inc(read, 1)
                if s.B:
                    aos = []
                    for q in range(2):
                        read, w = filled(f"ao{q}")
                        aos.append((read, w.rearrange("p (h d) -> p h d", h=NH)))
                        dve.tensor_scalar(den[:, q, :], aos[q][1][:, :, DH + 1], 1e-12, None, ALU.mult)
                    dve.drain()
                    for q in range(2):
                        dve.tensor_tensor(den[:, q, :], den[:, q, :], aos[q][1][:, :, DH], ALU.max)
                    dve.drain()
                    dve.reciprocal(rden[:, :, :], den[:, :, :])
                    dve.drain()
                    for q in range(2):
                        dve.tensor_tensor(o[:, q, :].rearrange("p (h d) -> p h d", h=NH), aos[q][1][:, :, 0:DH],
                                          rden[:, q, :].rearrange("p (h a) -> p h a", a=1).to_broadcast([P, NH, DH]),
                                          ALU.mult).then_inc(aos[q][0], 1)
                    dve.drain().then_inc(o_ready, 1)
                if s.C:
                    norm_heads(1)
                if s.F:
                    for c in range(2):
                        read, w = filled(f"qkv{c}")
                        dve.tensor_tensor(qk[:, c, :], w[:, 0:2 * D], bqkv_s[:, 0:2 * D], ALU.add)
                        dve.tensor_tensor(flat(vall[:, bass.ds(2 * s.f + c, 1), :]), w[:, 2 * D:3 * D],
                                          bqkv_s[:, 2 * D:3 * D], ALU.add).then_inc(read, 1)
                if s.B:
                    read, w = filled("oT")
                    dve.tensor_copy(oT[:, :], w[:, 0:S]).then_inc(read, 1)
                    read, w = filled("att")
                    xa = xs[:, bass.ds(2 * s.b, 2), :]
                    dve.tensor_tensor(xa, xa,
                                      w[:, 0:S].rearrange("p (c d) -> p c d", c=2), ALU.add).then_inc(read, 1)
                    statistics(0, [flat(xs[:, bass.ds(2 * s.b + c, 1), :]) for c in range(2)],
                               1.0 + LN_EPS, LN_EPS * LN_EPS, x1_var_ready)
                if s.F:
                    dve.drain()
                    dve.tensor_tensor(sq, qk[:, :, :], qk[:, :, :], ALU.mult)
                    dve.drain()
                    dve.tensor_reduce(out=ss[:, :, :, :].rearrange("p c k h -> p (c k h)"),
                                      in_=sq.rearrange("p c (g d) -> p (c g) d", d=DH), op=ALU.add, axis=AX)
                    dve.drain()
                    dve.tensor_scalar(ss[:, :, :, :], ss[:, :, :, :], 1e-24, None, ALU.max).then_inc(ss_ready, 1)

                def rotary_keys(n):
                    read, w = filled(f"kx{n}")
                    dve.tensor_tensor(kcs[:, n, :, :].rearrange("p a b -> p (a b)"), w, rope, ALU.mult).then_inc(read, 1)

                if s.B:
                    rotary_keys(0)
                    rotary_keys(1)
                if s.C:
                    norm_heads(2)
                if s.B:
                    rotary_keys(2)
                    rotary_keys(3)
                    dve.wait_ge(x1_rs_ready, s.b + 1)
                    norm_pair(dve, lambda c: ln[:, c, :], lambda c: flat(xs[:, bass.ds(2 * s.b + c, 1), :]),
                              lambda c: mv2[:, c, 0:1], lambda c: rs4[:, c:c + 1], ln_ready)
                    read, w = filled("latT")
                    dve.tensor_scalar(lT[:, :], w[:, 0:S], gam_s[:, 2:3], gam_s[:, 3:4], ALU.mult, ALU.add)\
                       .then_inc(read, 1)
                if s.F:
                    dve.wait_ge(l2_ready, s.f + 1)
                    for kind in range(2):
                        dve.tensor_tensor(
                            qn[:, kind, :, :].rearrange("p c (h d) -> p c h d", h=NH),
                            qk[:, :, kind * D:kind * D + D].rearrange("p c (h d) -> p c h d", h=NH),
                            l2[:, :, kind, :].rearrange("p c (h a) -> p c h a", a=1).to_broadcast([P, 2, NH, DH]), ALU.mult)
                    dve.drain()

                    def twice(ap):
                        return ap.rearrange("p g (a d) -> p g a d", a=1).to_broadcast([P, 2 * NH, 2, DH])

                    for kind in range(2):
                        unit = qn[:, kind, :, :].rearrange("p c (h d) -> p (c h) d", h=NH)
                        high = stack[:, kind, :, 0:3:2, :] if kind == 0 else stack[:, kind, :, 0:2, :]
                        dve.tensor_copy(high, twice(unit))
                    dve.drain()
                    for kind in range(2):
                        unit = qn[:, kind, :, :].rearrange("p c (h d) -> p (c h) d", h=NH)
                        low = stack[:, kind, :, 1:4:2, :] if kind == 0 else stack[:, kind, :, 2:4, :]
                        last = dve.tensor_tensor(low, twice(unit), twice(stack[:, kind, :, 0, :]), ALU.subtract)
                    last.then_inc(stack_ready, 1)
                if s.C:
                    norm_heads(3)
                if s.B:
                    dve.tensor_tensor(kf[:, :, 0:S], kcs[:, :, 0, :], kcs[:, :, 1, :], ALU.add)
                    for n in range(2):
                        read, w = filled(f"q{n}")
                        for odd in range(2):
                            rows = slice(XD * odd, XD * odd + XD)
                            last = dve.tensor_scalar(qf[rows, 4 * n + odd:4 * n + 4:2, :],
                                                     w[rows, :].rearrange("p (a b) -> p a b", a=2),
                                                     XD ** -0.5, None, ALU.mult)
                        last.then_inc(read, 1)
                if s.F:
                    for name, dst in (("qS", qT), ("kS", kT)):
                        read, w = filled(name)
                        dve.tensor_copy(dst[:, :, :].rearrange("p a b -> p (a b)"), w.bitcast(F16)).then_inc(read, 1)
                if s.B:
                    for n in range(2):
                        read, w = filled(f"kl{n}")
                        dve.tensor_copy(kf[:, 2 * n:2 * n + 2, S:2 * S], w.rearrange("p (a b) -> p a b", a=2))\
                           .then_inc(read, 1)
                    dve.drain().then_inc(heads_ready, 1)
                if s.B:
                    for n in range(2 * XH):
                        read, w = filled(f"mx{n}")
                        dve.tensor_reduce(out=mx[:, n % 2, n // 2:n // 2 + 1], in_=w, op=ALU.max, axis=AX).then_inc(read, 1)
                    dve.drain()
                    dve.tensor_scalar(negm[:, :, :], mx[:, :, :], -1.0, None, ALU.mult).then_inc(negm_ready, 1)
                if s.B:
                    read, w = filled("mT")
                    dve.tensor_copy(mT[0:XH, :], w[0:XH, :].bitcast(BF16)[:, 0:S]).then_inc(read, 1)
                if s.C:
                    for n in range(2):
                        read, w = filled(f"o2T{n}")
                        dve.tensor_copy(o2T[:, 2 * n:2 * n + 2, :].rearrange("p a b -> p (a b)"), w).then_inc(read, 1)
                def values_over_sums(g):
                    hs = slice(4 * g, 4 * g + 4)
                    dve.wait_ge(fold_done, s.a * 4 + g + 1)
                    dve.tensor_reduce(out=ncol[:, hs, :], in_=L[:, hs, :, P:P + P // 2], op=ALU.add, axis=AX)
                    dve.drain()
                    dve.reciprocal(rcol[:, hs, :], ncol[:, hs, :])
                    dve.drain()
                    for c in range(2):
                        dve.tensor_tensor(vp[:, hs, c, 0:DH],
                                          vall[:, bass.ds(2 * s.a + c, 1), 32 * g:32 * g + 32]
                                          .rearrange("p a (h d) -> p (a h) d", h=4),
                                          rcol[:, hs, c:c + 1].to_broadcast([P, 4, DH]), ALU.mult)
                    dve.tensor_copy(vp[:, hs, :, DH], rcol[:, hs, :]).then_inc(vp_ready, 1)

                if s.A:
                    values_over_sums(0)
                for g in range(4):
                    if s.A:
                        if g < 3:
                            values_over_sums(g + 1)
                        if s.t == 0 and g == 0:
                            dve.wait_ge(zeroed, 16 * 7)
                        dve.wait_ge(av_done, s.a * 4 + g + 1)
                        dve.tensor_copy(aoT[:, g, :], psAg[:, g % 2, :]).then_inc(ao_stored, 1)
                    if s.F:
                        wait(dve, av_done, s.f * 4 + g - 3)
                        for pair in range(2):
                            dve.wait_ge(cos_done, s.f * 8 + 2 * g + pair + 1)
                            dve.tensor_scalar(X[:, 4 * g + 2 * pair:4 * g + 2 * pair + 2, :, :].rearrange("p a b c -> p (a b c)"),
                                              psC[:, :, :].rearrange("p a b -> p (a b)"),
                                              float(np.float32(-1.0 + CLIP)), float(np.float32(1.0 - CLIP)),
                                              ALU.max, ALU.min).then_inc(clip_done, 1)
                    if s.C and g == 0:
                        read, w = filled("xo")
                        xo_t = xs[:, bass.ds(2 * s.c, 2), :]
                        dve.tensor_tensor(xo_t, xo_t, w[:, 0:S].rearrange("p (c d) -> p c d", c=2), ALU.add).then_inc(read, 1)
                        statistics(2, [flat(xs[:, bass.ds(2 * s.c + c, 1), :]) for c in range(2)], 1.0, LN_EPS, x2_var_ready)
                    if s.C and g == 1:
                        dve.wait_ge(x2_rs_ready, s.c + 1)
                        norm_pair(dve, lambda c: yn[:, c, :], lambda c: flat(xs[:, bass.ds(2 * s.c + c, 1), :]),
                                  lambda c: mv2[:, 2 + c, 0:1], lambda c: rs4[:, 2 + c:3 + c], yn_ready)
                        dve.drain()
                        dve.tensor_copy(y3[:, bass.ds(2 * s.c, 2), :], yn[:, :, :])
                        read, w = filled("yT")
                        dve.tensor_copy(yTs[:, :], w[:, 0:S])
                        dve.tensor_copy(yT[:, bass.ds(s.c * S, S)], w[:, 0:S]).then_inc(read, 1)
                        read, w = filled("logits")
                        dve.tensor_copy(lgs[:, bass.ds(2 * s.c, 2), :], w[:, 0:2 * NE].rearrange("p (c e) -> p c e", c=2))\
                           .then_inc(read, 1)
                    if s.B and g == 2:
                        norm_heads(0)
            each_step(dve, body)

            def bc8(ap):
                return ap.rearrange("p (t a) -> p t a", a=1).to_broadcast([P, NT, NE])

            sc, pm, ex, rank, slot, valid = (r16[:, n, :] for n in range(6))
            experts = cst_s[:, C_EXP:C_EXP + NE].rearrange("p (a e) -> p a e", a=1).to_broadcast([P, NT, NE])
            dve.drain()
            dve.tensor_reduce(out=sc, in_=lgs[:, :, :], op=ALU.max, axis=AX)
            dve.drain()
            dve.tensor_tensor(tmp8[:, :, :], lgs[:, :, :], bc8(sc), ALU.subtract).then_inc(lg_sub, 1)
            dve.wait_ge(lg_exp, 1)
            dve.tensor_reduce(out=sc, in_=probs[:, :, :], op=ALU.add, axis=AX)
            dve.drain()
            dve.reciprocal(sc, sc)
            dve.drain()
            dve.tensor_tensor(probs[:, :, :], probs[:, :, :], bc8(sc), ALU.mult)
            dve.drain()
            dve.tensor_reduce(out=pm, in_=probs[:, :, :], op=ALU.max, axis=AX)
            dve.drain()
            dve.wait_ge(diff_done, 4 * NB)
            dve.tensor_copy(pbc, pm.rearrange("p (t a) -> p t a", a=1).to_broadcast([P, NT, P])).then_inc(pbc_ready, 1)
            dve.tensor_tensor(tmp8[:, :, :], probs[:, :, :], bc8(pm), ALU.is_ge)
            dve.drain()
            dve.tensor_tensor(tmp8[:, :, :], tmp8[:, :, :], experts, ALU.mult)
            dve.drain()
            dve.tensor_reduce(out=ex, in_=tmp8[:, :, :], op=ALU.min, axis=AX)
            dve.drain()
            dve.tensor_tensor(hot[:, :, :], bc8(ex), experts, ALU.is_equal)
            dve.drain()
            dve.tensor_copy(hotb[:, :, :], hot[:, :, :])
            dve.wait_ge(prow_filled, 1)
            for n in range(4):
                dve.tensor_copy(prow[:, n * 512:(n + 1) * 512], ring[n])
            dve.drain().then_inc(prow_ready, 1)
            tri = cst_s[:, C_TRI:C_TRI + P]
            for j in range(NT):
                r = j % 4
                if j >= 4:
                    dve.wait_ge(g_used, j - 3)
                pj = r16[:, 1, j:j + 1]
                own = prow[:, j * P:(j + 1) * P]
                dve.scalar_tensor_tensor(eqd[:, j % 2, :], own, pj, tri, ALU.is_equal, ALU.mult)
                if j > 0:
                    dve.tensor_scalar(G[:, r, 0:j * P], prow[:, 0:j * P], pj, None, ALU.is_lt)
                if j < NT - 1:
                    dve.tensor_scalar(G[:, r, (j + 1) * P:NT * P], prow[:, (j + 1) * P:NT * P], pj, None, ALU.is_le)
                dve.drain()
                dve.scalar_tensor_tensor(G[:, r, j * P:(j + 1) * P], own, pj, eqd[:, j % 2, :], ALU.is_lt, ALU.add)\
                   .then_inc(g_ready, 1)
            dve.wait_ge(rank_done, 1)
            dve.tensor_tensor(tmp8[:, :, :], psR, hot[:, :, :], ALU.mult)
            dve.drain()
            dve.tensor_reduce(out=rank, in_=tmp8[:, :, :], op=ALU.add, axis=AX)
            dve.drain()
            dve.tensor_scalar(slot, ex, float(CAP), float((NE - 1) * CAP), ALU.mult, ALU.add)
            dve.tensor_scalar(valid, ex, float(-NE), None, ALU.is_gt)
            dve.drain()
            dve.tensor_tensor(slot, slot, rank, ALU.add)
            dve.scalar_tensor_tensor(valid, rank, float(CAP), valid, ALU.is_lt, ALU.mult)
            dve.drain()
            far = cst_s[:, C_FAR:C_FAR + NT]
            dve.tensor_tensor(slot, slot, far, ALU.subtract)
            dve.drain()
            dve.tensor_tensor(slot, slot, valid, ALU.mult)
            dve.drain()
            dve.tensor_tensor(slot, slot, far, ALU.add)
            dve.drain()
            dve.tensor_copy(dest[:, :], slot).then_inc(dest_ready, 1)

            def store_inputs(m):
                e = blocks[m][0]
                dve.wait_ge(xinT_filled, e)
                if e > 2:
                    dve.wait_ge(h_filled, FC * (m - 1))
                dve.tensor_copy(xinT[:, e % 2, :], psW[:, 0, 0:CAP]).then_inc(xinT_ready, 1)

            def store_outputs(m):
                e, blk = blocks[m]
                dve.wait_ge(y_filled, m + 1)
                if e == 0:
                    dve.tensor_copy(res[:, 4 * blk:4 * blk + 4, :],
                                    ybank[m % 2].rearrange("p (t d) -> p t d", t=4)).then_inc(y_stored, 1)
                else:
                    if e > 2:
                        dve.wait_ge(y_saved[e % 2], 32 * ((e - 1) // 2))
                    dve.tensor_copy(yo[:, e % 2, 0:2, :],
                                    ybank[m % 2][:, 0:2 * D].rearrange("p (c d) -> p c d", c=2))
                    dve.tensor_copy(yo[0:CAP - 2 * P, e % 2, 2, :], ybank[m % 2][0:CAP - 2 * P, 2 * D:3 * D])\
                       .then_inc(y_stored, 1)

            dve.wait_ge(exp_b_loaded, 32)
            for m in range(len(blocks)):
                if blocks[m][0] > 0:
                    store_inputs(m)
                store_hidden(dve, m, 1)
                if m > 0:
                    store_outputs(m - 1)
            store_outputs(len(blocks) - 1)

            for n in range(4):
                dve.wait_ge(gathered, 16 * NT) if n == 0 else None
                dve.tensor_tensor(xs[:, 4 * n:4 * n + 4, :], xs[:, 4 * n:4 * n + 4, :],
                                  res[:, 4 * n:4 * n + 4, :], ALU.add).then_inc(final_ready, 1)

        @block.tensor
        def _(pe):
            pe.wait_ge(attn_w_loaded, 80)
            pe.wait_ge(dve_consts, 2)

            def body(s):
                def fill(name):
                    bank, u, w = W(s, name)
                    wait(pe, work_read[bank], u)
                    return work_filled[bank], w

                def stored(name):
                    bank, u, _ = W(s, name)
                    pe.wait_ge(work_read[bank], u + 1)

                def turn(name, src, ready, value):
                    pe.wait_ge(ready, value)
                    full, w = fill(name)
                    for c in range(2):
                        mm = pe.transpose(w[:, c * P:(c + 1) * P], src[:, c, :], ident)
                    mm.then_inc(full, 1)

                def values(n, src):
                    if n == 0:
                        wait(pe, exps_done, s.b * XH)
                    else:
                        pe.wait_ge(v_stored, 2 * s.b + 1)
                    for c in range(2):
                        mm = pe.matmul(psS[:, 2 * c:2 * c + 2, :].rearrange("p a b -> p (a b)"),
                                       src[:, c * P:(c + 1) * P], wv_s[:, :], start=True, stop=True)
                    mm.then_inc(v_filled, 1)

                def rotary_keys(n):
                    full, w = fill(f"kx{n}")
                    if n == 0:
                        stored("ctxT")
                    pe.matmul(w[:, 0:S], wk_s[:, n * P:(n + 1) * P], cT[:, :], start=True, stop=True)
                    pe.matmul(w[:, S:2 * S], wks_s[:, n * P:(n + 1) * P], cT[:, :], start=True, stop=True)\
                      .then_inc(full, 1)

                def keys_or_queries(name, weights):
                    for n in range(2):
                        full, w = fill(f"{name}{n}")
                        for m in range(2):
                            c = 2 * n + m
                            mm = pe.matmul(w[:, m * S:(m + 1) * S], weights[:, c * P:(c + 1) * P], lT[:, :],
                                           start=True, stop=True)
                        mm.then_inc(full, 1)

                def scores(n, h):
                    wait(pe, exps_done, n * XH + h)
                    for c in range(KC):
                        dst = psS[:, c, :]
                        pe.matmul(dst, kf[:, h // 2, c * P:(c + 1) * P], qf[:, h, :], start=True, stop=False)
                        mm = pe.matmul(dst, sel_s[:, h * P:(h + 1) * P], mT[:, :], start=False, stop=True)
                    mm.then_inc(scores_done, 1)

                def weighted(n, h):
                    pe.wait_ge(exps_done, n * XH + h + 1)
                    wait(pe, oh_stored, n * XH + h)
                    for c in range(KC):
                        mm = pe.matmul(psPh[0:XD + 1, h % 2, :], V[:, c, h, :], E[:, h % 2, c, :],
                                       start=(c == 0), stop=(c == KC - 1))
                    mm.then_inc(pv_done, 1)

                def turn_heads(batch, n):
                    pe.wait_ge(oh_stored, batch * XH + 2 * n + 2)
                    full, w = fill(f"pT{n}")
                    for m in range(2):
                        for q in range(2):
                            at = (2 * m + q) * (XD + 1)
                            mm = pe.transpose(w[:, at:at + XD + 1], oh[:, (2 * n + m) % 4, q * P:(q + 1) * P],
                                              ident[0:XD + 1, 0:XD + 1])
                    mm.then_inc(full, 1)

                if s.F:
                    turn("xnT", xn, xn_ready, s.f + 1)
                if s.B:
                    turn("ctxT", cn, cn_ready, s.b + 1)
                if s.B:
                    pe.wait_ge(ao_stored, s.b * 4 + 4)
                    for q in range(2):
                        full, w = fill(f"ao{q}")
                        for g in range(4):
                            mm = pe.transpose(w[:, g * P:(g + 1) * P], aoT[:, g, q * P:(q + 1) * P], ident)
                        mm.then_inc(full, 1)
                if s.C:
                    scores(s.c, 5)
                    turn_heads(s.c, 1)
                    weighted(s.c, 4)
                if s.F:
                    for c in range(2):
                        full, w = fill(f"qkv{c}")
                        if c == 0:
                            stored("xnT")
                        pe.matmul(w[:, 0:3 * D], xnT[:, c * P:(c + 1) * P], wqkv_s[:, :], start=True, stop=True)\
                          .then_inc(full, 1)
                if s.B:
                    turn("oT", o, o_ready, s.b + 1)
                    full, w = fill("att")
                    stored("oT")
                    for c in range(2):
                        pe.matmul(w[:, c * D:(c + 1) * D], ones_row[:, :], bout_s[:, :], start=True, stop=False)
                        mm = pe.matmul(w[:, c * D:(c + 1) * D], oT[:, c * P:(c + 1) * P], wout_s[:, :], start=False, stop=True)
                    mm.then_inc(full, 1)
                if s.B:
                    rotary_keys(0)
                if s.C:
                    scores(s.c, 6)
                    weighted(s.c, 5)
                if s.B:
                    rotary_keys(1)
                if s.C:
                    turn_heads(s.c, 2)
                    scores(s.c, 7)
                    weighted(s.c, 6)
                if s.B:
                    rotary_keys(2)
                    rotary_keys(3)
                    turn("latT", ln, ln_ready, s.b + 1)
                if s.C:
                    weighted(s.c, 7)
                    turn_heads(s.c, 3)
                if s.B:
                    stored("latT")
                    keys_or_queries("q", wq_s)
                if s.F:
                    pe.wait_ge(stack_ready, s.f + 1)
                    for kind, name in enumerate(("qS", "kS")):
                        full, w = fill(name)
                        wv_ = w.bitcast(F16).rearrange("p (g c t) -> p g c t", g=4, c=2)
                        for g in range(4):
                            for c in range(2):
                                src = stack[:, kind, c * NH + 4 * g:c * NH + 4 * g + 4, :, :].rearrange("p h s d -> p (h s d)")
                                mm = pe.transpose(wv_[:, g, c, :], src, id16[:, :])
                        mm.then_inc(full, 1)
                if s.B:
                    keys_or_queries("kl", wk_s)
                    values(0, lT)
                if s.B:
                    pe.wait_ge(heads_ready, s.b + 1)
                    for n in range(2 * XH):
                        h, c = n // 2, n % 2
                        full, w = fill(f"mx{n}")
                        pe.matmul(w, qb[:, h, 2 * c * P + 1:2 * (c + 1) * P:2], kb[:, h // 2, 1:4 * S:2],
                                  start=True, stop=True).then_inc(full, 1)
                        if n == 5:
                            values(1, cT)
                if s.B:
                    pe.wait_ge(negm_ready, s.b + 1)
                    full, w = fill("mT")
                    for c in range(2):
                        mm = pe.transpose(w[0:XH, :].bitcast(BF16)[:, c * P:(c + 1) * P], negm[:, c, :], idb[:, :])
                    mm.then_inc(full, 1)
                    stored("mT")
                    pe.wait_ge(v_stored, 2 * s.b + 2)
                    scores(s.b, 0)
                if s.C:
                    for n in range(2):
                        full, w = fill(f"o2T{n}")
                        for m in range(2):
                            for q in range(2):
                                c = 2 * n + m
                                mm = pe.transpose(w[:, m * S + q * P:m * S + (q + 1) * P], o2[:, q, c * P:(c + 1) * P], ident)
                        mm.then_inc(full, 1)
                def attention(g):
                    pe.wait_ge(vp_ready, s.a * 4 + g + 1)
                    wait(pe, ao_stored, s.a * 4 + g)
                    for c in range(2):
                        for j in range(4):
                            h = 4 * g + j
                            mm = pe.matmul(psAg[32 * j:32 * j + DH + 2, g % 2, :], vp[:, h, c, :], X[:, h, c, :],
                                           start=(c == 0), stop=(c == 1), tile_position=(0, 32 * j))
                    mm.then_inc(av_done, 1)

                def cosines(g, pair):
                    if g == 0 and pair == 0:
                        stored("kS")
                    wait(pe, clip_done, s.f * 8 + 2 * g + pair)
                    for c in range(2):
                        for m in range(2):
                            j = 2 * pair + m
                            rows = slice(32 * j, 32 * j + 32)
                            mm = pe.matmul(psC[:, m, c * S:(c + 1) * S], kT[rows, g, c * P:(c + 1) * P], qT[rows, g, :],
                                           start=True, stop=True)
                    mm.then_inc(cos_done, 1)

                for g in range(4):
                    if s.A:
                        attention(g)
                    if s.F:
                        cosines(g, 0)
                    if s.B:
                        scores(s.b, g + 1)
                    if s.C and g == 0:
                        full, w = fill("xo")
                        stored("o2T1")
                        for q in range(2):
                            for c in range(4):
                                mm = pe.matmul(w[:, q * D:(q + 1) * D], o2T[:, c, q * P:(q + 1) * P], wo_s[:, c, :],
                                               start=(c == 0), stop=(c == 3))
                        mm.then_inc(full, 1)
                    if s.F:
                        cosines(g, 1)
                    if s.B:
                        weighted(s.b, g)
                    if s.C and g == 1:
                        turn("yT", yn, yn_ready, s.c + 1)
                        full, w = fill("logits")
                        stored("yT")
                        for c in range(2):
                            mm = pe.matmul(w[:, c * NE:(c + 1) * NE], yTs[:, c * P:(c + 1) * P], wr_s[:, :],
                                           start=True, stop=True)
                        mm.then_inc(full, 1)
                    if s.B and g == 2:
                        turn_heads(s.b, 0)
            each_step(pe, body)

            pe.wait_ge(pbc_ready, 1)
            for t in range(NT):
                mm = pe.transpose(ring[t // 4][:, (t % 4) * P:(t % 4 + 1) * P], pbc[:, t, :], ident)
            mm.then_inc(prow_filled, 1)
            pe.wait_ge(exp_w_loaded, 32)
            pe.wait_ge(exp_b_loaded, 32)
            pe.wait_ge(prow_ready, 1)

            count = [0, 0]

            def hidden(e, src, width):
                for c in range(FC):
                    n = count[0]
                    if n >= 4:
                        m = n - 4
                        pe.wait_ge(h_even if m % 2 == 0 else h_odd, m // 2 + 1)
                    pe.matmul(ring[n % 4][:, 0:width], w1_s[:, e, c * P:(c + 1) * P], src, start=True, stop=True)\
                      .then_inc(h_filled, 1)
                    count[0] += 1

            def outputs(e, tiles):
                m = count[1]
                pe.wait_ge(h_even, 2 * (m + 1))
                pe.wait_ge(h_odd, 2 * (m + 1))
                if m >= 2:
                    pe.wait_ge(y_stored, m - 1)
                at = 0
                for t, rows in enumerate(tiles):
                    dst = ybank[m % 2][0:rows, t * D:(t + 1) * D]
                    pe.matmul(dst, ones_row[:, 0:rows], b2_s[:, e * D:(e + 1) * D], start=True, stop=False)
                    for c in range(FC):
                        mm = pe.matmul(dst, hT[m % 2][:, c, at:at + rows], w2_s[:, e, c, :], start=False, stop=(c == FC - 1))
                    at += rows
                mm.then_inc(y_filled, 1)
                count[1] += 1

            pe.matmul(psR.rearrange("p t e -> p (t e)"), zb[:, :], zb[:, :], start=True, stop=False, skip_group_check=True)
            for j in range(NT):
                pe.wait_ge(g_ready, j + 1)
                for t in range(NT):
                    mm = pe.matmul(psR[:, t, :], G[:, j % 4, t * P:(t + 1) * P], hotb[:, j, :], start=False,
                                   stop=(j == NT - 1), skip_group_check=True)
                mm.then_inc(g_used, 1)
            pe.drain().then_inc(rank_done, 1)

            def inputs(m):
                e = blocks[m][0]
                pe.wait_ge(xin_loaded[(e - 1) % 4], 32 * ((e + 3) // 4))
                if e > 1:
                    pe.wait_ge(xinT_ready, e - 1)
                at = 0
                for c, rows in enumerate((P, P, CAP - 2 * P)):
                    mm = pe.transpose(psW[:, 0, at:at + rows], xin[0:rows, (e - 1) % 4, c, :], ident[0:rows, 0:rows])
                    at += rows
                mm.then_inc(xinT_filled, 1)
                pe.wait_ge(xinT_ready, e)

            def hidden(m):
                e, blk = blocks[m]
                src = yT[:, blk * FF:(blk + 1) * FF] if e == 0 else xinT[:, e % 2, :]
                for c in range(FC):
                    if m > 0:
                        pe.wait_ge(h_odd if c % 2 else h_even, 2 * (m - 1) + c // 2 + 1)
                    pe.matmul(ring[c][:, 0:FF if e == 0 else CAP], w1_s[:, e, c * P:(c + 1) * P], src,
                              start=True, stop=True).then_inc(h_filled, 1)

            def outputs(m):
                e, blk = blocks[m]
                pe.wait_ge(h_even, 2 * (m + 1))
                pe.wait_ge(h_odd, 2 * (m + 1))
                if m >= 2:
                    pe.wait_ge(y_stored, m - 1)
                at = 0
                for t, rows in enumerate((P, P, P, P) if e == 0 else (P, P, CAP - 2 * P)):
                    dst = ybank[m % 2][0:rows, t * D:(t + 1) * D]
                    pe.matmul(dst, ones_row[:, 0:rows], b2_s[:, e * D:(e + 1) * D], start=True, stop=False)
                    for c in range(FC):
                        mm = pe.matmul(dst, hT[m % 2][:, c, at:at + rows], w2_s[:, e, c, :], start=False, stop=(c == FC - 1))
                    at += rows
                mm.then_inc(y_filled, 1)

            for m in range(len(blocks)):
                if blocks[m][0] > 0:
                    inputs(m)
                hidden(m)
                if m > 0:
                    outputs(m - 1)
            outputs(len(blocks) - 1)

    return nc


def kernel(x, ctx_1024, L0_attn_w_qkv, L0_attn_b_qkv, L0_attn_w_out, L0_attn_b_out, L0_xattn_gamma_x,
           L0_xattn_beta_x, L0_xattn_gamma_l, L0_xattn_beta_l, L0_xattn_Wq, L0_xattn_Wkv, L0_xattn_Wo,
           L0_ffn_router_w, L0_ffn_W1, L0_ffn_b1, L0_ffn_W2, L0_ffn_b2):
    import concourse.bacc as bacc
    from concourse.bass_utils import run_bass_kernel_spmd

    cst, sel = shape_constants()
    wkv = np.asarray(L0_xattn_Wkv)
    wk = wkv[:, 0:INNER]
    arrays = {
        "x": np.asarray(x).reshape(NB * S, D),
        "ctx_in": np.asarray(ctx_1024).reshape(NB * S, D),
        "wqkv": np.asarray(L0_attn_w_qkv).T,
        "bqkv": np.broadcast_to(np.asarray(L0_attn_b_qkv), (P, 3 * D)),
        "wout": np.asarray(L0_attn_w_out).T,
        "bout": np.asarray(L0_attn_b_out).reshape(1, D),
        "gam": np.stack([np.asarray(a) for a in (L0_xattn_gamma_x, L0_xattn_beta_x, L0_xattn_gamma_l,
                                                 L0_xattn_beta_l)], axis=1),
        "wq": np.asarray(L0_xattn_Wq),
        "wk": wk,
        "wks": wk.reshape(D, XH, 2, XD // 2)[:, :, ::-1, :].reshape(D, INNER),
        "wv": wkv[:, INNER:],
        "wo": np.asarray(L0_xattn_Wo),
        "wr": np.asarray(L0_ffn_router_w).T,
        "w1": np.asarray(L0_ffn_W1),
        "b1": np.asarray(L0_ffn_b1).reshape(NE, FC, P).transpose(2, 0, 1).reshape(P, NE * FC),
        "w2": np.asarray(L0_ffn_W2),
        "b2": np.asarray(L0_ffn_b2).reshape(1, NE * D),
        "cst": cst,
        "sel": sel,
    }
    arrays = {f"in_{name}": np.ascontiguousarray(a) for name, a in arrays.items()}
    nc = bacc.Bacc("TRN2", target_bir_lowering=False, num_devices=1)
    args = [nc.dram_tensor(n, a.shape, mybir.dt.from_np(a.dtype), kind="ExternalInput").ap() for n, a in arrays.items()]
    out = nc.dram_tensor("out_x", (NB * S, D), F32, kind="ExternalOutput").ap()
    build(nc, *args, out)
    r = run_bass_kernel_spmd(nc, [arrays], core_ids=[0])
    return r.results[0]["out_x"].reshape(NB, S, D)
```

```python
import math
from contextlib import ExitStack

import numpy as np

import concourse.bass as bass
from concourse import mybir

ALU = mybir.AluOpType
ACT = mybir.ActivationFunctionType
AX = mybir.AxisListType.X
F32 = mybir.dt.float32
F16 = mybir.dt.float16
BF16 = mybir.dt.bfloat16
I32 = mybir.dt.int32

P = 128
NB, S, D = 8, 256, 128
NT = NB * S // P
NH, DH = 16, 8
XH, XD = 8, 64
INNER = XH * XD
KC = 2 * S // P
NE, FF = 8, 512
FC = FF // P
CAP = math.ceil(NB * S / NE * 1.25)
SLOTS = (NE - 1) * CAP
FILL = max(p for p in range(1, P + 1) if SLOTS % p == 0)
ROW = D + 1
LN_EPS = 1e-5
CLIP = 1e-7
DECAY = -3.2
FAR = 100000
LE_TABLE, TA_TABLE = "natural_log_exp_and_others", "sigmoid_and_others"

C_ID, C_ROPE, C_TRI, C_EXP, C_FAR, C_END = 0, 128, 128 + 512, 768, 776, 792


def shape_constants():
    c = np.zeros((P, C_END), np.float32)
    c[:, C_ID:C_ID + P] = np.eye(P)
    half = XD // 2
    inv = (1.0 / 10000.0 ** (np.arange(0, XD, 2, dtype=np.float32) / XD)).astype(np.float32)
    theta = np.arange(S, dtype=np.float32)[None, :] * inv[:, None]
    row = np.arange(P) % XD
    ang = theta[row % half]
    c[:, C_ROPE:C_ROPE + S] = np.cos(ang)
    c[:, C_ROPE + S:C_ROPE + 2 * S] = np.sin(ang) * np.where(row < half, -1.0, 1.0)[:, None]
    c[:, C_TRI:C_TRI + P] = np.arange(P)[:, None] < np.arange(P)[None, :]
    c[:, C_EXP:C_EXP + NE] = np.arange(NE) - NE
    c[:, C_FAR:C_FAR + NT] = FAR + np.arange(P)[:, None] + P * np.arange(NT)[None, :]
    sel = np.zeros((XH, XH, P), np.float32)
    sel[np.arange(XH), np.arange(XH), :] = 1.0
    return c, sel.reshape(XH, XH * P)


class Step:

    def __init__(self, t=None, r=None):
        self.t = t
        if r is None:
            self.f, self.a, self.b, self.c = t + 1, t, t - 1, t - 2
            self.F, self.A, self.B, self.C = (0 <= n < NB for n in (t + 1, t, t - 1, t - 2))
        else:
            self.f, self.a, self.b, self.c = r + 3, r + 2, r + 1, r
            self.F = self.A = self.B = self.C = True
            self.t = None
            self.r = r

    def uses(self):
        u = []
        u += ["xnT"] * self.F + ["ctxT", "ao0", "ao1"] * self.B + ["pT1"] * self.C + ["qkv0", "qkv1"] * self.F
        u += ["oT", "att", "kx0", "kx1"] * self.B + ["pT2"] * self.C + ["kx2", "kx3", "latT"] * self.B
        u += ["pT3"] * self.C + ["q0", "q1"] * self.B + ["qS", "kS"] * self.F + ["kl0", "kl1"] * self.B
        u += ["o2T0", "o2T1"] * self.C + [f"mx{n}" for n in range(2 * XH)] * self.B + ["mT"] * self.B
        u += ["xo", "yT", "logits"] * self.C + ["pT0"] * self.B
        return u

    def use(self, name):
        here = self.uses()
        at = here.index(name)
        bank = at % 2
        local = at // 2
        def rises(t):
            n = len(Step(t).uses())
            return (n + 1 - bank) // 2
        if self.t is not None:
            return bank, sum(rises(t) for t in range(-1, self.t)) + local
        before = sum(rises(t) for t in range(-1, 2))
        return bank, self.r * rises(2) + (before + local)


def each_step(engine, body):
    for t in (-1, 0, 1):
        body(Step(t))
    with engine.Fori(0, 5) as r:
        body(Step(r=r))
    for t in (7, 8, 9):
        body(Step(t))


def wait(engine, sem, value):
    if not isinstance(value, int) or value > 0:
        engine.wait_ge(sem, value)


def build(nc, x, ctx_in, wqkv, bqkv, wout, bout, gam, wq, wk, wks, wv, wo, wr, w1, b1, w2, b2, cst, sel, out):
    ctx = ExitStack()
    with ctx:
        def sb(name, shape, dt=F32):
            return ctx.enter_context(nc.sbuf_tensor(name, shape, dt))

        def pb(name, shape, dt=F32):
            return ctx.enter_context(nc.psum_tensor(name, shape, dt))

        def sem(name):
            return ctx.enter_context(nc.semaphore(name))

        xs = sb("xs", [P, NT, D])
        cx = sb("cx", [P, NT, D])
        vall = sb("vall", [P, NT, ROW])
        y3 = vall
        yT = cx[:, :, :].rearrange("p t d -> p (t d)")
        lgs = sb("lgs", [P, NT, NE])
        wqkv_s = sb("wqkv_s", [P, 3 * D])
        bqkv_s = sb("bqkv_s", [P, 3 * D])
        wout_s = sb("wout_s", [P, D])
        bout_s = sb("bout_s", [1, D])
        gam_s = sb("gam_s", [P, 4])
        wq_s = sb("wq_s", [P, INNER])
        wk_s = sb("wk_s", [P, INNER])
        wks_s = sb("wks_s", [P, INNER])
        wv_s = sb("wv_s", [P, INNER])
        wo_s = sb("wo_s", [P, 4, D])
        wr_s = sb("wr_s", [P, NE])
        b1_s = sb("b1_s", [P, NE, FC])
        cst_s = sb("cst_s", [P, C_END])
        sel_s = sb("sel_s", [P, XH * P], BF16)
        id16 = sb("id16", [P, P], F16)
        idb = sb("idb", [P, P], BF16)
        ones_row = sb("ones_row", [1, P])
        cols = sb("cols", [P, 2])
        ident = cst_s[:, C_ID:C_ID + P]
        rope = cst_s[:, C_ROPE:C_ROPE + 2 * S]

        st = sb("st", [P, 2 * NT, 6])
        mv = sb("mv", [P, 2 * NT, 2])
        lnrs = sb("lnrs", [P, 2 * NT])
        lnvar = sb("lnvar", [P, 2 * NT])
        st2 = sb("st2", [P, 4, 6])
        mv2 = sb("mv2", [P, 4, 2])
        var4 = sb("var4", [P, 4])
        lv4 = sb("lv4", [P, 4])
        rs4 = sb("rs4", [P, 4])

        xn = sb("xn", [P, 2, D])
        xnT = sb("xnT", [P, S])
        qk = sb("qk", [P, 2, 2 * D])
        ss = sb("ss", [P, 2, 2, NH])
        l2 = sb("l2", [P, 2, 2, NH])
        qn = sb("qn", [P, 2, 2, D])
        sq = qn[:, :, :, :].rearrange("p k c d -> p k (c d)")
        stack = sb("stack", [P, 2, 2 * NH, 4, DH], F16)
        qT = sb("qT", [P, 4, S], F16)
        kT = sb("kT", [P, 4, S], F16)
        X = sb("X", [P, NH, 2, S])
        L = sb("L", [P, NH, 2, S])
        ncol = sb("ncol", [P, NH, 2])
        rcol = sb("rcol", [P, NH, 2])
        vp = sb("vp", [P, NH, 2, DH + 2])
        aoT = sb("aoT", [P, 4, S])
        den = sb("den", [P, 2, NH])
        rden = sb("rden", [P, 2, NH])
        o = sb("o", [P, 2, D])
        oT = sb("oT", [P, S])

        cn = sb("cn", [P, 2, D])
        cT = sb("cT", [P, S])
        ln = sb("ln", [P, 2, D])
        lT = sb("lT", [P, S])
        kcs = sb("kcs", [P, 4, 2, S])
        kf = sb("kf", [P, 4, 2 * S])
        qf = sb("qf", [P, XH, S])
        kb = kf[:, :, :].bitcast(BF16)
        qb = qf[:, :, :].bitcast(BF16)
        V = sb("V", [P, KC, XH, XD + 1])
        mx = sb("mx", [P, 2, XH])
        negm = sb("negm", [P, 2, XH], BF16)
        mT = sb("mT", [P, S], BF16)
        E = sb("E", [P, 2, KC, S])
        sel_f = E[:, :, :, :].rearrange("p a b c -> p (a b c)")[0:XH, 0:XH * P]
        rpv = sb("rpv", [P, 2, 4])
        oh = sb("oh", [XD + 1, 4, S])
        o2 = sb("o2", [P, 2, INNER])
        o2T = sb("o2T", [P, 4, S])
        yn = sb("yn", [P, 2, D])
        yTs = sb("yTs", [P, S])

        Xf = X[:, :, :, :].rearrange("p a b c -> p (a b c)")
        w1_s = Xf[:, 0:NE * FF].rearrange("p (e f) -> p e f", e=NE)
        w2_s = Xf[:, NE * FF:2 * NE * FF].rearrange("p (e c d) -> p e c d", e=NE, c=FC)
        Lf = L[:, :, :, :].rearrange("p a b c -> p (a b c)")
        res = Lf[:, 0:NT * D].rearrange("p (t d) -> p t d", t=NT)
        pbc = Lf[:, 0:NT * P].rearrange("p (t q) -> p t q", t=NT)
        prow = Lf[:, NT * P:2 * NT * P]
        G = Lf[:, 2 * NT * P:4 * NT * P].bitcast(BF16).rearrange("p (r q) -> p r q", r=4)
        o2f = o2[:, :, :].rearrange("p a b -> p (a b)")
        probs, tmp8, hot = (o2f[:, n * NT * NE:(n + 1) * NT * NE].rearrange("p (t e) -> p t e", t=NT) for n in range(3))
        hotb = o2f[:, 768:768 + NT * NE // 2].bitcast(BF16).rearrange("p (t e) -> p t e", t=NT)
        dest = o2f[:, 832:832 + NT].bitcast(I32)
        r16 = o2f[:, 848:848 + 6 * NT].rearrange("p (n t) -> p n t", n=6)
        eqd = o2f[:, 512:512 + 2 * P].rearrange("p (r q) -> p r q", r=2)
        empty = aoT[:, :, :].rearrange("p g q -> p (g q)")[0:FILL, 0:ROW]
        zb = sb("zb", [P, P], BF16)
        ids = sb("ids", [P, NE - 1, 3], I32)
        xin = E[:, :, :, :].rearrange("p a b c -> p (a b c)")[:, 0:4 * 3 * ROW].rearrange("p (r c d) -> p r c d", r=4, c=3)
        xinT = kcs[:, :, :, :].rearrange("p a b c -> p (a b c)")[:, 0:2 * CAP].rearrange("p (r s) -> p r s", r=2)
        b2_s = kcs[:, :, :, :].rearrange("p a b c -> p (a b c)")[:, 2 * CAP:2 * CAP + NE * D]
        hT = [kf, sb("hT1", [P, FC, 2 * S])]
        yo = o2T[:, :, :].rearrange("p a b -> p (a b)")[:, 0:2 * 3 * D].rearrange("p (r c d) -> p r c d", r=2, c=3)

        x_slots = nc.dram_tensor("x_slots", (SLOTS, ROW), F32, kind="Internal").ap()

        psW = pb("psW", [P, 2, 512])
        psC = pb("psC", [P, 2, 512])
        psS = pb("psS", [P, KC, S])
        psA = pb("psA", [P, 512])
        psP = pb("psP", [P, 512])
        psAg = psA[:, :].rearrange("p (g q) -> p g q", g=2)
        psPh = psP[:, :].rearrange("p (h q) -> p h q", h=2)
        ring = [psC[:, 0, :], psC[:, 1, :], psS[:, 0:2, :].rearrange("p a b -> p (a b)"),
                psS[:, 2:4, :].rearrange("p a b -> p (a b)")]
        psR = psA[:, 0:NT * NE].rearrange("p (t e) -> p t e", t=NT)

        x0_loaded = sem("x0_loaded")
        x_loaded, ctx_loaded, attn_w_loaded = sem("x_loaded"), sem("ctx_loaded"), sem("attn_w_loaded")
        xattn_w_loaded, exp_b_loaded, exp_w_loaded = sem("xattn_w_loaded"), sem("exp_b_loaded"), sem("exp_w_loaded")
        dve_consts = sem("dve_consts")
        x_var_ready, x_rs_ready = sem("x_var_ready"), sem("x_rs_ready")
        work_filled = [sem(f"work_filled{n}") for n in range(2)]
        work_read = [sem(f"work_read{n}") for n in range(2)]
        xn_ready, ss_ready, l2_ready, stack_ready = sem("xn_ready"), sem("ss_ready"), sem("l2_ready"), sem("stack_ready")
        cos_done, clip_done, ln_done, diff_done = sem("cos_done"), sem("clip_done"), sem("ln_done"), sem("diff_done")
        act_chain, kern_done, vp_ready, av_done = sem("act_chain"), sem("kern_done"), sem("vp_ready"), sem("av_done")
        ao_stored, o_ready, oh_stored = sem("ao_stored"), sem("o_ready"), sem("oh_stored")
        x1_var_ready, x1_rs_ready = sem("x1_var_ready"), sem("x1_rs_ready")
        x2_var_ready, x2_rs_ready = sem("x2_var_ready"), sem("x2_rs_ready")
        cn_ready, ln_ready, yn_ready = sem("cn_ready"), sem("ln_ready"), sem("yn_ready")
        heads_ready = sem("heads_ready")
        fold_done = sem("fold_done")
        v_filled, v_stored = sem("v_filled"), sem("v_stored")
        negm_ready, scores_done, exps_done, pv_done = sem("negm_ready"), sem("scores_done"), sem("exps_done"), sem("pv_done")
        lg_sub, lg_exp, pbc_ready, prow_filled, prow_ready = sem("lg_sub"), sem("lg_exp"), sem("pbc_ready"), sem("prow_filled"), sem("prow_ready")
        g_ready, g_used, rank_done, dest_ready = sem("g_ready"), sem("g_used"), sem("rank_done"), sem("dest_ready")
        zeroed, scattered = sem("zeroed"), sem("scattered")
        xin_loaded = [sem(f"xin_loaded{n}") for n in range(4)]
        xinT_filled, xinT_ready = sem("xinT_filled"), sem("xinT_ready")
        h_filled, y_filled, y_stored = sem("h_filled"), sem("y_filled"), sem("y_stored")
        final_ready, out_done = sem("final_ready"), sem("out_done")
        y_saved = [sem(f"y_saved{n}") for n in range(2)]

        block = ctx.enter_context(nc.Block())

        def W(s, name):
            bank, n = s.use(name)
            return bank, n, psW[:, bank, :]

        blocks = [(0, blk) for blk in range(4)] + [(e, 0) for e in range(1, NE)]

        def store_hidden(eng, m, first, done):
            e, _ = blocks[m]
            eng.wait_ge(y_filled, m - 1)
            for c in range(first, FC, 2):
                eng.wait_ge(h_filled, FC * m + c + 1)
                dst, src, bias = hT[m % 2][:, c, 0:CAP], ring[c][:, 0:CAP], b1_s[:, e, c:c + 1]
                if first == 0:
                    eng.activation(dst, src, ACT.Relu, bias=bias).then_inc(done, 1)
                else:
                    eng.tensor_scalar(dst, src, bias, 0.0, ALU.add, ALU.max).then_inc(done, 1)

        h_even, h_odd = sem("h_even"), sem("h_odd")
        h0_stored, y0_stored = sem("h0_stored"), sem("y0_stored")
        ybank = [psP[:, :], psW[:, 1, :]]

        @block.sync
        def _(sp):
            x_v = x.rearrange("(t p) d -> p t d", p=P)
            sp.dma_start(xs[:, 0:2, :], x_v[:, 0:2, :]).then_inc(x0_loaded, 16)
            for dst, src in ((cst_s, cst), (wqkv_s, wqkv), (bqkv_s, bqkv), (wout_s, wout), (bout_s, bout)):
                sp.dma_start(dst[:, :], src).then_inc(attn_w_loaded, 16)
            sp.dma_start(xs[:, 2:NT, :], x_v[:, 2:NT, :]).then_inc(x_loaded, 16)
            sp.dma_start(cx[:, :, :], ctx_in.rearrange("(t p) d -> p t d", p=P)).then_inc(ctx_loaded, 16)
            for dst, src in ((gam_s, gam), (wk_s, wk), (wks_s, wks), (wv_s, wv), (wq_s, wq), (sel_f, sel), (wr_s, wr)):
                sp.dma_start(dst if dst is sel_f else dst[:, :], src).then_inc(xattn_w_loaded, 16)
            sp.dma_start(wo_s[:, :, :], wo.rearrange("(c p) d -> p c d", p=P)).then_inc(xattn_w_loaded, 16)
            sp.dma_start(b1_s[:, :, :], b1.rearrange("p (e c) -> p e c", e=NE)).then_inc(exp_b_loaded, 16)
            sp.wait_ge(dve_consts, 1)
            sp.dma_start(x_slots.rearrange("(p r) w -> p r w", p=FILL),
                         empty.rearrange("p (r w) -> p r w", r=1).to_broadcast([FILL, SLOTS // FILL, ROW])).then_inc(zeroed, 16)

            sp.wait_ge(heads_ready, NB)
            sp.dma_start(b2_s, b2).then_inc(exp_b_loaded, 16)
            sp.wait_ge(av_done, 4 * NB)
            sp.dma_start(w1_s, w1.rearrange("e p f -> p e f")).then_inc(exp_w_loaded, 16)
            sp.dma_start(w2_s, w2.rearrange("e (c p) d -> p e c d", p=P)).then_inc(exp_w_loaded, 16)

            out_v = out.rearrange("(t p) d -> p t d", p=P)
            for n in range(4):
                sp.wait_ge(final_ready, n + 1)
                sp.dma_start(out_v[:, 4 * n:4 * n + 4, :], xs[:, 4 * n:4 * n + 4, :]).then_inc(out_done, 16)
            sp.wait_ge(scattered, 16 * NT)
            for e in range(1, NE):
                r = (e - 1) % 4
                if e > 4:
                    sp.wait_ge(xinT_ready, e - 4)
                row = (e - 1) * CAP
                sp.dma_start(xin[:, r, 0:2, :], x_slots[row:row + 2 * P, :].rearrange("(c p) d -> p c d", p=P))\
                  .then_inc(xin_loaded[r], 16)
                sp.dma_start(xin[0:CAP - 2 * P, r, 2, :], x_slots[row + 2 * P:row + CAP, :]).then_inc(xin_loaded[r], 16)
            sp.wait_ge(out_done, 64)
            for r in range(2):
                sp.wait_ge(y_saved[r], 48 * len(range(r or 2, NE, 2)))
            sp.wait_ge(zeroed, 16)

        @block.gpsimd
        def _(pool):
            def body(s):
                if not s.A:
                    return
                for g in range(4):
                    pool.wait_ge(ln_done, s.a * 4 + g + 1)
                    pool.tensor_tensor(X[:, 4 * g:4 * g + 4, :, :], X[:, 4 * g:4 * g + 4, :, :],
                                       L[:, 4 * g:4 * g + 4, :, :], ALU.subtract).then_inc(diff_done, 1)

                for g in range(1, 4):
                    hs = slice(4 * g, 4 * g + 4)
                    pool.wait_ge(kern_done, s.a * 4 + g + 1)
                    pool.tensor_tensor(L[:, hs, :, 0:P], X[:, hs, :, 0:P], X[:, hs, :, P:S], ALU.add)
                    pool.drain()
                    pool.tensor_tensor(L[:, hs, :, P:P + P // 2], L[:, hs, :, 0:P // 2], L[:, hs, :, P // 2:P], ALU.add)\
                        .then_inc(fold_done, 1)

            each_step(pool, body)

            pool.wait_ge(dest_ready, 1)
            pool.wait_ge(zeroed, 16)
            for t in range(NT):
                pool.indirect_dma_start(x_slots, bass.IndirectOffsetOnAxis(ap=dest[:, t:t + 1], axis=0),
                                        y3[:, t, :], None, bounds_check=SLOTS - 1, oob_is_err=False)\
                    .then_inc(scattered, 16)
            pool.wait_ge(out_done, 64)
            for e in range(1, NE):
                pool.wait_ge(y_stored, e)
                for c, rows in enumerate((P, P, CAP - 2 * P)):
                    pool.indirect_dma_start(out, bass.IndirectOffsetOnAxis(ap=ids[0:rows, e - 1, c:c + 1], axis=0),
                                            yo[0:rows, e % 2, c, :], None, bounds_check=NB * S - 1, oob_is_err=False,
                                            compute_op=ALU.add).then_inc(y_saved[e % 2], 16)

        @block.scalar
        def _(act):
            act.preload_act_table_set(LE_TABLE)

            def load_inv_std(tiles, n):
                act.wait_ge(x_var_ready, n)
                act.activation(lnrs[:, tiles], lnvar[:, tiles], ACT.Ln)
                act.drain()
                act.activation(lnrs[:, tiles], lnrs[:, tiles], ACT.Exp, scale=-0.5).then_inc(x_rs_ready, 1)

            load_inv_std(slice(0, 2), 1)

            def head(n, h):
                act.wait_ge(scores_done, n * XH + h + 1)
                wait(act, pv_done, n * XH + h - 1)
                act.activation(E[:, h % 2, :, :], psS[:, :, :], ACT.Exp).then_inc(exps_done, 1)

            def store_head(n, h):
                act.wait_ge(pv_done, n * XH + h + 1)
                act.activation(oh[:, h % 4, :], psPh[0:XD + 1, h % 2, :], ACT.Copy).then_inc(oh_stored, 1)

            def inv_std(c, var, rs, value):
                act.wait_ge(var, value)
                act.activation(lv4[:, c:c + 2], var4[:, c:c + 2], ACT.Ln)
                act.drain()
                act.activation(rs4[:, c:c + 2], lv4[:, c:c + 2], ACT.Exp, scale=-0.5).then_inc(rs, 1)

            def body(s):
                def value_tiles(n):
                    if n == 0:
                        wait(act, pv_done, s.b * XH)
                    act.wait_ge(v_filled, 2 * s.b + n + 1)
                    act.activation(V[:, 2 - 2 * n:4 - 2 * n, :, 0:XD],
                                   psS[:, :, :].rearrange("p (t c) (h d) -> p t (c h) d", t=2, d=XD), ACT.Copy)\
                       .then_inc(v_stored, 1)

                def head_lengths():
                    act.wait_ge(ss_ready, s.f + 1)
                    act.activation(l2[:, :, :, :], ss[:, :, :, :], ACT.Ln)
                    act.drain()
                    act.activation(l2[:, :, :, :], l2[:, :, :, :], ACT.Exp, scale=-0.5).then_inc(l2_ready, 1)

                for g in range(4):
                    if s.C:
                        head(s.c, 4 + g)
                        store_head(s.c, 3 + g)
                    if s.A:
                        hs = slice(4 * g, 4 * g + 4)
                        act.wait_ge(clip_done, s.a * 8 + 2 * g + 2)
                        act.activation(L[:, hs, :, :], X[:, hs, :, :], ACT.Ln, bias=1.0)
                        act.activation(X[:, hs, :, :], X[:, hs, :, :], ACT.Ln, bias=1.0, scale=-1.0)\
                           .then_inc(ln_done, 1)
                    if g == 2 and s.B:
                        inv_std(0, x1_var_ready, x1_rs_ready, s.b + 1)
                    if g == 2 and s.F and s.t != 0:
                        head_lengths()
                if s.C:
                    store_head(s.c, XH - 1)
                if s.t == 0:
                    load_inv_std(slice(2, 2 * NT), 2)
                if s.A:
                    act.preload_act_table_set(TA_TABLE)
                    for g in range(4):
                        act.wait_ge(diff_done, s.a * 4 + g + 1)
                        xg = X[:, 4 * g:4 * g + 4, :, :]
                        act.activation(xg, xg, ACT.Tanh, scale=0.25).then_inc(act_chain, 1)
                if s.B:
                    value_tiles(0)
                if s.A:
                    for g in range(4):
                        act.wait_ge(act_chain, s.a * 12 + g + 1)
                        xg = X[:, 4 * g:4 * g + 4, :, :]
                        act.activation(xg, xg, ACT.Arctan).then_inc(act_chain, 1)
                        if g == 2 and s.B:
                            value_tiles(1)
                    act.preload_act_table_set(LE_TABLE)
                elif s.B:
                    value_tiles(1)

                def log_angle(g):
                    act.wait_ge(act_chain, s.a * 12 + 4 + g + 1)
                    xg = X[:, 4 * g:4 * g + 4, :, :]
                    act.activation(xg, xg, ACT.Ln, bias=cols[:, 0:1], scale=2.0).then_inc(act_chain, 1)

                def kernel_value(g):
                    act.wait_ge(act_chain, s.a * 12 + 8 + g + 1)
                    xg = X[:, 4 * g:4 * g + 4, :, :]
                    act.activation(xg, xg, ACT.Exp, scale=DECAY).then_inc(kern_done, 1)

                if s.t == 0:
                    head_lengths()
                if s.A:
                    log_angle(0)
                    kernel_value(0)
                    log_angle(1)
                for g in range(4):
                    if s.A and g < 2:
                        log_angle(g + 2)
                    if s.A and g < 2:
                        kernel_value(g + 1)
                    if s.A and g == 1:
                        kernel_value(3)
                    if s.B:
                        head(s.b, g)
                        if g > 0:
                            store_head(s.b, g - 1)
                    if s.C and g == 1:
                        inv_std(2, x2_var_ready, x2_rs_ready, s.c + 1)
            each_step(act, body)

            act.wait_ge(lg_sub, 1)
            act.activation(probs[:, :, :], tmp8[:, :, :], ACT.Exp).then_inc(lg_exp, 1)
            act.wait_ge(exp_b_loaded, 32)
            for m in range(4):
                if m >= 2:
                    act.wait_ge(y_filled, m - 1)
                for c in range(FC):
                    act.wait_ge(h_filled, FC * m + c + 1)
                    act.activation(hT[m % 2][:, c, :], ring[c], ACT.Relu, bias=b1_s[:, 0, c:c + 1]).then_inc(h0_stored, 1)
                act.wait_ge(y_filled, m + 1)
                act.activation(res[:, 4 * m:4 * m + 4, :], ybank[m % 2].rearrange("p (t d) -> p t d", t=4), ACT.Copy)\
                   .then_inc(y0_stored, 1)
            for m in range(4, len(blocks)):
                store_hidden(act, m, 0, h_even)

        def norm_pair(dve, dst, src, mean, rs, done):
            for c in range(2):
                last = dve.tensor_scalar(dst(c), src(c), mean(c), rs(c), ALU.subtract, ALU.mult)
            last.then_inc(done, 1)

        @block.vector
        def _(dve):
            dve.memset(empty[:, 0:D], 0.0)
            dve.memset(empty[:, D:ROW], float(FAR))
            dve.drain().then_inc(dve_consts, 1)
            dve.memset(zb[:, :], 0.0)
            dve.memset(qf[:, :, :], 0.0)
            dve.memset(sel_s[:, :], 0.0)
            dve.memset(mT[:, :], 0.0)
            dve.memset(ones_row[:, :], 1.0)
            dve.memset(cols[:, 0:1], 1.0 + math.pi / 2)
            dve.memset(vp[:, :, :, DH + 1:DH + 2], 1.0)
            dve.memset(V[:, :, :, XD:XD + 1], 1.0)
            dve.memset(psA[:, :], 0.0)
            def load_statistics(tiles):
                for t in tiles:
                    dve.bn_stats(st[:, t, :], xs[:, t, :] if t < NT else cx[:, t - NT, :])

            def load_variances(first, last):
                dve.drain()
                for t in range(first, last):
                    dve.bn_aggr(mv[:, t, :], st[:, t, :])
                dve.drain()
                dve.tensor_scalar(lnvar[:, first:last], mv[:, first:last, 1], LN_EPS, None, ALU.add).then_inc(x_var_ready, 1)

            dve.wait_ge(x0_loaded, 16)
            load_statistics(range(2))
            load_variances(0, 2)
            dve.wait_ge(attn_w_loaded, 80)
            dve.tensor_scalar(vall[:, :, D], cst_s[:, C_FAR:C_FAR + NT], float(-FAR), None, ALU.add)
            dve.tensor_copy(idb[:, :], ident)
            dve.tensor_copy(id16[:, :], ident).then_inc(dve_consts, 1)
            dve.wait_ge(x_rs_ready, 1)

            def flat(ap):
                return ap.rearrange("p a b -> p (a b)")

            def body(s):
                if s.t == 0:
                    load_variances(2, 2 * NT)
                    dve.wait_ge(xattn_w_loaded, 128)
                    dve.tensor_copy(sel_s[0:XH, :], sel_f).then_inc(dve_consts, 1)
                    dve.wait_ge(x_rs_ready, 2)
                def filled(name):
                    bank, u, w = W(s, name)
                    dve.wait_ge(work_filled[bank], u + 1)
                    return work_read[bank], w

                def norm_heads(n):
                    read, w = filled(f"pT{n}")
                    heads = w[:, 0:4 * (XD + 1)].rearrange("p (h q d) -> p h q d", h=2, q=2)
                    dve.reciprocal(rpv[:, n % 2, :].rearrange("p (h q) -> p h q", h=2), heads[:, :, :, XD])
                    dve.drain()
                    dst = o2[:, :, 2 * n * XD:(2 * n + 2) * XD].rearrange("p q (h d) -> p h q d", h=2)
                    dve.tensor_tensor(dst, heads[:, :, :, 0:XD],
                                      rpv[:, n % 2, :].rearrange("p (h q a) -> p h q a", h=2, a=1).to_broadcast([P, 2, 2, XD]),
                                      ALU.mult).then_inc(read, 1)

                def statistics(c, sources, scale, shift, ready):
                    dve.drain()
                    for n, src in enumerate(sources):
                        dve.bn_stats(st2[:, c + n, :], src)
                    dve.drain()
                    for n in range(2):
                        dve.bn_aggr(mv2[:, c + n, :], st2[:, c + n, :])
                    dve.drain()
                    dve.tensor_scalar(var4[:, c:c + 2], mv2[:, c:c + 2, 1], scale, shift, ALU.mult, ALU.add).then_inc(ready, 1)

                if s.F:
                    norm_pair(dve, lambda c: xn[:, c, :], lambda c: flat(xs[:, bass.ds(2 * s.f + c, 1), :]),
                              lambda c: flat(mv[:, bass.ds(2 * s.f + c, 1), 0:1]),
                              lambda c: lnrs[:, bass.ds(2 * s.f + c, 1)], xn_ready)
                if s.B:
                    norm_pair(dve, lambda c: cn[:, c, :], lambda c: flat(cx[:, bass.ds(2 * s.b + c, 1), :]),
                              lambda c: flat(mv[:, bass.ds(NT + 2 * s.b + c, 1), 0:1]),
                              lambda c: lnrs[:, bass.ds(NT + 2 * s.b + c, 1)], cn_ready)
                if s.F:
                    read, w = filled("xnT")
                    dve.tensor_copy(xnT[:, :], w[:, 0:S]).then_inc(read, 1)
                if s.B:
                    read, w = filled("ctxT")
                    dve.tensor_scalar(cT[:, :], w[:, 0:S], gam_s[:, 0:1], gam_s[:, 1:2], ALU.mult, ALU.add)\
                       .then_inc(read, 1)
                if s.B:
                    aos = []
                    for q in range(2):
                        read, w = filled(f"ao{q}")
                        aos.append((read, w.rearrange("p (h d) -> p h d", h=NH)))
                        dve.tensor_scalar(den[:, q, :], aos[q][1][:, :, DH + 1], 1e-12, None, ALU.mult)
                    dve.drain()
                    for q in range(2):
                        dve.tensor_tensor(den[:, q, :], den[:, q, :], aos[q][1][:, :, DH], ALU.max)
                    dve.drain()
                    dve.reciprocal(rden[:, :, :], den[:, :, :])
                    dve.drain()
                    for q in range(2):
                        dve.tensor_tensor(o[:, q, :].rearrange("p (h d) -> p h d", h=NH), aos[q][1][:, :, 0:DH],
                                          rden[:, q, :].rearrange("p (h a) -> p h a", a=1).to_broadcast([P, NH, DH]),
                                          ALU.mult).then_inc(aos[q][0], 1)
                    dve.drain().then_inc(o_ready, 1)
                if s.C:
                    norm_heads(1)
                if s.F:
                    for c in range(2):
                        read, w = filled(f"qkv{c}")
                        dve.tensor_tensor(qk[:, c, :], w[:, 0:2 * D], bqkv_s[:, 0:2 * D], ALU.add)
                        dve.tensor_tensor(flat(vall[:, bass.ds(2 * s.f + c, 1), 0:D]), w[:, 2 * D:3 * D],
                                          bqkv_s[:, 2 * D:3 * D], ALU.add).then_inc(read, 1)
                if s.B:
                    read, w = filled("oT")
                    dve.tensor_copy(oT[:, :], w[:, 0:S]).then_inc(read, 1)
                    read, w = filled("att")
                    xa = xs[:, bass.ds(2 * s.b, 2), :]
                    dve.tensor_tensor(xa, xa,
                                      w[:, 0:S].rearrange("p (c d) -> p c d", c=2), ALU.add).then_inc(read, 1)
                    statistics(0, [flat(xs[:, bass.ds(2 * s.b + c, 1), :]) for c in range(2)],
                               1.0 + LN_EPS, LN_EPS * LN_EPS, x1_var_ready)
                if s.F:
                    dve.drain()
                    dve.tensor_tensor(sq, qk[:, :, :], qk[:, :, :], ALU.mult)
                    dve.drain()
                    dve.tensor_reduce(out=ss[:, :, :, :].rearrange("p c k h -> p (c k h)"),
                                      in_=sq.rearrange("p c (g d) -> p (c g) d", d=DH), op=ALU.add, axis=AX)
                    dve.drain()
                    dve.tensor_scalar(ss[:, :, :, :], ss[:, :, :, :], 1e-24, None, ALU.max).then_inc(ss_ready, 1)

                def rotary_keys(n):
                    read, w = filled(f"kx{n}")
                    dve.tensor_tensor(kcs[:, n, :, :].rearrange("p a b -> p (a b)"), w, rope, ALU.mult).then_inc(read, 1)

                if s.B:
                    rotary_keys(0)
                    rotary_keys(1)
                if s.C:
                    norm_heads(2)
                if s.B:
                    rotary_keys(2)
                    rotary_keys(3)
                    dve.wait_ge(x1_rs_ready, s.b + 1)
                    norm_pair(dve, lambda c: ln[:, c, :], lambda c: flat(xs[:, bass.ds(2 * s.b + c, 1), :]),
                              lambda c: mv2[:, c, 0:1], lambda c: rs4[:, c:c + 1], ln_ready)
                    read, w = filled("latT")
                    dve.tensor_scalar(lT[:, :], w[:, 0:S], gam_s[:, 2:3], gam_s[:, 3:4], ALU.mult, ALU.add)\
                       .then_inc(read, 1)
                if s.F:
                    dve.wait_ge(l2_ready, s.f + 1)
                    for kind in range(2):
                        dve.tensor_tensor(
                            qn[:, kind, :, :].rearrange("p c (h d) -> p c h d", h=NH),
                            qk[:, :, kind * D:kind * D + D].rearrange("p c (h d) -> p c h d", h=NH),
                            l2[:, :, kind, :].rearrange("p c (h a) -> p c h a", a=1).to_broadcast([P, 2, NH, DH]), ALU.mult)
                    dve.drain()

                    def twice(ap):
                        return ap.rearrange("p g (a d) -> p g a d", a=1).to_broadcast([P, 2 * NH, 2, DH])

                    for kind in range(2):
                        unit = qn[:, kind, :, :].rearrange("p c (h d) -> p (c h) d", h=NH)
                        high = stack[:, kind, :, 0:3:2, :] if kind == 0 else stack[:, kind, :, 0:2, :]
                        dve.tensor_copy(high, twice(unit))
                    dve.drain()
                    for kind in range(2):
                        unit = qn[:, kind, :, :].rearrange("p c (h d) -> p (c h) d", h=NH)
                        low = stack[:, kind, :, 1:4:2, :] if kind == 0 else stack[:, kind, :, 2:4, :]
                        last = dve.tensor_tensor(low, twice(unit), twice(stack[:, kind, :, 0, :]), ALU.subtract)
                    last.then_inc(stack_ready, 1)
                if s.C:
                    norm_heads(3)
                if s.B:
                    dve.tensor_tensor(kf[:, :, 0:S], kcs[:, :, 0, :], kcs[:, :, 1, :], ALU.add)
                    for n in range(2):
                        read, w = filled(f"q{n}")
                        for odd in range(2):
                            rows = slice(XD * odd, XD * odd + XD)
                            last = dve.tensor_scalar(qf[rows, 4 * n + odd:4 * n + 4:2, :],
                                                     w[rows, :].rearrange("p (a b) -> p a b", a=2),
                                                     XD ** -0.5, None, ALU.mult)
                        last.then_inc(read, 1)
                if s.F:
                    for name, dst in (("qS", qT), ("kS", kT)):
                        read, w = filled(name)
                        dve.tensor_copy(dst[:, :, :].rearrange("p a b -> p (a b)"), w.bitcast(F16)).then_inc(read, 1)
                if s.B:
                    for n in range(2):
                        read, w = filled(f"kl{n}")
                        dve.tensor_copy(kf[:, 2 * n:2 * n + 2, S:2 * S], w.rearrange("p (a b) -> p a b", a=2))\
                           .then_inc(read, 1)
                    dve.drain().then_inc(heads_ready, 1)
                if s.C:
                    for n in range(2):
                        read, w = filled(f"o2T{n}")
                        dve.tensor_copy(o2T[:, 2 * n:2 * n + 2, :].rearrange("p a b -> p (a b)"), w).then_inc(read, 1)
                if s.B:
                    for n in range(2 * XH):
                        read, w = filled(f"mx{n}")
                        dve.tensor_reduce(out=mx[:, n % 2, n // 2:n // 2 + 1], in_=w, op=ALU.max, axis=AX).then_inc(read, 1)
                    dve.drain()
                    dve.tensor_scalar(negm[:, :, :], mx[:, :, :], -1.0, None, ALU.mult).then_inc(negm_ready, 1)
                if s.B:
                    read, w = filled("mT")
                    dve.tensor_copy(mT[0:XH, :], w[0:XH, :].bitcast(BF16)[:, 0:S]).then_inc(read, 1)
                def values_over_sums(g):
                    hs = slice(4 * g, 4 * g + 4)
                    if g == 0:
                        dve.wait_ge(kern_done, s.a * 4 + 1)
                        dve.tensor_reduce(out=ncol[:, hs, :], in_=X[:, hs, :, :], op=ALU.add, axis=AX)
                    else:
                        dve.wait_ge(fold_done, s.a * 3 + g)
                        dve.tensor_reduce(out=ncol[:, hs, :], in_=L[:, hs, :, P:P + P // 2], op=ALU.add, axis=AX)
                    dve.drain()
                    dve.reciprocal(rcol[:, hs, :], ncol[:, hs, :])
                    dve.drain()
                    for c in range(2):
                        dve.tensor_tensor(vp[:, hs, c, 0:DH],
                                          vall[:, bass.ds(2 * s.a + c, 1), 32 * g:32 * g + 32]
                                          .rearrange("p a (h d) -> p (a h) d", h=4),
                                          rcol[:, hs, c:c + 1].to_broadcast([P, 4, DH]), ALU.mult)
                    dve.tensor_copy(vp[:, hs, :, DH], rcol[:, hs, :]).then_inc(vp_ready, 1)

                if s.A:
                    values_over_sums(0)
                for g in range(4):
                    if s.A:
                        if g < 3:
                            values_over_sums(g + 1)
                        if s.t == 0 and g == 0:
                            dve.wait_ge(zeroed, 16)
                        dve.wait_ge(av_done, s.a * 4 + g + 1)
                        dve.tensor_copy(aoT[:, g, :], psAg[:, g % 2, :]).then_inc(ao_stored, 1)
                    if s.F:
                        wait(dve, av_done, s.f * 4 + g - 3)
                        for pair in range(2):
                            dve.wait_ge(cos_done, s.f * 8 + 2 * g + pair + 1)
                            dve.tensor_scalar(X[:, 4 * g + 2 * pair:4 * g + 2 * pair + 2, :, :].rearrange("p a b c -> p (a b c)"),
                                              psC[:, :, :].rearrange("p a b -> p (a b)"),
                                              float(np.float32(-1.0 + CLIP)), float(np.float32(1.0 - CLIP)),
                                              ALU.max, ALU.min).then_inc(clip_done, 1)
                            if s.t == -1:
                                n = 2 * g + pair
                                if n == 0:
                                    dve.wait_ge(x_loaded, 16)
                                    dve.wait_ge(ctx_loaded, 16)
                                load_statistics(range(2 + 4 * n, min(6 + 4 * n, 2 * NT)))
                    if s.C and g == 0:
                        read, w = filled("xo")
                        xo_t = xs[:, bass.ds(2 * s.c, 2), :]
                        dve.tensor_tensor(xo_t, xo_t, w[:, 0:S].rearrange("p (c d) -> p c d", c=2), ALU.add).then_inc(read, 1)
                        statistics(2, [flat(xs[:, bass.ds(2 * s.c + c, 1), :]) for c in range(2)], 1.0, LN_EPS, x2_var_ready)
                    if s.C and g == 1:
                        dve.wait_ge(x2_rs_ready, s.c + 1)
                        norm_pair(dve, lambda c: yn[:, c, :], lambda c: flat(xs[:, bass.ds(2 * s.c + c, 1), :]),
                                  lambda c: mv2[:, 2 + c, 0:1], lambda c: rs4[:, 2 + c:3 + c], yn_ready)
                        dve.drain()
                        dve.tensor_copy(y3[:, bass.ds(2 * s.c, 2), 0:D], yn[:, :, :])
                        read, w = filled("yT")
                        dve.tensor_copy(yTs[:, :], w[:, 0:S])
                        dve.tensor_copy(yT[:, bass.ds(s.c * S, S)], w[:, 0:S]).then_inc(read, 1)
                        read, w = filled("logits")
                        dve.tensor_copy(lgs[:, bass.ds(2 * s.c, 2), :], w[:, 0:2 * NE].rearrange("p (c e) -> p c e", c=2))\
                           .then_inc(read, 1)
                    if s.B and g == 2:
                        norm_heads(0)
            each_step(dve, body)

            def bc8(ap):
                return ap.rearrange("p (t a) -> p t a", a=1).to_broadcast([P, NT, NE])

            sc, pm, ex, rank, slot, valid = (r16[:, n, :] for n in range(6))
            experts = cst_s[:, C_EXP:C_EXP + NE].rearrange("p (a e) -> p a e", a=1).to_broadcast([P, NT, NE])
            dve.drain()
            dve.tensor_reduce(out=sc, in_=lgs[:, :, :], op=ALU.max, axis=AX)
            dve.drain()
            dve.tensor_tensor(tmp8[:, :, :], lgs[:, :, :], bc8(sc), ALU.subtract).then_inc(lg_sub, 1)
            dve.wait_ge(lg_exp, 1)
            dve.tensor_reduce(out=sc, in_=probs[:, :, :], op=ALU.add, axis=AX)
            dve.drain()
            dve.reciprocal(sc, sc)
            dve.drain()
            dve.tensor_tensor(probs[:, :, :], probs[:, :, :], bc8(sc), ALU.mult)
            dve.drain()
            dve.tensor_reduce(out=pm, in_=probs[:, :, :], op=ALU.max, axis=AX)
            dve.drain()
            dve.wait_ge(diff_done, 4 * NB)
            dve.tensor_copy(pbc, pm.rearrange("p (t a) -> p t a", a=1).to_broadcast([P, NT, P])).then_inc(pbc_ready, 1)
            dve.tensor_tensor(tmp8[:, :, :], probs[:, :, :], bc8(pm), ALU.is_ge)
            dve.drain()
            dve.tensor_tensor(tmp8[:, :, :], tmp8[:, :, :], experts, ALU.mult)
            dve.drain()
            dve.tensor_reduce(out=ex, in_=tmp8[:, :, :], op=ALU.min, axis=AX)
            dve.drain()
            dve.tensor_tensor(hot[:, :, :], bc8(ex), experts, ALU.is_equal)
            dve.drain()
            dve.tensor_copy(hotb[:, :, :], hot[:, :, :])
            dve.wait_ge(prow_filled, 1)
            for n in range(4):
                dve.tensor_copy(prow[:, n * 512:(n + 1) * 512], ring[n])
            dve.drain().then_inc(prow_ready, 1)
            tri = cst_s[:, C_TRI:C_TRI + P]
            for j in range(NT):
                r = j % 4
                if j >= 4:
                    dve.wait_ge(g_used, j - 3)
                pj = r16[:, 1, j:j + 1]
                own = prow[:, j * P:(j + 1) * P]
                dve.scalar_tensor_tensor(eqd[:, j % 2, :], own, pj, tri, ALU.is_equal, ALU.mult)
                if j > 0:
                    dve.tensor_scalar(G[:, r, 0:j * P], prow[:, 0:j * P], pj, None, ALU.is_lt)
                if j < NT - 1:
                    dve.tensor_scalar(G[:, r, (j + 1) * P:NT * P], prow[:, (j + 1) * P:NT * P], pj, None, ALU.is_le)
                dve.drain()
                dve.scalar_tensor_tensor(G[:, r, j * P:(j + 1) * P], own, pj, eqd[:, j % 2, :], ALU.is_lt, ALU.add)\
                   .then_inc(g_ready, 1)
            dve.wait_ge(rank_done, 1)
            dve.tensor_tensor(tmp8[:, :, :], psR, hot[:, :, :], ALU.mult)
            dve.drain()
            dve.tensor_reduce(out=rank, in_=tmp8[:, :, :], op=ALU.add, axis=AX)
            dve.drain()
            dve.tensor_scalar(slot, ex, float(CAP), float((NE - 1) * CAP), ALU.mult, ALU.add)
            dve.tensor_scalar(valid, ex, float(-NE), None, ALU.is_gt)
            dve.drain()
            dve.tensor_tensor(slot, slot, rank, ALU.add)
            dve.scalar_tensor_tensor(valid, rank, float(CAP), valid, ALU.is_lt, ALU.mult)
            dve.drain()
            dve.tensor_scalar(sc, valid, -1.0, 1.0, ALU.mult, ALU.add)
            far = cst_s[:, C_FAR:C_FAR + NT]
            dve.tensor_tensor(slot, slot, far, ALU.subtract)
            dve.drain()
            dve.tensor_tensor(slot, slot, valid, ALU.mult)
            dve.drain()
            dve.tensor_tensor(slot, slot, far, ALU.add)
            dve.drain()
            dve.tensor_copy(dest[:, :], slot).then_inc(dest_ready, 1)
            dve.wait_ge(y0_stored, 4)
            for t in range(NT):
                last = dve.scalar_tensor_tensor(xs[:, t, :], res[:, t, :], sc[:, t:t + 1], xs[:, t, :], ALU.mult, ALU.add)
                if t % 4 == 3:
                    last.then_inc(final_ready, 1)

            def store_inputs(m):
                e = blocks[m][0]
                dve.wait_ge(xin_loaded[(e - 1) % 4], 32 * ((e + 3) // 4))
                dve.tensor_copy(ids[:, e - 1, 0:2], xin[:, (e - 1) % 4, 0:2, D])
                dve.tensor_copy(ids[0:CAP - 2 * P, e - 1, 2:3], xin[0:CAP - 2 * P, (e - 1) % 4, 2, D:ROW])
                dve.wait_ge(xinT_filled, e)
                if e > 2:
                    dve.wait_ge(h_filled, FC * (m - 1))
                dve.tensor_copy(xinT[:, e % 2, :], psW[:, 0, 0:CAP]).then_inc(xinT_ready, 1)

            def store_outputs(m):
                e, _ = blocks[m]
                dve.wait_ge(y_filled, m + 1)
                if e > 2:
                    dve.wait_ge(y_saved[e % 2], 48 * ((e - 1) // 2))
                bias = b2_s[:, e * D:(e + 1) * D]
                dve.tensor_tensor(yo[:, e % 2, 0:2, :], ybank[m % 2][:, 0:2 * D].rearrange("p (c d) -> p c d", c=2),
                                  bias.rearrange("p (c d) -> p c d", c=1).to_broadcast([P, 2, D]), ALU.add)
                rows = CAP - 2 * P
                dve.tensor_tensor(yo[0:rows, e % 2, 2, :], ybank[m % 2][0:rows, 2 * D:3 * D], bias[0:rows, :], ALU.add)\
                   .then_inc(y_stored, 1)

            dve.wait_ge(exp_b_loaded, 32)
            store_inputs(4)
            for m in range(4, len(blocks)):
                store_hidden(dve, m, 1, h_odd)
                if m < len(blocks) - 1:
                    store_inputs(m + 1)
                if m > 4:
                    store_outputs(m - 1)
            store_outputs(len(blocks) - 1)

        @block.tensor
        def _(pe):
            pe.wait_ge(attn_w_loaded, 80)
            pe.wait_ge(dve_consts, 2)

            def body(s):
                if s.t == 1:
                    pe.wait_ge(dve_consts, 3)
                def fill(name):
                    bank, u, w = W(s, name)
                    wait(pe, work_read[bank], u)
                    return work_filled[bank], w

                def stored(name):
                    bank, u, _ = W(s, name)
                    pe.wait_ge(work_read[bank], u + 1)

                def turn(name, src, ready, value):
                    pe.wait_ge(ready, value)
                    full, w = fill(name)
                    for c in range(2):
                        mm = pe.transpose(w[:, c * P:(c + 1) * P], src[:, c, :], ident)
                    mm.then_inc(full, 1)

                def values(n, src):
                    if n == 0:
                        wait(pe, exps_done, s.b * XH)
                    else:
                        pe.wait_ge(v_stored, 2 * s.b + 1)
                    for c in range(2):
                        mm = pe.matmul(psS[:, 2 * c:2 * c + 2, :].rearrange("p a b -> p (a b)"),
                                       src[:, c * P:(c + 1) * P], wv_s[:, :], start=True, stop=True)
                    mm.then_inc(v_filled, 1)

                def rotary_keys(n):
                    full, w = fill(f"kx{n}")
                    if n == 0:
                        stored("ctxT")
                    pe.matmul(w[:, 0:S], wk_s[:, n * P:(n + 1) * P], cT[:, :], start=True, stop=True)
                    pe.matmul(w[:, S:2 * S], wks_s[:, n * P:(n + 1) * P], cT[:, :], start=True, stop=True)\
                      .then_inc(full, 1)

                def keys_or_queries(name, weights):
                    for n in range(2):
                        full, w = fill(f"{name}{n}")
                        for m in range(2):
                            c = 2 * n + m
                            mm = pe.matmul(w[:, m * S:(m + 1) * S], weights[:, c * P:(c + 1) * P], lT[:, :],
                                           start=True, stop=True)
                        mm.then_inc(full, 1)

                def scores(n, h):
                    wait(pe, exps_done, n * XH + h)
                    for c in range(KC):
                        dst = psS[:, c, :]
                        pe.matmul(dst, kf[:, h // 2, c * P:(c + 1) * P], qf[:, h, :], start=True, stop=False)
                        mm = pe.matmul(dst, sel_s[:, h * P:(h + 1) * P], mT[:, :], start=False, stop=True)
                    mm.then_inc(scores_done, 1)

                def weighted(n, h):
                    pe.wait_ge(exps_done, n * XH + h + 1)
                    wait(pe, oh_stored, n * XH + h)
                    for c in range(KC):
                        mm = pe.matmul(psPh[0:XD + 1, h % 2, :], V[:, c, h, :], E[:, h % 2, c, :],
                                       start=(c == 0), stop=(c == KC - 1))
                    mm.then_inc(pv_done, 1)

                def turn_heads(batch, n):
                    pe.wait_ge(oh_stored, batch * XH + 2 * n + 2)
                    full, w = fill(f"pT{n}")
                    for m in range(2):
                        for q in range(2):
                            at = (2 * m + q) * (XD + 1)
                            mm = pe.transpose(w[:, at:at + XD + 1], oh[:, (2 * n + m) % 4, q * P:(q + 1) * P],
                                              ident[0:XD + 1, 0:XD + 1])
                    mm.then_inc(full, 1)

                if s.F:
                    turn("xnT", xn, xn_ready, s.f + 1)
                if s.B:
                    turn("ctxT", cn, cn_ready, s.b + 1)
                if s.B:
                    pe.wait_ge(ao_stored, s.b * 4 + 4)
                    for q in range(2):
                        full, w = fill(f"ao{q}")
                        for g in range(4):
                            mm = pe.transpose(w[:, g * P:(g + 1) * P], aoT[:, g, q * P:(q + 1) * P], ident)
                        mm.then_inc(full, 1)
                if s.C:
                    scores(s.c, 5)
                    turn_heads(s.c, 1)
                    weighted(s.c, 4)
                if s.F:
                    for c in range(2):
                        full, w = fill(f"qkv{c}")
                        if c == 0:
                            stored("xnT")
                        pe.matmul(w[:, 0:3 * D], xnT[:, c * P:(c + 1) * P], wqkv_s[:, :], start=True, stop=True)\
                          .then_inc(full, 1)
                if s.B:
                    turn("oT", o, o_ready, s.b + 1)
                    full, w = fill("att")
                    stored("oT")
                    for c in range(2):
                        pe.matmul(w[:, c * D:(c + 1) * D], ones_row[:, :], bout_s[:, :], start=True, stop=False)
                        mm = pe.matmul(w[:, c * D:(c + 1) * D], oT[:, c * P:(c + 1) * P], wout_s[:, :], start=False, stop=True)
                    mm.then_inc(full, 1)
                if s.B:
                    rotary_keys(0)
                if s.C:
                    scores(s.c, 6)
                    weighted(s.c, 5)
                if s.B:
                    rotary_keys(1)
                if s.C:
                    turn_heads(s.c, 2)
                    scores(s.c, 7)
                    weighted(s.c, 6)
                if s.B:
                    rotary_keys(2)
                    rotary_keys(3)
                    turn("latT", ln, ln_ready, s.b + 1)
                if s.C:
                    weighted(s.c, 7)
                    turn_heads(s.c, 3)
                if s.B:
                    stored("latT")
                    keys_or_queries("q", wq_s)
                if s.F:
                    pe.wait_ge(stack_ready, s.f + 1)
                    for kind, name in enumerate(("qS", "kS")):
                        full, w = fill(name)
                        wv_ = w.bitcast(F16).rearrange("p (g c t) -> p g c t", g=4, c=2)
                        for g in range(4):
                            for c in range(2):
                                src = stack[:, kind, c * NH + 4 * g:c * NH + 4 * g + 4, :, :].rearrange("p h s d -> p (h s d)")
                                mm = pe.transpose(wv_[:, g, c, :], src, id16[:, :])
                        mm.then_inc(full, 1)
                if s.B:
                    keys_or_queries("kl", wk_s)
                    values(0, lT)
                if s.C:
                    for n in range(2):
                        full, w = fill(f"o2T{n}")
                        for m in range(2):
                            for q in range(2):
                                c = 2 * n + m
                                mm = pe.transpose(w[:, m * S + q * P:m * S + (q + 1) * P], o2[:, q, c * P:(c + 1) * P], ident)
                        mm.then_inc(full, 1)
                if s.B:
                    pe.wait_ge(heads_ready, s.b + 1)
                    for n in range(2 * XH):
                        h, c = n // 2, n % 2
                        full, w = fill(f"mx{n}")
                        pe.matmul(w, qb[:, h, 2 * c * P + 1:2 * (c + 1) * P:2], kb[:, h // 2, 1:4 * S:2],
                                  start=True, stop=True).then_inc(full, 1)
                        if n == 5:
                            values(1, cT)
                if s.B:
                    pe.wait_ge(negm_ready, s.b + 1)
                    full, w = fill("mT")
                    for c in range(2):
                        mm = pe.transpose(w[0:XH, :].bitcast(BF16)[:, c * P:(c + 1) * P], negm[:, c, :], idb[:, :])
                    mm.then_inc(full, 1)
                    stored("mT")
                    pe.wait_ge(v_stored, 2 * s.b + 2)
                    scores(s.b, 0)
                def attention(g):
                    pe.wait_ge(vp_ready, s.a * 4 + g + 1)
                    wait(pe, ao_stored, s.a * 4 + g)
                    for c in range(2):
                        for j in range(4):
                            h = 4 * g + j
                            mm = pe.matmul(psAg[32 * j:32 * j + DH + 2, g % 2, :], vp[:, h, c, :], X[:, h, c, :],
                                           start=(c == 0), stop=(c == 1), tile_position=(0, 32 * j))
                    mm.then_inc(av_done, 1)

                def cosines(g, pair):
                    if g == 0 and pair == 0:
                        stored("kS")
                    wait(pe, clip_done, s.f * 8 + 2 * g + pair)
                    for c in range(2):
                        for m in range(2):
                            j = 2 * pair + m
                            rows = slice(32 * j, 32 * j + 32)
                            mm = pe.matmul(psC[:, m, c * S:(c + 1) * S], kT[rows, g, c * P:(c + 1) * P], qT[rows, g, :],
                                           start=True, stop=True)
                    mm.then_inc(cos_done, 1)

                for g in range(4):
                    if s.A:
                        attention(g)
                    if s.F:
                        cosines(g, 0)
                    if s.B:
                        scores(s.b, g + 1)
                    if s.C and g == 0:
                        full, w = fill("xo")
                        stored("o2T1")
                        for q in range(2):
                            for c in range(4):
                                mm = pe.matmul(w[:, q * D:(q + 1) * D], o2T[:, c, q * P:(q + 1) * P], wo_s[:, c, :],
                                               start=(c == 0), stop=(c == 3))
                        mm.then_inc(full, 1)
                    if s.F:
                        cosines(g, 1)
                    if s.B:
                        weighted(s.b, g)
                    if s.C and g == 1:
                        turn("yT", yn, yn_ready, s.c + 1)
                        full, w = fill("logits")
                        stored("yT")
                        for c in range(2):
                            mm = pe.matmul(w[:, c * NE:(c + 1) * NE], yTs[:, c * P:(c + 1) * P], wr_s[:, :],
                                           start=True, stop=True)
                        mm.then_inc(full, 1)
                    if s.B and g == 2:
                        turn_heads(s.b, 0)
            each_step(pe, body)

            pe.wait_ge(pbc_ready, 1)
            for t in range(NT):
                mm = pe.transpose(ring[t // 4][:, (t % 4) * P:(t % 4 + 1) * P], pbc[:, t, :], ident)
            mm.then_inc(prow_filled, 1)
            pe.wait_ge(exp_w_loaded, 32)
            pe.wait_ge(exp_b_loaded, 32)
            pe.wait_ge(prow_ready, 1)

            def hidden(m, banks):
                e, blk = blocks[m]
                src = yT[:, blk * FF:(blk + 1) * FF] if e == 0 else xinT[:, e % 2, :]
                for c in banks:
                    if 0 < m <= 4:
                        pe.wait_ge(h0_stored, FC * (m - 1) + c + 1)
                    elif m > 4:
                        pe.wait_ge(h_odd if c % 2 else h_even, 2 * (m - 5) + c // 2 + 1)
                    pe.matmul(ring[c][:, 0:FF if e == 0 else CAP], w1_s[:, e, c * P:(c + 1) * P], src,
                              start=True, stop=True).then_inc(h_filled, 1)

            def outputs(m, tiles):
                e, blk = blocks[m]
                if tiles[0] == 0:
                    if e == 0:
                        pe.wait_ge(h0_stored, FC * (m + 1))
                    else:
                        pe.wait_ge(h_even, 2 * (m - 3))
                        pe.wait_ge(h_odd, 2 * (m - 3))
                    if 2 <= m < 6:
                        pe.wait_ge(y0_stored, m - 1)
                    elif m >= 6:
                        pe.wait_ge(y_stored, m - 5)
                for t in tiles:
                    rows = P if e == 0 or t < 2 else CAP - 2 * P
                    dst = ybank[m % 2][0:rows, t * D:(t + 1) * D]
                    if e == 0:
                        pe.matmul(dst, ones_row[:, 0:rows], b2_s[0:1, 0:D], start=True, stop=False)
                    for c in range(FC):
                        mm = pe.matmul(dst, hT[m % 2][:, c, t * P:t * P + rows], w2_s[:, e, c, :],
                                       start=(e > 0 and c == 0), stop=(c == FC - 1))
                if tiles[-1] == (3 if e == 0 else 2):
                    mm.then_inc(y_filled, 1)

            pe.matmul(psR.rearrange("p t e -> p (t e)"), zb[:, :], zb[:, :], start=True, stop=False, skip_group_check=True)
            for j in range(NT):
                m, part = j // 4, j % 4
                if part < 2:
                    hidden(m, (2 * part, 2 * part + 1))
                else:
                    outputs(m, (2 * part - 4, 2 * part - 3))
                pe.wait_ge(g_ready, j + 1)
                for t in range(NT):
                    mm = pe.matmul(psR[:, t, :], G[:, j % 4, t * P:(t + 1) * P], hotb[:, j, :], start=False,
                                   stop=(j == NT - 1), skip_group_check=True)
                mm.then_inc(g_used, 1)
            pe.drain().then_inc(rank_done, 1)

            def inputs(m):
                e = blocks[m][0]
                pe.wait_ge(xin_loaded[(e - 1) % 4], 32 * ((e + 3) // 4))
                if e > 1:
                    pe.wait_ge(xinT_ready, e - 1)
                at = 0
                for c, rows in enumerate((P, P, CAP - 2 * P)):
                    mm = pe.transpose(psW[:, 0, at:at + rows], xin[0:rows, (e - 1) % 4, c, 0:D], ident[0:rows, 0:rows])
                    at += rows
                mm.then_inc(xinT_filled, 1)

            inputs(4)
            for m in range(4, len(blocks)):
                pe.wait_ge(xinT_ready, blocks[m][0])
                hidden(m, range(FC))
                if m < len(blocks) - 1:
                    inputs(m + 1)
                if m > 4:
                    outputs(m - 1, (0, 1, 2))
            outputs(len(blocks) - 1, (0, 1, 2))

    return nc


def kernel(x, ctx_1024, L0_attn_w_qkv, L0_attn_b_qkv, L0_attn_w_out, L0_attn_b_out, L0_xattn_gamma_x,
           L0_xattn_beta_x, L0_xattn_gamma_l, L0_xattn_beta_l, L0_xattn_Wq, L0_xattn_Wkv, L0_xattn_Wo,
           L0_ffn_router_w, L0_ffn_W1, L0_ffn_b1, L0_ffn_W2, L0_ffn_b2):
    import concourse.bacc as bacc
    from concourse.bass_utils import run_bass_kernel_spmd

    cst, sel = shape_constants()
    wkv = np.asarray(L0_xattn_Wkv)
    wk = wkv[:, 0:INNER]
    arrays = {
        "x": np.asarray(x).reshape(NB * S, D),
        "ctx_in": np.asarray(ctx_1024).reshape(NB * S, D),
        "wqkv": np.asarray(L0_attn_w_qkv).T,
        "bqkv": np.broadcast_to(np.asarray(L0_attn_b_qkv), (P, 3 * D)),
        "wout": np.asarray(L0_attn_w_out).T,
        "bout": np.asarray(L0_attn_b_out).reshape(1, D),
        "gam": np.stack([np.asarray(a) for a in (L0_xattn_gamma_x, L0_xattn_beta_x, L0_xattn_gamma_l,
                                                 L0_xattn_beta_l)], axis=1),
        "wq": np.asarray(L0_xattn_Wq),
        "wk": wk,
        "wks": wk.reshape(D, XH, 2, XD // 2)[:, :, ::-1, :].reshape(D, INNER),
        "wv": wkv[:, INNER:],
        "wo": np.asarray(L0_xattn_Wo),
        "wr": np.asarray(L0_ffn_router_w).T,
        "w1": np.asarray(L0_ffn_W1),
        "b1": np.asarray(L0_ffn_b1).reshape(NE, FC, P).transpose(2, 0, 1).reshape(P, NE * FC),
        "w2": np.asarray(L0_ffn_W2),
        "b2": np.broadcast_to(np.asarray(L0_ffn_b2).reshape(1, NE * D), (P, NE * D)),
        "cst": cst,
        "sel": sel,
    }
    arrays = {f"in_{name}": np.ascontiguousarray(a) for name, a in arrays.items()}
    nc = bacc.Bacc("TRN2", target_bir_lowering=False, num_devices=1)
    args = [nc.dram_tensor(n, a.shape, mybir.dt.from_np(a.dtype), kind="ExternalInput").ap() for n, a in arrays.items()]
    out = nc.dram_tensor("out_x", (NB * S, D), F32, kind="ExternalOutput").ap()
    build(nc, *args, out)
    r = run_bass_kernel_spmd(nc, [arrays], core_ids=[0])
    return r.results[0]["out_x"].reshape(NB, S, D)
```
